# Optimizing a Trainium2 kernel written in Bass

```python
import numpy as np
import jax
import jax.numpy as jnp

def _softmax(x, axis=-1):
    return jax.nn.softmax(x, axis=axis)

def _gelu(x):
    return jax.nn.gelu(x, approximate=True)

def _silu(x):
    return jax.nn.silu(x)

def _sigmoid(x):
    return jax.nn.sigmoid(x)

def _layernorm(x, axis=-1, eps=1e-05):
    m = jnp.mean(x, axis=axis, keepdims=True)
    v = jnp.var(x, axis=axis, keepdims=True)
    return (x - m) / jnp.sqrt(v + eps)

def _scatter_add(tgt, idx, src, axis=0):
    return tgt.at[idx].add(src)

def _segment_sum(src, seg, n):
    return jax.ops.segment_sum(src, seg, n)
kernel_name = 'mk_decoder_postln_d2_seqx_r4_600ef4'

def setup_inputs(seed: int=0):
    np.random.seed(seed)
    _w = jnp.asarray

    def _rec_inputs():
        import jax
        import jax.numpy as jnp
        _rk = jax.random.key(seed)
        x = -0.0002928 + 1 * jax.random.normal(jax.random.fold_in(_rk, 1), (2, 1024, 256), jnp.float32)
        _lenS = 1024 - jax.random.randint(jax.random.fold_in(_rk, 7), (2,), 0, max(1, 1024 // 4) + 1, jnp.int32)
        _lenS2 = 77 - jax.random.randint(jax.random.fold_in(_rk, 8), (2,), 0, max(1, 77 // 4) + 1, jnp.int32)
        _ctx_1024P = jax.random.normal(jax.random.fold_in(_rk, 11), (2, 16, 256), jnp.float32)
        _ctx_1024c = jax.random.dirichlet(jax.random.fold_in(_rk, 511), 0.3 * jnp.ones((16,), jnp.float32), (2, 77))
        _ctx_1024t = jnp.einsum('bsk,bkd->bsd', _ctx_1024c, _ctx_1024P)
        _ctx_1024t = _ctx_1024t * jax.lax.rsqrt(jnp.mean(jnp.square(_ctx_1024t)) + 1e-12) * 0.953939
        ctx_1024 = 4.13588e-05 + 0.999923 * (_ctx_1024t + 0.3 * jax.random.normal(jax.random.fold_in(_rk, 611), (2, 77, 256), jnp.float32))
        _validS = jnp.arange(1024)[None, :] < _lenS[:, None]
        _validS2 = jnp.arange(77)[None, :] < _lenS2[:, None]
        _causal = jnp.tril(jnp.ones((1024, 1024), dtype=bool))
        mask_Bx1xSxS2_ik0 = jnp.where(jnp.broadcast_to(_validS2[:, None, None, :], (2, 1, 1024, 77)), 0, 1).astype(jnp.int32)
        return (x, ctx_1024, mask_Bx1xSxS2_ik0)
    x, ctx_1024, mask_Bx1xSxS2_ik0 = _rec_inputs()

    def _L0_attn_setup():
        import jax, jax.numpy as jnp
        import numpy as np
        D_MODEL = 256
        N_BLOCKS = 4
        D_STATE = 16
        D_CONV = 4
        EXPAND = 2
        DT_RANK = 64
        D_INNER = EXPAND * D_MODEL
        BATCH = 2
        SEQLEN = 256

        def _layer_norm(x, w, b):
            m = jnp.mean(x, -1, keepdims=True)
            v = jnp.mean((x - m) ** 2, -1, keepdims=True)
            return (x - m) * jax.lax.rsqrt(v + 1e-05) * w + b

        def _selective_scan(u, dt, A, Bm, Cm, Dp):
            dA = jnp.exp(dt[..., None] * A)
            dBu = (dt * u)[..., None] * Bm[:, :, None, :]

            def step(h, inp):
                dA_t, dBu_t, C_t = inp
                h = dA_t * h + dBu_t
                y = jnp.einsum('ben,bn->be', h, C_t)
                return (h, y)
            h0 = jnp.zeros((u.shape[0], u.shape[2], A.shape[1]), u.dtype)
            xs = (jnp.moveaxis(dA, 1, 0), jnp.moveaxis(dBu, 1, 0), jnp.moveaxis(Cm, 1, 0))
            _, ys = jax.lax.scan(step, h0, xs)
            y = jnp.moveaxis(ys, 0, 1)
            return y + u * Dp

        def _mamba(x, in_w, cw, cb, xw, dtw, dtb, A_log, Dp, ow):
            L = x.shape[1]
            xz = x @ in_w
            u, z = jnp.split(xz, 2, axis=-1)
            K = cw.shape[1]
            up = jnp.pad(u, ((0, 0), (K - 1, 0), (0, 0)))
            conv = cb + sum((up[:, k:k + L, :] * cw[:, k] for k in range(K)))
            u = jax.nn.silu(conv)
            dbl = u @ xw
            dt = jax.nn.softplus(dbl[..., :DT_RANK] @ dtw + dtb)
            Bm = dbl[..., DT_RANK:DT_RANK + D_STATE]
            Cm = dbl[..., DT_RANK + D_STATE:]
            A = -jnp.exp(A_log)
            y = _selective_scan(u, dt, A, Bm, Cm, Dp)
            y = y * jax.nn.silu(z)
            return y @ ow

        def _forward(x, norm_w, norm_b, in_proj_w, conv_w, conv_b, xproj_w, dtproj_w, dtproj_b, A_log, skip_D, out_proj_w, fn_w, fn_b):
            for i in range(N_BLOCKS):
                h = _layer_norm(x, norm_w[i], norm_b[i])
                h = _mamba(h, in_proj_w[i], conv_w[i], conv_b[i], xproj_w[i], dtproj_w[i], dtproj_b[i], A_log[i], skip_D[i], out_proj_w[i])
                x = x + h
            return _layer_norm(x, fn_w, fn_b)
        key = jax.random.key(seed)
        ks = jax.random.split(key, 8)
        s = 0.02
        f = lambda k, sh: jax.random.normal(k, sh, dtype=jnp.float32) * s
        return {'x': jax.random.normal(ks[0], (BATCH, SEQLEN, D_MODEL), dtype=jnp.float32), 'norm_w': jnp.ones((N_BLOCKS, D_MODEL), jnp.float32), 'norm_b': jnp.zeros((N_BLOCKS, D_MODEL), jnp.float32), 'in_proj_w': f(ks[1], (N_BLOCKS, D_MODEL, 2 * D_INNER)), 'conv_w': f(ks[2], (N_BLOCKS, D_INNER, D_CONV)), 'conv_b': jnp.zeros((N_BLOCKS, D_INNER), jnp.float32), 'xproj_w': f(ks[3], (N_BLOCKS, D_INNER, DT_RANK + 2 * D_STATE)), 'dtproj_w': f(ks[4], (N_BLOCKS, DT_RANK, D_INNER)), 'dtproj_b': jnp.full((N_BLOCKS, D_INNER), -4.6, jnp.float32), 'A_log': jnp.tile(jnp.log(jnp.arange(1, D_STATE + 1, dtype=jnp.float32))[None, None, :], (N_BLOCKS, D_INNER, 1)), 'skip_D': jnp.ones((N_BLOCKS, D_INNER), jnp.float32), 'out_proj_w': f(ks[5], (N_BLOCKS, D_INNER, D_MODEL)), 'fn_w': jnp.ones((D_MODEL,), jnp.float32), 'fn_b': jnp.zeros((D_MODEL,), jnp.float32)}
    _L0_attn_all = _L0_attn_setup()
    _L0_attn_in = {k: v for k, v in _L0_attn_all.items() if k in ('norm_w', 'norm_b', 'in_proj_w', 'conv_w', 'conv_b', 'xproj_w', 'dtproj_w', 'dtproj_b', 'A_log', 'skip_D', 'out_proj_w', 'fn_w', 'fn_b')}
    del _L0_attn_all

    def _L0_xattn_setup():
        import jax, jax.numpy as jnp
        import numpy as np
        DIM = 256
        H = 16
        DH = DIM // H
        LN_EPS = 1e-05

        def _linear_params(key, din, dout):
            kw, kb = jax.random.split(key)
            bound = 1.0 / np.sqrt(din)
            W = jax.random.uniform(kw, (din, dout), jnp.float32, -bound, bound)
            b = jax.random.uniform(kb, (dout,), jnp.float32, -bound, bound)
            return (W, b)

        def _layernorm(x, g, b):
            m = jnp.mean(x, axis=-1, keepdims=True)
            v = jnp.mean(jnp.square(x - m), axis=-1, keepdims=True)
            return (x - m) * jax.lax.rsqrt(v + LN_EPS) * g + b

        def _split_heads(x):
            B, N, _ = x.shape
            return x.reshape(B, N, H, DH).transpose(2, 0, 1, 3).reshape(H * B, N, DH)

        def _merge_heads(x, B):
            _, N, _ = x.shape
            return x.reshape(H, B, N, DH).transpose(1, 2, 0, 3).reshape(B, N, DIM)
        key = jax.random.key(seed)
        ks = jax.random.split(key, 10)
        inp = {'Q': jax.random.normal(ks[0], (8, 128, DIM), jnp.float32), 'K1': jax.random.normal(ks[1], (8, 256, DIM), jnp.float32), 'K2': jax.random.normal(ks[2], (8, 256, DIM), jnp.float32)}
        for name, k in zip(['q', 'k1', 'k2', 'v1', 'v2', 'o'], ks[3:9]):
            W, b = _linear_params(k, DIM, DIM)
            inp['W' + name] = W
            inp['b' + name] = b
        inp['g0'] = jnp.ones((DIM,), jnp.float32)
        inp['beta0'] = jnp.zeros((DIM,), jnp.float32)
        inp['g1'] = jnp.ones((DIM,), jnp.float32)
        inp['beta1'] = jnp.zeros((DIM,), jnp.float32)
        return inp
    _L0_xattn_all = _L0_xattn_setup()
    _L0_xattn_in = {k: v for k, v in _L0_xattn_all.items() if k in ('Wq', 'bq', 'Wk1', 'bk1', 'Wk2', 'bk2', 'Wv1', 'bv1', 'Wv2', 'bv2', 'Wo', 'bo', 'g0', 'beta0', 'g1', 'beta1')}
    del _L0_xattn_all

    def _L0_ffn_setup():
        import jax, jax.numpy as jnp
        import numpy as np
        EMB = 256
        HID = 512
        HEADS = 16
        HEAD_DIM = EMB // HEADS
        EXPERTS = 8
        TOPK = 2
        EPS = 1e-05

        def layernorm(x, scale, shift):
            mean = jnp.mean(x, axis=-1, keepdims=True)
            var = jnp.mean((x - mean) ** 2, axis=-1, keepdims=True)
            return scale * (x - mean) / jnp.sqrt(var + EPS) + shift

        def attention(x, wq, wk, wv, wo, bo):
            b, t, _ = x.shape
            q = (x @ wq).reshape(b, t, HEADS, HEAD_DIM)
            k = (x @ wk).reshape(b, t, HEADS, HEAD_DIM)
            v = (x @ wv).reshape(b, t, HEADS, HEAD_DIM)
            scores = jnp.einsum('bqhd,bkhd->bhqk', q, k)
            mask = jnp.arange(t)[:, None] < jnp.arange(t)[None, :]
            scores = jnp.where(mask, -jnp.inf, scores)
            attn = jax.nn.softmax(scores / np.sqrt(HEAD_DIM), axis=-1)
            ctx = jnp.einsum('bhqk,bkhd->bqhd', attn, v).reshape(b, t, EMB)
            return ctx @ wo + bo

        def moe_ff(x, gate_w, w1, w2, w3):
            b, t, d = x.shape
            xf = x.reshape(b * t, d)
            scores = xf @ gate_w
            topk_scores, topk_idx = jax.lax.top_k(scores, TOPK)
            topk_probs = jax.nn.softmax(topk_scores, axis=-1)
            weight = jnp.sum(jax.nn.one_hot(topk_idx, EXPERTS, dtype=xf.dtype) * topk_probs[..., None], axis=1)
            h = jax.nn.silu(jnp.einsum('td,edh->eth', xf, w1)) * jnp.einsum('td,edh->eth', xf, w2)
            out_e = jnp.einsum('eth,ehd->etd', h, w3)
            out = jnp.einsum('etd,te->td', out_e, weight)
            return out.reshape(b, t, d)
        key = jax.random.key(seed)
        ks = jax.random.split(key, 12)
        s = lambda k, shape, fan: jax.random.normal(k, shape, jnp.float32) / np.sqrt(fan)
        return {'x': jax.random.normal(ks[0], (2, 512, EMB), jnp.float32), 'ln1_scale': jnp.ones((EMB,), jnp.float32), 'ln1_shift': jnp.zeros((EMB,), jnp.float32), 'wq': s(ks[1], (EMB, EMB), EMB), 'wk': s(ks[2], (EMB, EMB), EMB), 'wv': s(ks[3], (EMB, EMB), EMB), 'wo': s(ks[4], (EMB, EMB), EMB), 'bo': jnp.zeros((EMB,), jnp.float32), 'ln2_scale': jnp.ones((EMB,), jnp.float32), 'ln2_shift': jnp.zeros((EMB,), jnp.float32), 'gate_w': s(ks[5], (EMB, EXPERTS), EMB), 'w1': s(ks[6], (EXPERTS, EMB, HID), EMB), 'w2': s(ks[7], (EXPERTS, EMB, HID), EMB), 'w3': s(ks[8], (EXPERTS, HID, EMB), HID)}
    _L0_ffn_all = _L0_ffn_setup()
    _L0_ffn_in = {k: v for k, v in _L0_ffn_all.items() if k in ('ln1_scale', 'ln1_shift', 'wq', 'wk', 'wv', 'wo', 'bo', 'ln2_scale', 'ln2_shift', 'gate_w', 'w1', 'w2', 'w3')}
    del _L0_ffn_all

    def _L1_attn_setup():
        import jax, jax.numpy as jnp
        import numpy as np
        D_MODEL = 256
        N_HEADS = 16
        D_HIDDEN = 1024
        BATCH = 2
        N_CTX = 512

        def _split_heads(t, n_heads):
            B, S, D = t.shape
            return t.reshape(B, S, n_heads, D // n_heads).transpose(0, 2, 1, 3)
        key = jax.random.key(seed)
        ks = jax.random.split(key, 4)
        scale = 0.02
        x = jax.random.normal(ks[0], (BATCH, N_CTX, D_MODEL), dtype=jnp.float32)
        Wk = jax.random.normal(ks[1], (D_MODEL, D_MODEL), dtype=jnp.float32) * scale
        bk = jnp.zeros((D_MODEL,), dtype=jnp.float32)
        Wv = jax.random.normal(ks[2], (D_MODEL, D_HIDDEN), dtype=jnp.float32) * scale
        bv = jnp.zeros((D_HIDDEN,), dtype=jnp.float32)
        Wf = jax.random.normal(ks[3], (D_HIDDEN, D_MODEL), dtype=jnp.float32) * scale
        bf = jnp.zeros((D_MODEL,), dtype=jnp.float32)
        return {'x': x, 'Wk': Wk, 'bk': bk, 'Wv': Wv, 'bv': bv, 'Wf': Wf, 'bf': bf}
    _L1_attn_all = _L1_attn_setup()
    _L1_attn_in = {k: v for k, v in _L1_attn_all.items() if k in ('Wk', 'bk', 'Wv', 'bv', 'Wf', 'bf')}
    del _L1_attn_all

    def _L1_xattn_setup():
        import jax, jax.numpy as jnp
        import numpy as np
        B, S, D, H = (4, 512, 256, 16)
        DK = D // H

        def _split_heads(x):
            b, s, _ = x.shape
            return x.reshape(b, s, H, DK).transpose(0, 2, 1, 3)
        key = jax.random.key(seed)
        ks = jax.random.split(key, 8)
        Q = jax.random.normal(ks[0], (B, S, D), dtype=jnp.float32)
        K = jax.random.normal(ks[1], (B, S, D), dtype=jnp.float32)
        V = jax.random.normal(ks[2], (B, S, D), dtype=jnp.float32)
        mask = jnp.broadcast_to(jnp.tril(jnp.ones((S, S), dtype=jnp.int32))[None, None], (B, 1, S, S))
        scale = 1.0 / np.sqrt(D)
        W_Q = jax.random.normal(ks[3], (D, D), dtype=jnp.float32) * scale
        W_K = jax.random.normal(ks[4], (D, D), dtype=jnp.float32) * scale
        W_V = jax.random.normal(ks[5], (D, D), dtype=jnp.float32) * scale
        W_O = jax.random.normal(ks[6], (D, D), dtype=jnp.float32) * scale
        return {'Q': Q, 'K': K, 'V': V, 'mask': mask, 'W_Q': W_Q, 'W_K': W_K, 'W_V': W_V, 'W_O': W_O}
    _L1_xattn_all = _L1_xattn_setup()
    _L1_xattn_in = {k: v for k, v in _L1_xattn_all.items() if k in ('W_Q', 'W_K', 'W_V', 'W_O')}
    del _L1_xattn_all

    def _L1_ffn_setup():
        import jax, jax.numpy as jnp
        import numpy as np
        MODEL_DIM = 256
        HIDDEN = 512
        NUM_GROUPS = 2
        EXPERTS_PER_GP = 4
        NUM_EXPERTS = NUM_GROUPS * EXPERTS_PER_GP
        TOP_K = 2
        B, T = (2, 512)

        def _swiglu(x):
            a, b = jnp.split(x, 2, axis=-1)
            return jax.nn.silu(a) * b
        key = jax.random.key(seed)
        ks = jax.random.split(key, 7)
        s = 0.02
        return {'x': jax.random.normal(ks[0], (B, T, MODEL_DIM), jnp.float32), 'w_in': jax.random.normal(ks[1], (HIDDEN * 2, MODEL_DIM), jnp.float32) * s, 'w_out': jax.random.normal(ks[2], (MODEL_DIM, HIDDEN), jnp.float32) * s, 'w1': jax.random.normal(ks[3], (HIDDEN * 2, MODEL_DIM), jnp.float32) * s, 'w2': jax.random.normal(ks[4], (NUM_EXPERTS, MODEL_DIM, HIDDEN), jnp.float32) * s, 'wg': jax.random.normal(ks[5], (NUM_GROUPS, MODEL_DIM), jnp.float32) * s, 'we': jax.random.normal(ks[6], (NUM_EXPERTS, MODEL_DIM), jnp.float32) * s, 'gb': jnp.zeros((NUM_GROUPS,), jnp.float32), 'eb': jnp.zeros((NUM_EXPERTS,), jnp.float32)}
    _L1_ffn_all = _L1_ffn_setup()
    _L1_ffn_in = {k: v for k, v in _L1_ffn_all.items() if k in ('w_in', 'w_out', 'w1', 'w2', 'wg', 'we', 'gb', 'eb')}
    del _L1_ffn_all
    return {'x': x, 'ctx_1024': ctx_1024, 'mask_Bx1xSxS2_ik0': mask_Bx1xSxS2_ik0, 'L0_attn_norm_w': _L0_attn_in['norm_w'], 'L0_attn_norm_b': _L0_attn_in['norm_b'], 'L0_attn_in_proj_w': _L0_attn_in['in_proj_w'], 'L0_attn_conv_w': _L0_attn_in['conv_w'], 'L0_attn_conv_b': _L0_attn_in['conv_b'], 'L0_attn_xproj_w': _L0_attn_in['xproj_w'], 'L0_attn_dtproj_w': _L0_attn_in['dtproj_w'], 'L0_attn_dtproj_b': _L0_attn_in['dtproj_b'], 'L0_attn_A_log': _L0_attn_in['A_log'], 'L0_attn_skip_D': _L0_attn_in['skip_D'], 'L0_attn_out_proj_w': _L0_attn_in['out_proj_w'], 'L0_attn_fn_w': _L0_attn_in['fn_w'], 'L0_attn_fn_b': _L0_attn_in['fn_b'], 'L0_xattn_Wq': _L0_xattn_in['Wq'], 'L0_xattn_bq': _L0_xattn_in['bq'], 'L0_xattn_Wk1': _L0_xattn_in['Wk1'], 'L0_xattn_bk1': _L0_xattn_in['bk1'], 'L0_xattn_Wk2': _L0_xattn_in['Wk2'], 'L0_xattn_bk2': _L0_xattn_in['bk2'], 'L0_xattn_Wv1': _L0_xattn_in['Wv1'], 'L0_xattn_bv1': _L0_xattn_in['bv1'], 'L0_xattn_Wv2': _L0_xattn_in['Wv2'], 'L0_xattn_bv2': _L0_xattn_in['bv2'], 'L0_xattn_Wo': _L0_xattn_in['Wo'], 'L0_xattn_bo': _L0_xattn_in['bo'], 'L0_xattn_g0': _L0_xattn_in['g0'], 'L0_xattn_beta0': _L0_xattn_in['beta0'], 'L0_xattn_g1': _L0_xattn_in['g1'], 'L0_xattn_beta1': _L0_xattn_in['beta1'], 'L0_ffn_ln1_scale': _L0_ffn_in['ln1_scale'], 'L0_ffn_ln1_shift': _L0_ffn_in['ln1_shift'], 'L0_ffn_wq': _L0_ffn_in['wq'], 'L0_ffn_wk': _L0_ffn_in['wk'], 'L0_ffn_wv': _L0_ffn_in['wv'], 'L0_ffn_wo': _L0_ffn_in['wo'], 'L0_ffn_bo': _L0_ffn_in['bo'], 'L0_ffn_ln2_scale': _L0_ffn_in['ln2_scale'], 'L0_ffn_ln2_shift': _L0_ffn_in['ln2_shift'], 'L0_ffn_gate_w': _L0_ffn_in['gate_w'], 'L0_ffn_w1': _L0_ffn_in['w1'], 'L0_ffn_w2': _L0_ffn_in['w2'], 'L0_ffn_w3': _L0_ffn_in['w3'], 'L1_attn_Wk': _L1_attn_in['Wk'], 'L1_attn_bk': _L1_attn_in['bk'], 'L1_attn_Wv': _L1_attn_in['Wv'], 'L1_attn_bv': _L1_attn_in['bv'], 'L1_attn_Wf': _L1_attn_in['Wf'], 'L1_attn_bf': _L1_attn_in['bf'], 'L1_xattn_W_Q': _L1_xattn_in['W_Q'], 'L1_xattn_W_K': _L1_xattn_in['W_K'], 'L1_xattn_W_V': _L1_xattn_in['W_V'], 'L1_xattn_W_O': _L1_xattn_in['W_O'], 'L1_ffn_w_in': _L1_ffn_in['w_in'], 'L1_ffn_w_out': _L1_ffn_in['w_out'], 'L1_ffn_w1': _L1_ffn_in['w1'], 'L1_ffn_w2': _L1_ffn_in['w2'], 'L1_ffn_wg': _L1_ffn_in['wg'], 'L1_ffn_we': _L1_ffn_in['we'], 'L1_ffn_gb': _L1_ffn_in['gb'], 'L1_ffn_eb': _L1_ffn_in['eb']}

def reference(x, ctx_1024, mask_Bx1xSxS2_ik0, L0_attn_norm_w, L0_attn_norm_b, L0_attn_in_proj_w, L0_attn_conv_w, L0_attn_conv_b, L0_attn_xproj_w, L0_attn_dtproj_w, L0_attn_dtproj_b, L0_attn_A_log, L0_attn_skip_D, L0_attn_out_proj_w, L0_attn_fn_w, L0_attn_fn_b, L0_xattn_Wq, L0_xattn_bq, L0_xattn_Wk1, L0_xattn_bk1, L0_xattn_Wk2, L0_xattn_bk2, L0_xattn_Wv1, L0_xattn_bv1, L0_xattn_Wv2, L0_xattn_bv2, L0_xattn_Wo, L0_xattn_bo, L0_xattn_g0, L0_xattn_beta0, L0_xattn_g1, L0_xattn_beta1, L0_ffn_ln1_scale, L0_ffn_ln1_shift, L0_ffn_wq, L0_ffn_wk, L0_ffn_wv, L0_ffn_wo, L0_ffn_bo, L0_ffn_ln2_scale, L0_ffn_ln2_shift, L0_ffn_gate_w, L0_ffn_w1, L0_ffn_w2, L0_ffn_w3, L1_attn_Wk, L1_attn_bk, L1_attn_Wv, L1_attn_bv, L1_attn_Wf, L1_attn_bf, L1_xattn_W_Q, L1_xattn_W_K, L1_xattn_W_V, L1_xattn_W_O, L1_ffn_w_in, L1_ffn_w_out, L1_ffn_w1, L1_ffn_w2, L1_ffn_wg, L1_ffn_we, L1_ffn_gb, L1_ffn_eb):
    import jax
    import jax.numpy as jnp

    def _L0_attn_ref(x, norm_w, norm_b, in_proj_w, conv_w, conv_b, xproj_w, dtproj_w, dtproj_b, A_log, skip_D, out_proj_w, fn_w, fn_b):
        import jax, jax.numpy as jnp
        import numpy as np
        D_MODEL = 256
        N_BLOCKS = 4
        D_STATE = 16
        D_CONV = 4
        EXPAND = 2
        DT_RANK = 64
        D_INNER = EXPAND * D_MODEL
        BATCH = 2
        SEQLEN = 256

        def _layer_norm(x, w, b):
            m = jnp.mean(x, -1, keepdims=True)
            v = jnp.mean((x - m) ** 2, -1, keepdims=True)
            return (x - m) * jax.lax.rsqrt(v + 1e-05) * w + b

        def _selective_scan(u, dt, A, Bm, Cm, Dp):
            dA = jnp.exp(dt[..., None] * A)
            dBu = (dt * u)[..., None] * Bm[:, :, None, :]

            def step(h, inp):
                dA_t, dBu_t, C_t = inp
                h = dA_t * h + dBu_t
                y = jnp.einsum('ben,bn->be', h, C_t)
                return (h, y)
            h0 = jnp.zeros((u.shape[0], u.shape[2], A.shape[1]), u.dtype)
            xs = (jnp.moveaxis(dA, 1, 0), jnp.moveaxis(dBu, 1, 0), jnp.moveaxis(Cm, 1, 0))
            _, ys = jax.lax.scan(step, h0, xs)
            y = jnp.moveaxis(ys, 0, 1)
            return y + u * Dp

        def _mamba(x, in_w, cw, cb, xw, dtw, dtb, A_log, Dp, ow):
            L = x.shape[1]
            xz = x @ in_w
            u, z = jnp.split(xz, 2, axis=-1)
            K = cw.shape[1]
            up = jnp.pad(u, ((0, 0), (K - 1, 0), (0, 0)))
            conv = cb + sum((up[:, k:k + L, :] * cw[:, k] for k in range(K)))
            u = jax.nn.silu(conv)
            dbl = u @ xw
            dt = jax.nn.softplus(dbl[..., :DT_RANK] @ dtw + dtb)
            Bm = dbl[..., DT_RANK:DT_RANK + D_STATE]
            Cm = dbl[..., DT_RANK + D_STATE:]
            A = -jnp.exp(A_log)
            y = _selective_scan(u, dt, A, Bm, Cm, Dp)
            y = y * jax.nn.silu(z)
            return y @ ow

        def _forward(x, norm_w, norm_b, in_proj_w, conv_w, conv_b, xproj_w, dtproj_w, dtproj_b, A_log, skip_D, out_proj_w, fn_w, fn_b):
            for i in range(N_BLOCKS):
                h = _layer_norm(x, norm_w[i], norm_b[i])
                h = _mamba(h, in_proj_w[i], conv_w[i], conv_b[i], xproj_w[i], dtproj_w[i], dtproj_b[i], A_log[i], skip_D[i], out_proj_w[i])
                x = x + h
            return _layer_norm(x, fn_w, fn_b)
        return _forward(x, norm_w, norm_b, in_proj_w, conv_w, conv_b, xproj_w, dtproj_w, dtproj_b, A_log, skip_D, out_proj_w, fn_w, fn_b)

    def _L0_xattn_ref(Q, K1, K2, Wq, bq, Wk1, bk1, Wk2, bk2, Wv1, bv1, Wv2, bv2, Wo, bo, g0, beta0, g1, beta1):
        import jax, jax.numpy as jnp
        import numpy as np
        DIM = 256
        H = 16
        DH = DIM // H
        LN_EPS = 1e-05

        def _linear_params(key, din, dout):
            kw, kb = jax.random.split(key)
            bound = 1.0 / np.sqrt(din)
            W = jax.random.uniform(kw, (din, dout), jnp.float32, -bound, bound)
            b = jax.random.uniform(kb, (dout,), jnp.float32, -bound, bound)
            return (W, b)

        def _layernorm(x, g, b):
            m = jnp.mean(x, axis=-1, keepdims=True)
            v = jnp.mean(jnp.square(x - m), axis=-1, keepdims=True)
            return (x - m) * jax.lax.rsqrt(v + LN_EPS) * g + b

        def _split_heads(x):
            B, N, _ = x.shape
            return x.reshape(B, N, H, DH).transpose(2, 0, 1, 3).reshape(H * B, N, DH)

        def _merge_heads(x, B):
            _, N, _ = x.shape
            return x.reshape(H, B, N, DH).transpose(1, 2, 0, 3).reshape(B, N, DIM)
        B = Q.shape[0]
        Qp = Q @ Wq + bq
        K1p = K1 @ Wk1 + bk1
        K2p = K2 @ Wk2 + bk2
        V1p = K1p @ Wv1 + bv1
        V2p = K2p @ Wv2 + bv2
        Q_ = _split_heads(Qp)
        K_ = jnp.concatenate([_split_heads(K1p), _split_heads(K2p)], axis=1)
        V_ = jnp.concatenate([_split_heads(V1p), _split_heads(V2p)], axis=1)
        scores = jnp.einsum('bqd,bkd->bqk', Q_, K_) / np.sqrt(DIM).astype(np.float32)
        A = jax.nn.softmax(scores, axis=1)
        out = Q_ + jnp.einsum('bqk,bkd->bqd', A, V_)
        out = _merge_heads(out, B)
        out = _layernorm(out, g0, beta0)
        out = out + jax.nn.relu(out @ Wo + bo)
        out = _layernorm(out, g1, beta1)
        return out

    def _L0_ffn_ref(x, ln1_scale, ln1_shift, wq, wk, wv, wo, bo, ln2_scale, ln2_shift, gate_w, w1, w2, w3):
        import jax, jax.numpy as jnp
        import numpy as np
        EMB = 256
        HID = 512
        HEADS = 16
        HEAD_DIM = EMB // HEADS
        EXPERTS = 8
        TOPK = 2
        EPS = 1e-05

        def layernorm(x, scale, shift):
            mean = jnp.mean(x, axis=-1, keepdims=True)
            var = jnp.mean((x - mean) ** 2, axis=-1, keepdims=True)
            return scale * (x - mean) / jnp.sqrt(var + EPS) + shift

        def attention(x, wq, wk, wv, wo, bo):
            b, t, _ = x.shape
            q = (x @ wq).reshape(b, t, HEADS, HEAD_DIM)
            k = (x @ wk).reshape(b, t, HEADS, HEAD_DIM)
            v = (x @ wv).reshape(b, t, HEADS, HEAD_DIM)
            scores = jnp.einsum('bqhd,bkhd->bhqk', q, k)
            mask = jnp.arange(t)[:, None] < jnp.arange(t)[None, :]
            scores = jnp.where(mask, -jnp.inf, scores)
            attn = jax.nn.softmax(scores / np.sqrt(HEAD_DIM), axis=-1)
            ctx = jnp.einsum('bhqk,bkhd->bqhd', attn, v).reshape(b, t, EMB)
            return ctx @ wo + bo

        def moe_ff(x, gate_w, w1, w2, w3):
            b, t, d = x.shape
            xf = x.reshape(b * t, d)
            scores = xf @ gate_w
            topk_scores, topk_idx = jax.lax.top_k(scores, TOPK)
            topk_probs = jax.nn.softmax(topk_scores, axis=-1)
            weight = jnp.sum(jax.nn.one_hot(topk_idx, EXPERTS, dtype=xf.dtype) * topk_probs[..., None], axis=1)
            h = jax.nn.silu(jnp.einsum('td,edh->eth', xf, w1)) * jnp.einsum('td,edh->eth', xf, w2)
            out_e = jnp.einsum('eth,ehd->etd', h, w3)
            out = jnp.einsum('etd,te->td', out_e, weight)
            return out.reshape(b, t, d)
        h = layernorm(x, ln1_scale, ln1_shift)
        x = x + attention(h, wq, wk, wv, wo, bo)
        h = layernorm(x, ln2_scale, ln2_shift)
        x = x + moe_ff(h, gate_w, w1, w2, w3)
        return x

    def _L1_attn_ref(x, Wk, bk, Wv, bv, Wf, bf):
        import jax, jax.numpy as jnp
        import numpy as np
        D_MODEL = 256
        N_HEADS = 16
        D_HIDDEN = 1024
        BATCH = 2
        N_CTX = 512

        def _split_heads(t, n_heads):
            B, S, D = t.shape
            return t.reshape(B, S, n_heads, D // n_heads).transpose(0, 2, 1, 3)
        B, S, D = x.shape
        H = N_HEADS
        Q = _split_heads(x, H)
        K = _split_heads(x @ Wk + bk, H)
        V = _split_heads(x @ Wv + bv, H)
        causal = jnp.tril(jnp.ones((S, S), dtype=bool))
        mask = jnp.where(causal, 0.0, -jnp.inf).astype(x.dtype)
        scores = jnp.einsum('bhqd,bhkd->bhqk', Q, K) + mask
        attn = jax.nn.softmax(scores, axis=-1)
        o = jnp.einsum('bhqk,bhkd->bhqd', attn, V)
        o = o.transpose(0, 2, 1, 3).reshape(B, S, -1)
        return x + jax.nn.gelu(o, approximate=False) @ Wf + bf

    def _L1_xattn_ref(Q, K, V, mask, W_Q, W_K, W_V, W_O):
        import jax, jax.numpy as jnp
        import numpy as np
        B, S, D, H = (4, 512, 256, 16)
        DK = D // H

        def _split_heads(x):
            b, s, _ = x.shape
            return x.reshape(b, s, H, DK).transpose(0, 2, 1, 3)
        q = _split_heads(Q @ W_Q.T)
        k = _split_heads(K @ W_K.T)
        v = _split_heads(V @ W_V.T)
        scores = jnp.einsum('bhqd,bhkd->bhqk', q, k) / jnp.sqrt(jnp.float32(DK))
        scores = jnp.where(mask == 0, -jnp.inf, scores)
        weights = jax.nn.softmax(scores, axis=-1)
        weights = jnp.nan_to_num(weights, nan=0.0)
        attn = jnp.einsum('bhqk,bhkd->bhqd', weights, v)
        attn = attn.transpose(0, 2, 1, 3).reshape(Q.shape[0], Q.shape[1], D)
        return attn @ W_O.T

    def _L1_ffn_ref(x, w_in, w_out, w1, w2, wg, we, gb, eb):
        import jax, jax.numpy as jnp
        import numpy as np
        MODEL_DIM = 256
        HIDDEN = 512
        NUM_GROUPS = 2
        EXPERTS_PER_GP = 4
        NUM_EXPERTS = NUM_GROUPS * EXPERTS_PER_GP
        TOP_K = 2
        B, T = (2, 512)

        def _swiglu(x):
            a, b = jnp.split(x, 2, axis=-1)
            return jax.nn.silu(a) * b
        Bs, Ts, C = x.shape
        S = Bs * Ts
        flat = x.reshape(S, C)
        shared = _swiglu(flat @ w_in.T) @ w_out.T
        g_probs = jax.nn.softmax(flat @ wg.T + gb, axis=-1)
        g_idx = jnp.argmax(g_probs, axis=-1)
        e_logits = flat @ we.T + eb
        egid = jnp.arange(NUM_EXPERTS) // EXPERTS_PER_GP
        masked = jnp.where(g_idx[:, None] == egid[None, :], e_logits, -jnp.inf)
        e_probs = jax.nn.softmax(masked, axis=-1)
        g_prob = jnp.take_along_axis(g_probs, g_idx[:, None], axis=1)
        p_expert = e_probs * g_prob
        topv, topi = jax.lax.top_k(p_expert, TOP_K)
        w_se = jnp.zeros((S, NUM_EXPERTS), x.dtype).at[jnp.arange(S)[:, None], topi].add(topv)
        h = _swiglu(flat @ w1.T)
        routed = jnp.zeros_like(shared)
        for e in range(NUM_EXPERTS):
            routed = routed + h * w_se[:, e:e + 1] @ w2[e].T
        return (shared + routed).reshape(Bs, Ts, C)
    x = _layernorm(x + _L0_attn_ref(x, L0_attn_norm_w, L0_attn_norm_b, L0_attn_in_proj_w, L0_attn_conv_w, L0_attn_conv_b, L0_attn_xproj_w, L0_attn_dtproj_w, L0_attn_dtproj_b, L0_attn_A_log, L0_attn_skip_D, L0_attn_out_proj_w, L0_attn_fn_w, L0_attn_fn_b), axis=-1)
    x = _layernorm(x + _L0_xattn_ref(x, ctx_1024, ctx_1024, L0_xattn_Wq, L0_xattn_bq, L0_xattn_Wk1, L0_xattn_bk1, L0_xattn_Wk2, L0_xattn_bk2, L0_xattn_Wv1, L0_xattn_bv1, L0_xattn_Wv2, L0_xattn_bv2, L0_xattn_Wo, L0_xattn_bo, L0_xattn_g0, L0_xattn_beta0, L0_xattn_g1, L0_xattn_beta1), axis=-1)
    x = _layernorm(x + _L0_ffn_ref(x, L0_ffn_ln1_scale, L0_ffn_ln1_shift, L0_ffn_wq, L0_ffn_wk, L0_ffn_wv, L0_ffn_wo, L0_ffn_bo, L0_ffn_ln2_scale, L0_ffn_ln2_shift, L0_ffn_gate_w, L0_ffn_w1, L0_ffn_w2, L0_ffn_w3), axis=-1)
    x = _layernorm(x + _L1_attn_ref(x, L1_attn_Wk, L1_attn_bk, L1_attn_Wv, L1_attn_bv, L1_attn_Wf, L1_attn_bf), axis=-1)
    x = _layernorm(x + _L1_xattn_ref(x, ctx_1024, ctx_1024, mask_Bx1xSxS2_ik0, L1_xattn_W_Q, L1_xattn_W_K, L1_xattn_W_V, L1_xattn_W_O), axis=-1)
    x = _layernorm(x + _L1_ffn_ref(x, L1_ffn_w_in, L1_ffn_w_out, L1_ffn_w1, L1_ffn_w2, L1_ffn_wg, L1_ffn_we, L1_ffn_gb, L1_ffn_eb), axis=-1)
    return x

_drawn_inputs = setup_inputs


def setup_inputs(seed=0):
    import zlib

    import numpy as np

    out = dict(_drawn_inputs(seed))
    spreads = {'L0_attn_norm_w': (1.0, 0.6),
     'L0_attn_norm_b': (0.0, 0.8),
     'L0_attn_conv_b': (0.0, 0.594),
     'L0_attn_dtproj_b': (-4.599999904632568, 0.6),
     'L0_attn_skip_D': (1.0, 0.6),
     'L0_attn_fn_w': (1.0, 0.2),
     'L0_attn_fn_b': (0.0, 0.1),
     'L0_xattn_g0': (1.0, 0.2),
     'L0_xattn_beta0': (0.0, 0.1),
     'L0_xattn_g1': (1.0, 0.2),
     'L0_xattn_beta1': (0.0, 0.1),
     'L0_ffn_ln1_scale': (1.0, 0.2),
     'L0_ffn_ln1_shift': (0.0, 0.1),
     'L0_ffn_bo': (0.0, 0.1),
     'L0_ffn_ln2_scale': (1.0, 0.2),
     'L0_ffn_ln2_shift': (0.0, 0.1),
     'L1_attn_bk': (0.0, 2.0),
     'L1_attn_bv': (0.0, 0.529),
     'L1_attn_bf': (0.0, 0.1),
     'L1_ffn_gb': (0.0, 0.8),
     'L1_ffn_eb': (0.0, 0.8)}
    factors = {'L0_attn_in_proj_w': 5.491,
     'L0_attn_conv_w': 8.0,
     'L0_attn_xproj_w': 8.0,
     'L0_attn_dtproj_w': 8.0,
     'L0_attn_A_log': 8.0,
     'L0_attn_out_proj_w': 5.09,
     'L0_xattn_bk1': 6.004,
     'L0_xattn_bk2': 7.635,
     'L0_xattn_bv1': 5.074,
     'L0_xattn_bv2': 4.838,
     'L1_attn_Wk': 7.706,
     'L1_attn_Wv': 5.23,
     'L1_attn_Wf': 3.101,
     'L1_ffn_w1': 8.0,
     'L1_ffn_w2': 8.0,
     'L1_ffn_wg': 8.0,
     'L1_ffn_we': 8.0,
     'L1_ffn_w_in': 8.0,
     'L1_ffn_w_out': 8.0}
    for name, (base, spread) in spreads.items():
        noise = np.random.default_rng([zlib.crc32(name.encode()), seed]).standard_normal(out[name].shape)
        drawn = base * np.exp(spread * noise) if base else spread * noise
        out[name] = jnp.asarray(drawn.astype(out[name].dtype))
    for name, factor in factors.items():
        out[name] = (out[name] * factor).astype(out[name].dtype)
    return out
```

```python
from contextlib import ExitStack

import concourse.bass as bass
from concourse import mybir

F32 = mybir.dt.float32
BF16 = mybir.dt.bfloat16
I32 = mybir.dt.int32
ALU = mybir.AluOpType
ACT = mybir.ActivationFunctionType
AX_X = mybir.AxisListType.X

P = 128
D = 256
DC = D // P
B = 2
S = 1024
TOK = B * S
NT = TOK // P
BT = S // P
BANK = 512
EPS = 1e-5
ARENA = 52480


class Shared:

    def __init__(self, nc, ctx, ins, out):
        self.nc, self.ctx, self.ins, self.out = nc, ctx, ins, out
        self.arena = ctx.enter_context(nc.sbuf_tensor("arena", [P, ARENA], F32))
        self.psum = ctx.enter_context(nc.psum_tensor("psum", [P, 8, BANK], F32))
        self.top = 0
        self.x = self.take("p (t d) -> p t d", NT * D, t=NT)
        self.ident = self.take(None, P)
        self.ident_bf = self.take(None, P // 2).bitcast(BF16)
        self.ones_row = self.take(None, P)
        self.ones_bf = self.take(None, P // 2).bitcast(BF16)
        self.phase, self.phase_sems = 0, []
        self.const_ready = ctx.enter_context(nc.semaphore("const_ready"))
        self.constants = (self.const_ready, 8)
        self.done = self.constants

    def norm_all(self):
        self.norm = Norm(self, "norm", NT)
        self.norm_runs = 0
        self.turn = Turn(self)

    def take(self, pattern, count, **sizes):
        assert self.top + count <= ARENA, (self.top, count)
        view = self.arena[:, self.top:self.top + count]
        self.top += count
        return view.rearrange(pattern, **sizes) if pattern else view

    def wait_apart(self, eng, sem, value):
        eng.wait_ge(self.const_ready, 1)
        eng.wait_ge(sem, value)

    def sem(self, name):
        handle = self.nc.alloc_semaphore(name=f"phase{self.phase}_{name}")
        self.phase_sems.append(handle)
        return handle


def constants(sh):
    def pool(eng):
        eng.memset(sh.ident, 0.0).then_inc(sh.const_ready, 1)
        eng.memset(sh.ident_bf, 0.0).then_inc(sh.const_ready, 1)
        eng.memset(sh.ones_row, 1.0).then_inc(sh.const_ready, 1)
        eng.memset(sh.ones_bf, 1.0).then_inc(sh.const_ready, 1)
        eng.wait_ge(sh.const_ready, 4)
        eng.affine_select(out=sh.ident, in_=sh.ident, compare_op=ALU.not_equal, fill=1.0, base=0,
                          pattern=[[-1, P]], channel_multiplier=1).then_inc(sh.const_ready, 2)
        eng.affine_select(out=sh.ident_bf, in_=sh.ident_bf, compare_op=ALU.not_equal, fill=1.0, base=0,
                          pattern=[[-1, P]], channel_multiplier=1).then_inc(sh.const_ready, 2)
    return {"pool": pool}


class Norm:

    def __init__(self, sh, name, tiles):
        self.sh = sh
        self.tiles = tiles
        self.bn = sh.take("p (t k) -> p t k", tiles * 6, t=tiles)
        self.mv = sh.take("p (t k) -> p t k", tiles * 2, t=tiles)
        self.std = sh.take(None, tiles)
        self.rstd = sh.take(None, tiles)
        self.stats = sh.sem(name + "_stats")
        self.std_ready = sh.sem(name + "_std")
        self.normed = sh.sem(name + "_normed")

    def stats_tile(self, eng, src, t):
        eng.bn_stats(self.bn[:, t, :], src).then_inc(self.stats, 1)

    def aggregate(self, eng, rep=0):
        n = self.tiles
        eng.wait_ge(self.stats, rep * (2 * n + 2) + n)
        eng.memset(self.rstd[:, 0:1], 0.0)
        for t in range(n):
            eng.bn_aggr(self.mv[:, t, :], self.bn[:, t, :]).then_inc(self.stats, 1)
        eng.wait_ge(self.stats, rep * (2 * n + 2) + 2 * n)
        eng.tensor_scalar(self.std, self.mv[:, :, 1], EPS, None, ALU.add).then_inc(self.stats, 1)

    def vector(self, eng, src, dst, rep=0, wait_std=True):
        n = self.tiles
        for t in range(n):
            self.stats_tile(eng, src(t), t)
        self.aggregate(eng, rep)
        self.normalize(eng, src, dst, rep)

    def normalize(self, eng, src, dst, rep=0):
        n = self.tiles
        eng.wait_ge(self.std_ready, rep + 1)
        eng.reciprocal(self.rstd, self.std).then_inc(self.stats, 1)
        eng.wait_ge(self.stats, rep * (2 * n + 2) + 2 * n + 2)
        for t in range(n):
            eng.tensor_scalar(dst(t), src(t), self.mv[:, t, 0:1], self.rstd[:, t:t + 1],
                              ALU.subtract, ALU.mult).then_inc(self.normed, 1)

    def scalar(self, eng, rep=0):
        n = self.tiles
        eng.wait_ge(self.stats, rep * (2 * n + 2) + 2 * n + 1)
        eng.activation(self.std, self.std, ACT.Sqrt).then_inc(self.std_ready, 1)

    def use(self):
        self.sh.norm_runs += 1
        return self.sh.norm_runs - 1


class Turn:

    def __init__(self, sh):
        self.sh = sh
        self.turned, self.taken = sh.sem("turned"), sh.sem("turn_taken")
        self.runs = 0

    def use(self):
        self.runs += 1
        return self.runs - 1

    def tensor(self, eng, src, run, ready):
        for c in range(DC):
            for q in range(NT // 4):
                for t in range(4):
                    if c == 0:
                        ready(eng, 4 * q + t)
                    mm = eng.transpose(self.sh.psum[:, 4 * c + q, t * P:(t + 1) * P],
                                       src(4 * q + t, c), self.sh.ident)
                mm.then_inc(self.turned, 1)

    def scalar(self, eng, dst, run, scale=None, bias=None):
        for c in range(DC):
            for q in range(NT // 4):
                eng.wait_ge(self.turned, 8 * run + 4 * c + q + 1)
                if scale is None:
                    ins = eng.activation(dst[:, c, q * BANK:(q + 1) * BANK], self.sh.psum[:, 4 * c + q, :], ACT.Copy)
                else:
                    ins = eng.activation(dst[:, c, q * BANK:(q + 1) * BANK], self.sh.psum[:, 4 * c + q, :],
                                         ACT.Identity, bias=bias[:, c:c + 1], scale=scale[:, c:c + 1])
                ins.then_inc(self.taken, 1)


def feature_columns(ap):
    return ap.rearrange("(c p) -> p c", p=P)


def on_all_partitions(ap, n=P):
    return ap.rearrange("(o d) -> o d", o=1).broadcast_to([n, ap.shape[0]])


FR = mybir.dt.float32r
HIGH = -4096


def high_part(eng, dst, src):
    return eng.tensor_scalar(dst.bitcast(I32), src.bitcast(I32), HIGH, None, ALU.bitwise_and)


def product_of_parts(eng, dst, a, b, first, last):
    (ah, al), (bh, bl) = [[part.bitcast(FR) for part in pair] for pair in (a, b)]
    eng.matmul(dst, ah, bh, start=first, stop=False)
    eng.matmul(dst, ah, bl, start=False, stop=False)
    return eng.matmul(dst, al, bh, start=False, stop=last)


def mamba(sh):
    nc, ins, ps = sh.nc, sh.ins, sh.psum
    NB, E, NS, R, KC = 4, 512, 16, 64, 4
    M = E // P
    H = S // BANK
    U = NS * M
    mark = sh.top
    w_in = sh.take("p (c n) -> p c n", DC * 2 * E, c=DC)
    w_x = sh.take("p (m n) -> p m n", M * (R + 2 * NS), m=M)
    w_dt = sh.take(None, E)
    w_out = sh.take("p (m n) -> p m n", M * D, m=M)
    n_w = sh.take(None, DC)
    n_b = sh.take(None, DC)
    cw = sh.take("p (m k) -> p m k", M * KC, m=M)
    cb = sh.take(None, M)
    dtb = sh.take(None, M)
    skip = sh.take(None, M)
    a_log = sh.take("p (m n) -> p m n", M * NS, m=M)
    a_exp = sh.take("p (m n) -> p m n", M * NS, m=M)
    a_neg = sh.take("p (m n) -> p m n", M * NS, m=M)
    skip_diag = sh.take("p (m q) -> p m q", M * P, m=M)
    PAD = KC - 1
    u_in = sh.take("p (m s) -> p m s", M * (PAD + S), m=M)
    sz = sh.take("p (m s) -> p m s", M * S, m=M)
    uc = sh.take("p (m s) -> p m s", M * S, m=M)
    dt = sh.take("p (m s) -> p m s", M * S, m=M)
    dtu = sh.take("p (m s) -> p m s", M * S, m=M)
    dt_low = sh.take(None, S)
    bc = u_in[:, 0, PAD:PAD + S]
    rest = u_in[:, 1, PAD:PAD + S]
    mid0 = u_in[:, 2, PAD:PAD + S // 2].bitcast(BF16)
    parts = sh.take(None, S // 2).bitcast(BF16)
    sel = sh.take("p (n q) -> p n q", 2 * NS * P // 2, n=2 * NS).bitcast(BF16)
    decay = sh.take("p (r m s) -> p r m s", 2 * M * BANK, r=2, m=M)
    drive = sh.take("p (r m s) -> p r m s", 2 * M * BANK, r=2, m=M)
    h = sh.take("p (r m s) -> p r m s", 2 * M * BANK, r=2, m=M)
    hc = sh.take("p (r m s) -> p r m s", 2 * M * BANK, r=2, m=M)
    hn = hc[:, 0].rearrange("p m s -> p (m s)").rearrange("p (t d) -> p t d", t=BT)
    hT = hc[:, 1].rearrange("p m s -> p (m s)").rearrange("p (c s) -> p c s", c=DC)
    b_sb = sh.take("p (r s) -> p r s", 2 * BANK, r=2)
    spare = sh.take(None, 1)
    carry = sh.take("p (n m) -> p n m", NS * M, n=NS)
    log_y = drive.rearrange("p r m s -> p (r m s)").rearrange("p (m s) -> p m s", m=M)
    rem = decay.rearrange("p r m s -> p (r m s)").rearrange("p (m s) -> p m s", m=M)
    norm = Norm(sh, "mb_norm", BT)

    x_loaded = sh.sem("mb_x_loaded")
    w_loaded = sh.sem("mb_w_loaded")
    sel_ready = sh.sem("mb_sel_ready")
    diag_ready, a_exped, a_ready = sh.sem("mb_diag_ready"), sh.sem("mb_a_exped"), sh.sem("mb_a_ready")
    turned = sh.sem("mb_turned")
    ht_ready = sh.sem("mb_ht_ready")
    u_done, u_copied = sh.sem("mb_u_done"), sh.sem("mb_u_copied")
    z_done, z_gated = sh.sem("mb_z_done"), sh.sem("mb_z_gated")
    tapped, conv = sh.sem("mb_tapped"), sh.sem("mb_conv")
    uc_ready = sh.sem("mb_uc_ready")
    xp_done, xp_copied = sh.sem("mb_xp_done"), sh.sem("mb_xp_copied")
    dt_done, v_ready = sh.sem("mb_dt_done"), sh.sem("mb_v_ready")
    neg_ready, ey_ready, rem_ready = sh.sem("mb_neg"), sh.sem("mb_ey"), sh.sem("mb_rem")
    corr_ready, log_ready, soft_ready = sh.sem("mb_corr"), sh.sem("mb_log"), sh.sem("mb_soft")
    dt_ready, dtu_ready = sh.sem("mb_dt_ready"), sh.sem("mb_dtu_ready")
    b_spread, c_spread, b_copied = sh.sem("mb_b_spread"), sh.sem("mb_c_spread"), sh.sem("mb_b_copied")
    decay_ready, drive_ready = sh.sem("mb_decay"), sh.sem("mb_drive")
    scanned, weighted, summed = sh.sem("mb_scanned"), sh.sem("mb_weighted"), sh.sem("mb_summed")
    y_gated = sh.sem("mb_y_gated")
    o_done, x_done = sh.sem("mb_o_done"), sh.sem("mb_x_done")
    carried = sh.sem("mb_carried")
    NW = 11
    CT = KC - 1
    ZM = 3
    CREDIT = 2 * M

    def sync(eng):
        eng.dma_start(sh.x, ins["x"].rearrange("b (t p) d -> p (b t) d", p=P)).then_inc(x_loaded, 16)

        def load(i):
            for dst, src in (
                (w_in, ins["L0_attn_in_proj_w"][i].rearrange("(c p) n -> p c n", p=P)),
                (w_x, ins["L0_attn_xproj_w"][i].rearrange("(m p) n -> p m n", p=P)),
                (w_dt[0:R, :], ins["L0_attn_dtproj_w"][i]),
                (w_out, ins["L0_attn_out_proj_w"][i].rearrange("(m p) n -> p m n", p=P)),
                (n_w, ins["L0_attn_norm_w"][i].rearrange("(c p) -> p c", p=P)),
                (n_b, ins["L0_attn_norm_b"][i].rearrange("(c p) -> p c", p=P)),
                (cw, ins["L0_attn_conv_w"][i].rearrange("(m p) k -> p m k", p=P)),
                (cb, ins["L0_attn_conv_b"][i].rearrange("(m p) -> p m", p=P)),
                (dtb, ins["L0_attn_dtproj_b"][i].rearrange("(m p) -> p m", p=P)),
                (skip, ins["L0_attn_skip_D"][i].rearrange("(m p) -> p m", p=P)),
                (a_log, ins["L0_attn_A_log"][i].rearrange("(m p) n -> p m n", p=P)),
            ):
                eng.dma_start(dst, src, allow_slow_non_contiguous=True).then_inc(w_loaded, 16)

        load(0)
        with eng.Fori(0, NB - 1) as i:
            eng.wait_ge(x_done, (i + 1) * (B * BT // 2))
            load(i + 1)

    def pool(eng):
        eng.memset(u_in[:, :, 0:PAD], 0.0).then_inc(sel_ready, 1)
        eng.memset(b_sb[:, 0, 0:1], 0.0).then_inc(drive_ready, CREDIT)
        eng.memset(sel, 0.0).then_inc(sel_ready, 1)
        for part in range(3):
            eng.wait_ge(sel_ready, part + 2)
            eng.affine_select(out=sel, in_=sel, compare_op=ALU.not_equal, fill=1.0, base=-32 * part,
                              pattern=[[-1, 2 * NS], [0, P]], channel_multiplier=1).then_inc(sel_ready, 1)
        with eng.Fori(0, NB) as i:
            with eng.Fori(0, B) as b:
                k = i * B + b
                eng.wait_ge(w_loaded, (i + 1) * (16 * NW))
                eng.wait_ge(uc_ready, k * M + 1)
                for m in range(M):
                    eng.tensor_tensor(skip_diag[:, m, :], sh.ident, skip[:, m:m + 1].to_broadcast([P, P]),
                                      ALU.mult).then_inc(diag_ready, 1)
                for m in range(M):
                    eng.wait_ge(rem_ready, k * M + m + 1)
                    eng.tensor_tensor(rem[:, m, :], dtu[:, m, :], rem[:, m, :], ALU.subtract)\
                        .then_inc(corr_ready, 1)
                sh.wait_apart(eng, dtu_ready, k * M + M)
                for s in range(H):
                    with eng.Fori(0, NS // 2) as pair:
                        for r in range(2):
                            n = (k * H + s) * NS + pair * 2 + r
                            eng.wait_ge(b_copied, n + 1)
                            for m in range(M):
                                eng.wait_ge(scanned, n * M + m + 1)
                                eng.tensor_tensor(drive[:, r, m, :], dtu[:, m, s * BANK:(s + 1) * BANK],
                                                  b_sb[:, r, :], ALU.mult).then_inc(drive_ready, 1)

    def scalar(eng):
        with eng.Fori(0, NB) as i:
            with eng.Fori(0, B) as b:
                k = i * B + b
                norm.scalar(eng, k)
                for c in range(DC):
                    for s in range(H):
                        eng.wait_ge(turned, k * (DC * H) + c * H + s + 1)
                        if c == 0 and s == 0:
                            eng.wait_ge(w_loaded, (i + 1) * (16 * NW))
                        eng.activation(hT[:, c, s * BANK:(s + 1) * BANK], ps[:, c * H + s, :], ACT.Identity,
                                       bias=n_b[:, c:c + 1], scale=n_w[:, c:c + 1]).then_inc(ht_ready, 1)
                for m in range(M):
                    for s in range(H):
                        eng.wait_ge(u_done, k * (M * H) + m * H + s + 1)
                        eng.activation(u_in[:, m, PAD + s * BANK:PAD + (s + 1) * BANK],
                                       ps[:, (m * H + s) % 8, :], ACT.Copy).then_inc(u_copied, 1)
                    eng.wait_ge(u_copied, k * (M * H) + (m + 1) * H)
                    eng.activation(uc[:, m, :], u_in[:, m, PAD:PAD + S], ACT.Identity, bias=cb[:, m:m + 1],
                                   scale=cw[:, m, PAD:PAD + 1]).then_inc(tapped, 1)

                def gate(m):
                    for s in range(H):
                        eng.wait_ge(z_done, k * (M * H) + m * H + s + 1)
                        eng.activation(sz[:, m, s * BANK:(s + 1) * BANK], ps[:, (m * H + s) % (ZM * H), :],
                                       ACT.Silu).then_inc(z_gated, 1)

                for m in range(M):
                    if m < ZM:
                        gate(m)
                    eng.wait_ge(conv, k * (CT * M) + (m + 1) * CT)
                    eng.activation(uc[:, m, :], uc[:, m, :], ACT.Silu).then_inc(uc_ready, 1)
                for m in range(M):
                    for s in range(H):
                        eng.wait_ge(dt_done, k * (M * H) + m * H + s + 1)
                        eng.activation(dt[:, m, s * BANK:(s + 1) * BANK], ps[:, (m * H + s) % 8, :],
                                       ACT.Identity, bias=dtb[:, m:m + 1]).then_inc(v_ready, 1)
                for m in range(M):
                    eng.wait_ge(neg_ready, k * M + m + 1)
                    eng.activation(dtu[:, m, :], dtu[:, m, :], ACT.Exp).then_inc(ey_ready, 1)
                eng.activation(a_exp, a_log, ACT.Exp).then_inc(a_exped, 1)
                for m in range(M):
                    eng.wait_ge(ey_ready, k * M + m + 1)
                    eng.activation(log_y[:, m, :], dtu[:, m, :], ACT.Ln, bias=1.0).then_inc(log_ready, 1)
                for m in range(ZM, M):
                    gate(m)
                eng.wait_ge(dtu_ready, k * M + M)
                for s in range(H):
                    def copy_b(n, r):
                        eng.wait_ge(b_spread, n + 1)
                        eng.wait_ge(drive_ready, (n + 1) * M)
                        eng.activation(b_sb[:, r, :], ps[:, 4 + r, :], ACT.Copy).then_inc(b_copied, 1)

                    def decays(n, state, r):
                        for m in range(M):
                            eng.wait_ge(scanned, n * M + m + 1)
                            eng.activation(decay[:, r, m, :], dt[:, m, s * BANK:(s + 1) * BANK], ACT.Exp,
                                           scale=a_neg[:, m, bass.ds(state, 1)]).then_inc(decay_ready, 1)

                    with eng.Fori(0, NS // 2) as pair:
                        for r in range(2):
                            n = (k * H + s) * NS + pair * 2 + r
                            copy_b(n, r)
                            decays(n, pair * 2 + r, r)

    def vector(eng):
        eng.memset(carry[:, 0, :], 0.0).then_inc(scanned, CREDIT)
        eng.wait_ge(x_loaded, 16)
        eng.wait_ge(sel_ready, 1)
        with eng.Fori(0, NB) as i:
            with eng.Fori(0, B) as b:
                k = i * B + b
                norm.vector(eng, lambda t: sh.x[:, b * BT + t, :], lambda t: hn[:, t, :], k)
                for m in range(M):
                    eng.wait_ge(tapped, k * M + m + 1)
                    for tap in range(KC - 2, -1, -1):
                        n = k * (CT * M) + m * CT + (CT - 1 - tap)
                        if tap < KC - 2:
                            eng.wait_ge(conv, n)
                        eng.scalar_tensor_tensor(out=uc[:, m, :], in0=u_in[:, m, tap:tap + S],
                                                 scalar=cw[:, m, tap:tap + 1], in1=uc[:, m, :],
                                                 op0=ALU.mult, op1=ALU.add).then_inc(conv, 1)
                eng.wait_ge(conv, k * (CT * M) + CT * M)
                for s in range(H):
                    cols = slice(s * BANK, (s + 1) * BANK)
                    eng.wait_ge(xp_done, k * H + s + 1)
                    eng.tensor_copy(dt_low[0:R, cols], ps[0:R, 6 + s, :]).then_inc(xp_copied, 1)
                    eng.tensor_copy(bc[0:32, cols], ps[R:R + 32, 6 + s, :]).then_inc(xp_copied, 1)
                XP = 2 * H + 6
                eng.wait_ge(xp_copied, k * XP + 2 * H)
                eng.tensor_copy(parts[0:32, :], bc[0:32, :]).then_inc(xp_copied, 1)
                eng.wait_ge(xp_copied, k * XP + 2 * H + 1)
                eng.tensor_tensor(rest[0:32, :], bc[0:32, :], parts[0:32, :], ALU.subtract).then_inc(xp_copied, 1)
                eng.wait_ge(xp_copied, k * XP + 2 * H + 2)
                eng.tensor_copy(mid0[0:32, :], rest[0:32, :]).then_inc(xp_copied, 1)
                eng.wait_ge(xp_copied, k * XP + 2 * H + 3)
                eng.tensor_copy(parts[32:64, :], mid0[0:32, :]).then_inc(xp_copied, 1)
                eng.tensor_tensor(rest[0:32, :], rest[0:32, :], mid0[0:32, :], ALU.subtract).then_inc(xp_copied, 1)
                eng.wait_ge(xp_copied, k * XP + 2 * H + 5)
                eng.tensor_copy(parts[64:96, :], rest[0:32, :]).then_inc(xp_copied, 1)
                for m in range(M):
                    eng.wait_ge(v_ready, k * (M * H) + (m + 1) * H)
                    eng.scalar_tensor_tensor(out=dtu[:, m, :], in0=dt[:, m, :], scalar=-1.0, in1=dt[:, m, :],
                                             op0=ALU.mult, op1=ALU.min).then_inc(neg_ready, 1)
                for m in range(M):
                    eng.wait_ge(ey_ready, k * M + m + 1)
                    eng.tensor_scalar(rem[:, m, :], dtu[:, m, :], 1.0, 1.0, ALU.add, ALU.subtract)\
                        .then_inc(rem_ready, 1)
                for m in range(M):
                    eng.wait_ge(log_ready, k * M + m + 1)
                    eng.scalar_tensor_tensor(out=dt[:, m, :], in0=dt[:, m, :], scalar=0.0, in1=log_y[:, m, :],
                                             op0=ALU.max, op1=ALU.add).then_inc(soft_ready, 1)
                for m in range(M):
                    eng.wait_ge(soft_ready, k * M + m + 1)
                    eng.wait_ge(corr_ready, k * M + m + 1)
                    eng.tensor_tensor(dt[:, m, :], dt[:, m, :], rem[:, m, :], ALU.add).then_inc(dt_ready, 1)
                eng.wait_ge(a_exped, k + 1)
                eng.tensor_scalar(a_neg, a_exp, -1.0, None, ALU.mult).then_inc(a_ready, 1)
                for m in range(M):
                    eng.wait_ge(dt_ready, k * M + m + 1)
                    eng.tensor_tensor(dtu[:, m, :], dt[:, m, :], uc[:, m, :], ALU.mult).then_inc(dtu_ready, 1)

                def state_step(s, n, state, r):
                    def scan(m):
                        eng.wait_ge(decay_ready, n * M + m + 1)
                        eng.wait_ge(drive_ready, CREDIT + n * M + m + 1)
                        first = 0.0 if s == 0 else carry[:, bass.ds(state, 1), m]
                        eng.tensor_tensor_scan(h[:, r, m, :], decay[:, r, m, :], drive[:, r, m, :], first,
                                               ALU.mult, ALU.add).then_inc(scanned, 1)

                    def weigh(m):
                        if m == 0:
                            eng.wait_ge(c_spread, n + 1)
                        eng.wait_ge(scanned, CREDIT + n * M + m + 1)
                        eng.tensor_tensor(hc[:, r, m, :], h[:, r, m, :], ps[:, 6 + r, :], ALU.mult)\
                            .then_inc(weighted, 1)

                    scan(0)
                    for m in range(1, M):
                        scan(m)
                        weigh(m - 1)
                    weigh(M - 1)
                    if s < H - 1:
                        eng.tensor_copy(carry[:, bass.ds(state, 1), :].rearrange("p o m -> p (o m)"),
                                        h[:, r, :, BANK - 1]).then_inc(carried, 1)

                for s in range(H):
                    if s > 0:
                        eng.wait_ge(carried, k * (NS * (H - 1)) + NS * s)
                        eng.memset(spare, 0.0)
                    with eng.Fori(0, NS // 2) as pair:
                        for r in range(2):
                            state_step(s, (k * H + s) * NS + pair * 2 + r, pair * 2 + r, r)
                    for m in range(M):
                        eng.wait_ge(summed, (k * H + s) * M + m + 1)
                        cols = slice(s * BANK, (s + 1) * BANK)
                        eng.tensor_tensor(sz[:, m, cols], ps[:, m, :], sz[:, m, cols], ALU.mult)\
                            .then_inc(y_gated, 1)
                for j in range(BT // 2):
                    eng.wait_ge(o_done, k * (BT // 2) + j + 1)
                    tiles = sh.x[:, bass.ds(b * BT + 2 * j, 2), :]
                    eng.tensor_tensor(tiles, tiles, ps[:, 4 + j, :].rearrange("p (t d) -> p t d", t=2), ALU.add)\
                        .then_inc(x_done, 1)

    def tensor(eng):
        eng.wait_ge(*sh.constants)
        eng.wait_ge(sel_ready, 5)
        with eng.Fori(0, NB) as i:
            with eng.Fori(0, B) as b:
                k = i * B + b
                for c in range(DC):
                    for s in range(H):
                        for t in range(BT // H):
                            if c == 0:
                                eng.wait_ge(norm.normed, k * BT + s * (BT // H) + t + 1)
                            mm = eng.transpose(ps[:, c * H + s, t * P:(t + 1) * P],
                                               hn[:, s * (BT // H) + t, c * P:(c + 1) * P], sh.ident)
                        mm.then_inc(turned, 1)
                eng.wait_ge(ht_ready, k * (DC * H) + DC * H)
                def in_projection(z, m):
                    for s in range(H):
                        j = m * H + s
                        bank = j % (ZM * H) if z else j
                        if z and m < ZM:
                            eng.wait_ge(u_copied, k * (M * H) + j + 1)
                        elif z:
                            eng.wait_ge(v_ready, k * (M * H) + bank + 1)
                        for c in range(DC):
                            mm = eng.matmul(ps[:, bank, :], w_in[:, c, z * E + m * P:z * E + (m + 1) * P],
                                            hT[:, c, s * BANK:(s + 1) * BANK], start=c == 0, stop=c == DC - 1)
                        mm.then_inc(z_done if z else u_done, 1)

                for m in range(M):
                    in_projection(0, m)
                for m in range(ZM):
                    in_projection(1, m)
                eng.wait_ge(u_copied, k * (M * H) + M * H)
                for m in range(M):
                    eng.wait_ge(uc_ready, k * M + m + 1)
                    for s in range(H):
                        mm = eng.matmul(ps[0:R + 2 * NS, 6 + s, :], w_x[:, m, :], uc[:, m, s * BANK:(s + 1) * BANK],
                                        start=m == 0, stop=m == M - 1)
                        if m == M - 1:
                            mm.then_inc(xp_done, 1)
                eng.wait_ge(xp_copied, k * (2 * H + 6) + 2 * H)
                eng.wait_ge(z_gated, k * (M * H) + ZM * H)
                for m in range(M):
                    for s in range(H):
                        eng.matmul(ps[:, (m * H + s) % 8, :], w_dt[0:R, m * P:(m + 1) * P],
                                   dt_low[0:R, s * BANK:(s + 1) * BANK], start=True, stop=True).then_inc(dt_done, 1)
                for m in range(ZM, M):
                    in_projection(1, m)
                eng.wait_ge(z_gated, k * (M * H) + M * H)
                eng.wait_ge(v_ready, k * (M * H) + M * H)
                eng.wait_ge(xp_copied, k * (2 * H + 6) + 2 * H + 6)
                eng.wait_ge(diag_ready, k * M + M)

                def spread(kind, s, state, r):
                    bank = 4 + 2 * kind + r
                    eng.matmul(ps[:, bank, :], sel[0:96, kind * NS + state, :], parts[0:96, s * BANK:(s + 1) * BANK],
                               start=True, stop=True).then_inc(c_spread if kind else b_spread, 1)

                def add_state(n, r, last):
                    for m in range(M):
                        eng.wait_ge(weighted, n * M + m + 1)
                        mm = eng.matmul(ps[:, m, :], sh.ident, hc[:, r, m, :], start=False, stop=last)
                        if last:
                            mm.then_inc(summed, 1)

                for s in range(H):
                    base = (k * H + s) * NS
                    for r in range(2):
                        spread(0, s, r, r)
                        spread(1, s, r, r)
                    if s > 0:
                        eng.wait_ge(y_gated, (k * H + s) * M)
                    for m in range(M):
                        eng.matmul(ps[:, m, :], skip_diag[:, m, :], uc[:, m, s * BANK:(s + 1) * BANK],
                                   start=True, stop=False)
                    with eng.Fori(0, NS // 2 - 1) as pair:
                        for r in range(2):
                            n = base + pair * 2 + r
                            eng.wait_ge(b_copied, n + 1)
                            spread(0, s, pair * 2 + 2 + r, r)
                            add_state(n, r, False)
                            spread(1, s, pair * 2 + 2 + r, r)
                    for r in range(2):
                        add_state(base + NS - 2 + r, r, r == 1)
                for t in range(BT):
                    if t % (BT // H) == 0:
                        eng.wait_ge(y_gated, (k * H + t // (BT // H) + 1) * M)
                    for m in range(M):
                        mm = eng.matmul(ps[:, 4 + t // 2, (t % 2) * D:(t % 2 + 1) * D], sz[:, m, t * P:(t + 1) * P],
                                        w_out[:, m, :], start=m == 0, stop=m == M - 1)
                    if t % 2:
                        mm.then_inc(o_done, 1)

    sh.done = (x_done, NB * B * BT // 2)
    sh.top = mark
    return {"sync": sync, "pool": pool, "scalar": scalar, "vector": vector, "tensor": tensor}


def mamba_out(sh):
    ins, nm = sh.ins, sh.norm
    mark = sh.top
    x0 = sh.take("p (t d) -> p t d", NT * D, t=NT)
    fw, fb = sh.take(None, D), sh.take(None, D)
    loaded, added = sh.sem("fn_loaded"), sh.sem("fn_added")
    run1, run2 = nm.use(), nm.use()
    before = sh.done

    def sync(eng):
        eng.wait_ge(*before)
        eng.dma_start(x0, ins["x"].rearrange("b (t p) d -> p (b t) d", p=P)).then_inc(loaded, 16)
        eng.dma_start(fw, on_all_partitions(ins["L0_attn_fn_w"])).then_inc(loaded, 16)
        eng.dma_start(fb, on_all_partitions(ins["L0_attn_fn_b"])).then_inc(loaded, 16)

    def tile(t):
        return sh.x[:, t, :]

    def scalar(eng):
        nm.scalar(eng, run1)
        nm.scalar(eng, run2)

    def vector(eng):
        eng.wait_ge(*before)
        nm.vector(eng, tile, tile, run1)
        eng.wait_ge(loaded, 48)
        eng.wait_ge(nm.normed, run1 * NT + NT)
        wide = [P, NT, D]
        for n, (v, op) in enumerate(((fw.unsqueeze(1).to_broadcast(wide), ALU.mult),
                                     (fb.unsqueeze(1).to_broadcast(wide), ALU.add), (x0, ALU.add))):
            if n:
                eng.wait_ge(added, n)
            eng.tensor_tensor(sh.x, sh.x, v, op).then_inc(added, 1)
        eng.wait_ge(added, 3)
        nm.vector(eng, tile, tile, run2)

    sh.done = (nm.normed, run2 * NT + NT)
    sh.top = mark
    return {"sync": sync, "scalar": scalar, "vector": vector}


HEADS, DH = 16, 16
G = 4
NG = HEADS // G
GROUPS = B * NG
PARTS = 3
Q_PARTS = (0, 1, 2, 0, 1, 0)
K_PARTS = (0, 0, 0, 1, 1, 2)
STACK = DH * len(Q_PARTS)
UNITS = [(h, t, kc) for t in range(BT) for h in range(G) for kc in range(t // 4 + 1)]


class Masks:

    def __init__(self, sh):
        self.sh = sh
        self.mask_q = sh.take(None, P // 2).bitcast(BF16)
        self.mask_k = sh.take(None, P // 2).bitcast(BF16)
        self.made = sh.sem("masks_made")
        self.ready = (self.made, 4)

    def pool(self, eng):
        made = self.made
        eng.memset(self.mask_q, 0.0).then_inc(made, 1)
        eng.memset(self.mask_k, 0.0).then_inc(made, 1)
        eng.wait_ge(made, 2)
        eng.affine_select(out=self.mask_q, in_=self.mask_q, compare_op=ALU.is_ge, fill=-1e30,
                          base=0, pattern=[[-1, P]], channel_multiplier=1).then_inc(made, 1)
        eng.affine_select(out=self.mask_k, in_=self.mask_k, compare_op=ALU.is_ge, fill=-1e30,
                          base=0, pattern=[[1, P]], channel_multiplier=-1).then_inc(made, 1)


def causal_attention(sh, name, dv, scale, v_load, out_tok):
    ps, nc = sh.psum, sh.nc
    packed = dv == DH
    VW = 32 if packed else 80
    ONE = DH if packed else dv
    OUTW = P if packed else VW
    RE = 3
    qs = sh.take(None, 2 * G * S // 2).bitcast(BF16).rearrange("p (r h s) -> p r h s", r=2, h=G)
    ks = sh.take(None, 2 * G * S // 2).bitcast(BF16).rearrange("p (r h s) -> p r h s", r=2, h=G)
    v = sh.take("p (r t h n) -> p r t h n", 2 * BT * G * VW, r=2, t=BT, h=G)
    mx = sh.take("p (k t h) -> p k t h", 2 * BT * G, k=2, t=BT)
    mr = sh.take("p (k t h) -> p k t h", 2 * BT * G, k=2, t=BT)
    mp = sh.take(None, BT * G * PARTS // 2).bitcast(BF16).rearrange("p (t h j) -> p t h j", t=BT, j=PARTS)
    mt = sh.take(None, S // 2).bitcast(BF16)
    ex = sh.take("p (r h s) -> p r h s", RE * 2 * BANK, r=RE, h=2)
    oa = sh.take("p (r s) -> p r s", 2 * BANK, r=2)
    rc = sh.take("p (r t h) -> p r t h", 2 * 4 * G, r=2, t=4)
    s = {k: sh.sem(f"{name}_{k}") for k in (
        "init", "s_done", "max_taken", "max_done", "mt_done", "mt_taken", "rows_in",
        "st_done", "exped", "av_done", "acc_taken", "turned", "recip", "scaled")}
    stacked = [sh.sem(f"{name}_stacked{r}") for r in range(2)]
    v_in = [sh.sem(f"{name}_v_in{r}") for r in range(2)]
    U1 = len(UNITS)
    if packed:
        units2 = [(qc, [(2 * hp, kt), (2 * hp + 1, kt)], qc) for qc in range(2) for kt in range(4 * qc + 4)
                  for hp in range(2)]
    else:
        units2 = [(qc, [(h, kt), (h, kt + 1)], qc * G + h) for qc in range(2) for h in range(G)
                  for kt in range(0, 4 * qc + 4, 2)]
    U2 = len(units2)
    OUTS = units2[-1][2] + 1
    last_of = {o: max(u for u in range(U2) if units2[u][2] == o) for o in range(OUTS)}
    A0, B0, ACC = 0, 2, 6
    STACK_DMAS = 12
    EARLY = U2 * 6 // 8
    TURN = min(EARLY + 1, U2 - 2)
    assert last_of[OUTS - 1] + 4 >= EARLY
    MAXES = 5

    def span(qc, kt):
        first = max(kt * P - qc * BANK, 0)
        return first, BANK - first

    def sync(eng, scratch, first_wait):
        def load(i, r):
            for side, (dst, which) in enumerate(((qs, Q_PARTS), (ks, K_PARTS))):
                for blk, part in enumerate(which):
                    src = scratch[side, part, bass.ds(i, 1)].rearrange("o (h d) s -> d (o h) s", h=G)
                    eng.dma_start(dst[blk * DH:(blk + 1) * DH, r], src).then_inc(stacked[r], 16)
            v_load(eng, i, v[:, r], v_in[r])

        def rows(i, r):
            eng.wait_ge(s["mt_taken"], i * 2 + 2)
            for h in range(G):
                eng.dma_start(qs[STACK:STACK + PARTS, r, h, :], mt[PARTS * h:PARTS * (h + 1), :])\
                    .then_inc(s["rows_in"], 16)

        eng.wait_ge(s["init"], 4)
        first_wait(eng)
        load(0, 0)
        load(1, 1)
        rows(0, 0)

        def body(i, r, more):
            if more:
                rows(i + 1, 1 - r)
            if not isinstance(i, int):
                eng.wait_ge(s["av_done"], (i + 1) * U2)
                load(i + 2, r)

        loop(eng, body)

    def loop(eng, body):
        with eng.Fori(0, GROUPS // 2 - 1) as pair:
            for r in range(2):
                body(pair * 2 + r, r, True)
        body(GROUPS - 2, 0, True)
        body(GROUPS - 1, 1, False)

    def pool(eng, start):
        for wait in start:
            eng.wait_ge(*wait)
        eng.memset(ks[STACK:STACK + PARTS], -1.0).then_inc(s["init"], 1)
        eng.wait_ge(s["init"], 1)
        eng.memset(v, 0.0).then_inc(s["init"], 1)
        eng.wait_ge(s["init"], 2)
        eng.memset(mp, 0.0).then_inc(s["init"], 1)
        eng.wait_ge(s["init"], 3)
        eng.memset(v[:, :, :, :, ONE:ONE + 1], 1.0).then_inc(s["init"], 1)

    def take_rows(eng, i):
        eng.wait_ge(s["mt_done"], i + 1)
        if not isinstance(i, int) or i > 0:
            eng.wait_ge(s["rows_in"], i * (16 * G))
        for c in range(2):
            eng.activation(mt[0:12, c * BANK:(c + 1) * BANK], ps[0:12, A0 + c, :], ACT.Copy)\
                .then_inc(s["mt_taken"], 1)

    def scalar(eng):
        def exponentials(i, r, more):
            for u, (qc, blocks, o) in enumerate(units2):
                eng.wait_ge(s["st_done"], i * U2 + u + 1)
                if u >= RE:
                    eng.wait_ge(s["av_done"], i * U2 + u - RE + 1)
                bank = B0 + 2 * (u % 2)
                widths = [span(qc, kt)[1] for _, kt in blocks]
                if widths[0] == widths[1]:
                    eng.activation(ex[:, u % RE, :, 0:widths[0]], ps[:, bank:bank + 2, 0:widths[0]], ACT.Exp,
                                   scale=scale).then_inc(s["exped"], 2)
                else:
                    for k, w in enumerate(widths):
                        eng.activation(ex[:, u % RE, k, 0:w], ps[:, bank + k, 0:w], ACT.Exp,
                                       scale=scale).then_inc(s["exped"], 1)
                for done in [n for n in range(OUTS) if min(last_of[n] + 2, U2 - 1) == u]:
                    take_output(i, done)
                if more and u == TURN + 1:
                    take_rows(eng, i + 1)

        def take_output(i, o):
            eng.wait_ge(s["av_done"], i * U2 + last_of[o] + 1)
            eng.activation(oa[0:OUTW, o % 2, :], ps[0:OUTW, ACC + o % 2, :], ACT.Copy).then_inc(s["acc_taken"], 1)

        take_rows(eng, 0)
        loop(eng, exponentials)

    def vector(eng):
        def maxima(i, lo, hi):
            for u in range(lo, hi):
                h, t, kc = UNITS[u]
                w = min((t + 1) * P - kc * BANK, BANK)
                eng.wait_ge(s["s_done"], i * U1 + u + 1)
                eng.tensor_reduce(mx[:, kc, t, h:h + 1], ps[:, A0 + u % 2, 0:w], AX_X, ALU.max)\
                    .then_inc(s["max_taken"], 1)

        def max_parts(i):
            eng.wait_ge(s["max_taken"], (i + 1) * U1)
            eng.tensor_tensor(mx[:, 0, 4:8, :], mx[:, 0, 4:8, :], mx[:, 1, 4:8, :], ALU.max).then_inc(s["max_done"], 1)
            eng.wait_ge(s["max_done"], i * MAXES + 1)
            eng.tensor_copy(mp[:, :, :, 0], mx[:, 0]).then_inc(s["max_done"], 1)
            eng.wait_ge(s["max_done"], i * MAXES + 2)
            eng.tensor_tensor(mr[:, 0], mx[:, 0], mp[:, :, :, 0], ALU.subtract).then_inc(s["max_done"], 1)
            eng.wait_ge(s["max_done"], i * MAXES + 3)
            eng.tensor_copy(mp[:, :, :, 1], mr[:, 0]).then_inc(s["max_done"], 1)
            eng.wait_ge(s["max_done"], i * MAXES + 4)
            eng.tensor_tensor(mp[:, :, :, 2], mr[:, 0], mp[:, :, :, 1], ALU.subtract).then_inc(s["max_done"], 1)

        def output(i, o):
            n = i * OUTS + o
            eng.wait_ge(s["turned"], n + 1)
            heads = G if packed else 1
            src = ps[:, ACC + o % 2, 0:4 * OUTW].rearrange("p (t h n) -> p t h n", t=4, h=heads)
            eng.reciprocal(rc[:, o % 2, :, 0:heads], src[:, :, :, ONE]).then_inc(s["recip"], 1)
            eng.wait_ge(s["recip"], n + 1)
            qc, h = (o, 0) if packed else (o // G, o % G)
            dst = out_tok(i, qc, h, heads)
            for t in range(4):
                eng.tensor_tensor(dst(t), src[:, t, :, 0:dv], rc[:, o % 2, t, 0:heads].unsqueeze(2)
                                  .to_broadcast([P, heads, dv]), ALU.mult).then_inc(s["scaled"], 1)

        eng.wait_ge(s["init"], 4)
        eng.memset(rc, 0.0).then_inc(s["scaled"], 4)
        maxima(0, 0, U1)
        max_parts(0)

        def body(i, r, more):
            lo = 0
            for o in range(OUTS):
                if more:
                    hi = min((last_of[o] + 4) * U1 // EARLY, U1)
                    maxima(i + 1, lo, hi)
                    if lo < U1 and hi == U1:
                        max_parts(i + 1)
                    lo = hi
                output(i, o)

        loop(eng, body)

    def tensor(eng):
        def score(i, r, u):
            h, t, kc = UNITS[u]
            w = min((t + 1) * P - kc * BANK, BANK)
            diagonal = kc == t // 4
            bank = A0 + u % 2
            if u == 0:
                eng.wait_ge(stacked[r], (i - r) * (8 * STACK_DMAS) + 16 * STACK_DMAS)
                if not isinstance(i, int) or i > 0:
                    eng.wait_ge(s["mt_taken"], i * 2)
            if u >= 2:
                eng.wait_ge(s["max_taken"], i * U1 + u - 1)
            mm = eng.matmul(ps[:, bank, 0:w], qs[0:STACK, r, h, t * P:(t + 1) * P],
                            ks[0:STACK, r, h, kc * BANK:kc * BANK + w], start=True, stop=not diagonal)
            if diagonal:
                mm = eng.matmul(ps[:, bank, w - P:w], sh.ident_bf, sh.masks.mask_q, start=False, stop=True)
            mm.then_inc(s["s_done"], 1)

        def turn_max(i):
            eng.wait_ge(s["max_done"], i * MAXES + 5)
            for c in range(2):
                for t in range(4):
                    mm = eng.matmul(ps[0:12, A0 + c, t * P:(t + 1) * P], mp[:, 4 * c + t].rearrange("p h j -> p (h j)"), sh.ident_bf,
                                    start=True, stop=True)
            mm.then_inc(s["mt_done"], 1)

        def products(i, r, u, between):
            qc, blocks, o = units2[u]
            eng.wait_ge(s["exped"], i * (2 * U2) + 2 * u + 2)
            if u == 0 or units2[u - 1][2] != o:
                eng.wait_ge(s["scaled"], 4 + i * (4 * OUTS) + 4 * max(o - 1, 0))
            for k, (h, kt) in enumerate(blocks):
                first, w = span(qc, kt)
                rows = slice(32 * h, 32 * h + 32) if packed else slice(0, VW)
                mm = eng.matmul(ps[rows, ACC + o % 2, first:BANK], v[:, r, kt, h, :], ex[:, u % RE, k, 0:w],
                                start=kt == 0, stop=kt == 4 * qc + 3)
                if k == 0 and between:
                    between(2)
            mm.then_inc(s["av_done"], 1)

        def turn_output(i, o):
            eng.wait_ge(s["acc_taken"], i * OUTS + o + 1)
            for t in range(4):
                mm = eng.transpose(ps[:, ACC + o % 2, t * OUTW:(t + 1) * OUTW], oa[0:OUTW, o % 2, t * P:(t + 1) * P],
                                   sh.ident[0:OUTW, 0:OUTW])
            mm.then_inc(s["turned"], 1)

        for u in range(U1):
            score(0, 0, u)
        turn_max(0)

        def body(i, r, more):
            lo = 0
            eng.wait_ge(s["rows_in"], (i + 1) * (16 * G))
            eng.wait_ge(v_in[r], (i - r) * (v_load.count // 2) + v_load.count)
            for u, (qc, blocks, o) in enumerate(units2):
                bank = B0 + 2 * (u % 2)
                if u >= 2:
                    eng.wait_ge(s["exped"], i * (2 * U2) + 2 * u - 2)
                hi = min((u + 1) * U1 // EARLY, U1) if more else 0
                cuts = [lo + (hi - lo) * q // 4 for q in range(5)] if more else [0] * 5

                def between(q):
                    for n in range(cuts[q], cuts[q + 1]):
                        score(i + 1, 1 - r, n)

                for k, (h, kt) in enumerate(blocks):
                    first, w = span(qc, kt)
                    diagonal = kt >= 4 * qc
                    mm = eng.matmul(ps[:, bank + k, 0:w], ks[0:STACK + PARTS, r, h, kt * P:(kt + 1) * P],
                                    qs[0:STACK + PARTS, r, h, qc * BANK + first:(qc + 1) * BANK],
                                    start=True, stop=not diagonal)
                    if diagonal:
                        mm = eng.matmul(ps[:, bank + k, 0:P], sh.ident_bf, sh.masks.mask_k, start=False, stop=True)
                    if k == 0:
                        between(0)
                mm.then_inc(s["st_done"], 1)
                between(1)
                if u >= 1:
                    products(i, r, u - 1, between)
                else:
                    between(2)
                between(3)
                lo = hi
                if more and u == TURN:
                    turn_max(i + 1)
                for n in range(OUTS):
                    if last_of[n] + 3 == u:
                        turn_output(i, n)
            products(i, r, U2 - 1, None)
            for n in range(OUTS):
                if last_of[n] + 3 > U2 - 1:
                    turn_output(i, n)

        loop(eng, body)

    ns = {"sync": sync, "pool": pool, "scalar": scalar, "vector": vector, "tensor": tensor}
    return s, OUTS, ns


def write_parts(sh, name, tasks, scratch, weights, hT, start):
    ps = sh.psum
    st = sh.take("p (r s) -> p r s", 2 * S, r=2)
    rest = sh.take("p (r s) -> p r s", 2 * S, r=2)
    part = [sh.take(None, S).bitcast(BF16).rearrange("p (r s) -> p r s", r=2) for _ in range(PARTS)]
    s = {k: sh.sem(f"{name}_{k}") for k in ("projected", "taken", "part0", "rest", "part1", "part2")}
    sent = [sh.sem(f"{name}_sent{r}") for r in range(2)]
    N = len(tasks)

    def tensor(eng):
        for n, (side, m, b, w, bias) in enumerate(t for t in tasks if t[3] is not None):
            if n >= 4:
                eng.wait_ge(s["taken"], n - 3 + (N - n_proj))
            for c in range(2):
                for k in range(DC):
                    mm = eng.matmul(ps[:, 2 * (n % 4) + c, :], w[:, k, m * P:(m + 1) * P],
                                    hT[:, k, b * S + c * BANK:b * S + (c + 1) * BANK], start=k == 0, stop=k == DC - 1)
            mm.then_inc(s["projected"], 1)

    def scalar(eng):
        proj = 0
        for n, (side, m, b, w, bias) in enumerate(tasks):
            if n >= 2:
                eng.wait_ge(s["rest"], n - 1)
                eng.wait_ge(sent[n % 2], (n // 2) * 48)
            if w is not None:
                proj += 1
                eng.wait_ge(s["projected"], proj)
                src = ps[:, 2 * ((proj - 1) % 4):2 * ((proj - 1) % 4) + 2, :].rearrange("p c s -> p (c s)")
            else:
                src = hT[:, m, b * S:(b + 1) * S]
            if bias is None:
                eng.activation(st[:, n % 2, :], src, ACT.Copy).then_inc(s["taken"], 1)
            else:
                eng.activation(st[:, n % 2, :], src, ACT.Identity, bias=bias[:, m:m + 1]).then_inc(s["taken"], 1)
            eng.wait_ge(s["taken"], n + 1)
            eng.activation(part[0][:, n % 2, :], st[:, n % 2, :], ACT.Copy).then_inc(s["part0"], 1)

    def vector(eng):
        for n in range(N):
            eng.wait_ge(s["part0"], n + 1)
            if n >= 2:
                eng.wait_ge(s["part2"], n - 1)
                eng.wait_ge(sent[n % 2], (n // 2) * 48)
            eng.tensor_tensor(rest[:, n % 2, :], st[:, n % 2, :], part[0][:, n % 2, :], ALU.subtract)\
                .then_inc(s["rest"], 1)
            eng.wait_ge(s["rest"], n + 1)
            eng.tensor_copy(part[1][:, n % 2, :], rest[:, n % 2, :]).then_inc(s["part1"], 1)

    def pool(eng):
        for n in range(N):
            eng.wait_ge(s["part1"], n + 1)
            if n >= 2:
                eng.wait_ge(sent[n % 2], (n // 2) * 48)
            eng.tensor_tensor(part[2][:, n % 2, :], rest[:, n % 2, :], part[1][:, n % 2, :], ALU.subtract)\
                .then_inc(s["part2"], 1)

    def sync(eng):
        for n, (side, m, b, w, bias) in enumerate(tasks):
            eng.wait_ge(s["part2"], n + 1)
            for j in range(PARTS):
                dst = scratch[side, j, b * NG + 2 * m:b * NG + 2 * m + 2].rearrange("g r s -> (g r) s")
                eng.dma_start(dst, part[j][:, n % 2, :]).then_inc(sent[n % 2], 16)

    n_proj = sum(t[3] is not None for t in tasks)
    return [(sem, 24 * N) for sem in sent], {"taken": s["taken"], "sync": sync, "scalar": scalar, "vector": vector, "pool": pool, "tensor": tensor}


def self_attention(sh):
    ins, nm, tn, ps = sh.ins, sh.norm, sh.turn, sh.psum
    before = sh.done
    acc = sh.acc
    mark = sh.top
    hT = sh.take("p (c s) -> p c s", DC * TOK, c=DC)
    v_all = sh.take("p (i t n) -> p i t n", NT * D, i=GROUPS, t=BT)
    o_tok = sh.take("p (t i n) -> p t i n", NT * D, i=GROUPS, t=BT)
    xn = o_tok.rearrange("p t i n -> p (t i n)").rearrange("p (t d) -> p t d", t=NT)
    w_all = sh.take("p (k c n) -> p k c n", 4 * DC * D, k=4, c=DC)
    bo = sh.take(None, 2 * D)
    ls, lb = sh.take(None, DC), sh.take(None, DC)
    scratch = sh.nc.dram_tensor("f0_parts", [2, PARTS, GROUPS, G * DH, S], BF16, kind="Internal").ap()
    loaded, kept = sh.sem("f0_loaded"), sh.sem("f0_kept")
    v_done, v_kept = sh.sem("f0_v_done"), sh.sem("f0_v_kept")
    o_done, x_done = sh.sem("f0_o_done"), sh.sem("f0_x_done")
    run, trun, trun2 = nm.use(), tn.use(), tn.use()
    tasks = [(side, m, b, w_all[:, side], None) for b in range(B) for m in range(2) for side in range(2)]
    inner = sh.top
    sent, wp = write_parts(sh, "f0p", tasks, scratch, w_all, hT, before)
    sh.top = inner

    def v_load(eng, i, dst, sem):
        for h in range(G):
            eng.dma_start(dst[:, :, h, 0:DH], v_all[:, bass.ds(i, 1), :, h * DH:(h + 1) * DH]
                          .rearrange("p o t n -> p (o t) n")).then_inc(sem, 16)
    v_load.count = 16 * G

    def out_tok(i, qc, h, heads):
        return lambda t: o_tok[:, qc * 4 + t, bass.ds(i, 1), :].rearrange("p o (h n) -> p (o h) n", h=heads)

    s, OUTS, att = causal_attention(sh, "f0", DH, DH ** -0.5, v_load, out_tok)

    def sync(eng):
        eng.wait_ge(*before)
        for k, w in enumerate(("wq", "wk", "wv", "wo")):
            eng.dma_start(w_all[:, k], ins["L0_ffn_" + w].rearrange("(c p) n -> p c n", p=P)).then_inc(loaded, 16)
        for k in range(2):
            eng.dma_start(bo[0:1, k * D:(k + 1) * D], ins["L0_ffn_bo"].rearrange("(o d) -> o d", o=1)).then_inc(loaded, 16)
        eng.dma_start(ls, feature_columns(ins["L0_ffn_ln1_scale"]), allow_slow_non_contiguous=True).then_inc(loaded, 16)
        eng.dma_start(lb, feature_columns(ins["L0_ffn_ln1_shift"]), allow_slow_non_contiguous=True).then_inc(loaded, 16)
        wp["sync"](eng)

        def first_wait(eng):
            for both in sent:
                eng.wait_ge(*both)
            eng.wait_ge(v_kept, 8)
        att["sync"](eng, scratch, first_wait)

    def pool(eng):
        wp["pool"](eng)
        att["pool"](eng, sent)

    def scalar(eng):
        nm.scalar(eng, run)
        eng.wait_ge(loaded, 16 * 8)
        tn.scalar(eng, hT, trun, scale=ls, bias=lb)
        wp["scalar"](eng)
        att["scalar"](eng)
        tn.scalar(eng, hT, trun2)

    def vector(eng):
        eng.wait_ge(*before)
        nm.vector(eng, lambda t: sh.x[:, t, :], lambda t: xn[:, t, :], run)
        eng.tensor_copy(acc, sh.x).then_inc(kept, 1)
        wp["vector"](eng)
        for j in range(8):
            eng.wait_ge(v_done, j + 1)
            dst = v_all[:, (j // 4) * NG:(j // 4 + 1) * NG, 2 * (j % 4):2 * (j % 4) + 2, :].rearrange("p g t n -> p t g n")
            src = ps[:, j, :].rearrange("p (t g n) -> p t g n", t=2, g=NG)
            for t in range(2):
                ins_ = eng.tensor_copy(dst[:, t], src[:, t])
            ins_.then_inc(v_kept, 1)
        att["vector"](eng)
        for j in range(NT // 2):
            eng.wait_ge(o_done, j + 1)
            tiles = sh.x[:, 2 * j:2 * j + 2, :]
            eng.tensor_tensor(tiles, tiles, ps[:, j, :].rearrange("p (t d) -> p t d", t=2), ALU.add)\
                .then_inc(x_done, 1)

    def tensor(eng):
        eng.wait_ge(*before)
        tn.tensor(eng, lambda t, c: xn[:, t, c * P:(c + 1) * P], trun, lambda e, t: e.wait_ge(nm.normed, run * NT + t + 1))
        eng.wait_ge(loaded, 16 * 8)
        eng.wait_ge(tn.taken, 8 * trun + 8)
        wp["tensor"](eng)
        eng.wait_ge(wp_taken, len(tasks))
        for t in range(NT):
            for k in range(DC):
                mm = eng.matmul(ps[:, t // 2, (t % 2) * D:(t % 2 + 1) * D], hT[:, k, t * P:(t + 1) * P], w_all[:, 2, k, :],
                                start=k == 0, stop=k == DC - 1)
            if t % 2:
                mm.then_inc(v_done, 1)
        eng.wait_ge(v_kept, 8)
        eng.wait_ge(*sh.masks.ready)
        att["tensor"](eng)
        eng.wait_ge(s["scaled"], 4 + 4 * OUTS * GROUPS)
        tn.tensor(eng, lambda t, c: o_tok[:, t % BT, (t // BT) * NG + 2 * c:(t // BT) * NG + 2 * c + 2, :]
                  .rearrange("p i n -> p (i n)"), trun2,
                  lambda e, t: None)
        eng.wait_ge(tn.taken, 8 * trun2 + 8)
        for t in range(NT):
            dst = ps[:, t // 2, (t % 2) * D:(t % 2 + 1) * D]
            for k in range(DC):
                eng.matmul(dst, hT[:, k, t * P:(t + 1) * P], w_all[:, 3, k, :], start=k == 0, stop=False)
            mm = eng.matmul(dst, sh.ones_row[0:1, :], bo[0:1, 0:D], start=False, stop=True)
            if t % 2:
                mm.then_inc(o_done, 1)

    wp_taken = wp["taken"]
    sh.done = (x_done, NT // 2)
    sh.top = mark
    return {"sync": sync, "pool": pool, "scalar": scalar, "vector": vector, "tensor": tensor}


def kept(sh):
    sh.acc = sh.take("p (t d) -> p t d", NT * D, t=NT)
    return {}


EXPERTS, HID = 8, 512
HC = HID // P
CH = TOK // BANK


class TopTwo:

    def __init__(self, sh, name, n):
        self.n = n
        self.order = sh.take(None, n)
        self.a = sh.take("p (t e) -> p t e", NT * n, t=NT)
        self.low = sh.take(None, NT)
        self.step = sh.sem(name + "_step")
        self.steps = 0

    def did(self, ins):
        self.steps += 1
        ins.then_inc(self.step, 1)

    def wait(self, eng):
        eng.wait_ge(self.step, self.steps)

    def start(self, eng):
        for e in range(self.n):
            self.did(eng.memset(self.order[:, e:e + 1], float(self.n - e)))
        self.wait(eng)

    def pick(self, eng, values, best, one):
        wide = [P, NT, self.n]
        self.did(eng.tensor_reduce(best, values, AX_X, ALU.max))
        self.wait(eng)
        self.did(eng.tensor_tensor(self.a, values, best.unsqueeze(2).to_broadcast(wide), ALU.is_equal))
        self.wait(eng)
        self.did(eng.tensor_tensor(self.a, self.a, self.order.unsqueeze(1).to_broadcast(wide), ALU.mult))
        self.wait(eng)
        self.did(eng.tensor_reduce(self.low, self.a, AX_X, ALU.max))
        self.wait(eng)
        self.did(eng.tensor_tensor(one, self.a, self.low.unsqueeze(2).to_broadcast(wide), ALU.is_equal))
        self.wait(eng)


def experts(sh):
    ins, nm, tn, ps = sh.ins, sh.norm, sh.turn, sh.psum
    before, acc = sh.done, sh.acc
    mark = sh.top
    E2 = EXPERTS // 2
    hT = sh.take("p (c s) -> p c s", DC * TOK, c=DC)
    xn = sh.take("p (t d) -> p t d", NT * D, t=NT)
    w12 = sh.take("p (r w c n) -> p r w c n", 2 * 2 * DC * HID, r=2, w=2, c=DC)
    w3 = sh.take("p (r c n) -> p r c n", 2 * HC * D, r=2, c=HC)
    silu = sh.take("p (r s) -> p r s", 2 * BANK, r=2)
    hid = sh.take("p (r m s) -> p r m s", 2 * HC * BANK, r=2, m=HC)
    gw = sh.take("p (c e) -> p c e", DC * EXPERTS, c=DC)
    ls, lb = sh.take(None, DC), sh.take(None, DC)
    gate = sh.take("p (t e) -> p t e", NT * EXPERTS, t=NT)
    one1 = sh.take("p (t e) -> p t e", NT * EXPERTS, t=NT)
    one2 = sh.take("p (t e) -> p t e", NT * EXPERTS, t=NT)
    wt = sh.take("p (t e) -> p t e", NT * EXPERTS, t=NT)
    best, prob = sh.take("p (k t) -> p k t", 2 * NT, k=2), sh.take("p (k t) -> p k t", 2 * NT, k=2)
    top = TopTwo(sh, "moe", EXPERTS)
    s = {k: sh.sem("moe_" + k) for k in ("loaded", "gated", "ratio", "ab_done", "silued", "hid_made", "o_done", "added")}
    w_in = [sh.sem(f"moe_w_in{r}") for r in range(2)]
    run, run2, trun = nm.use(), nm.use(), tn.use()
    UNITS_E = CH * HC
    ratio_at = EXPERTS + 1 + 5 + 1 + 5 + 1
    wide = [P, NT, EXPERTS]

    def loop(eng, body):
        with eng.Fori(0, E2 - 1) as pair:
            for r in range(2):
                body(pair * 2 + r, r, True)
        body(EXPERTS - 2, 0, True)
        body(EXPERTS - 1, 1, False)

    def sync(eng):
        eng.wait_ge(*before)
        eng.dma_start(gw, ins["L0_ffn_gate_w"].rearrange("(c p) e -> p c e", p=P)).then_inc(s["loaded"], 16)
        eng.dma_start(ls, feature_columns(ins["L0_ffn_ln2_scale"]), allow_slow_non_contiguous=True).then_inc(s["loaded"], 16)
        eng.dma_start(lb, feature_columns(ins["L0_ffn_ln2_shift"]), allow_slow_non_contiguous=True).then_inc(s["loaded"], 16)

        def load(e, r):
            for k in range(2):
                eng.dma_start(w12[:, r, k], ins[("L0_ffn_w1", "L0_ffn_w2")[k]][bass.ds(e, 1)]
                              .rearrange("o (c p) n -> p (o c) n", p=P)).then_inc(w_in[r], 16)
            eng.dma_start(w3[:, r], ins["L0_ffn_w3"][bass.ds(e, 1)].rearrange("o (c p) n -> p (o c) n", p=P))\
                .then_inc(w_in[r], 16)

        load(0, 0)
        load(1, 1)

        def body(e, r, more):
            if not isinstance(e, int):
                eng.wait_ge(s["o_done"], (e + 1) * CH)
                load(e + 2, r)
        loop(eng, body)

    def scalar(eng):
        nm.scalar(eng, run)
        eng.wait_ge(s["loaded"], 48)
        tn.scalar(eng, hT, trun, scale=ls, bias=lb)
        eng.wait_ge(top.step, ratio_at)
        eng.activation(prob[:, 1], prob[:, 1], ACT.Exp).then_inc(s["ratio"], 1)
        with eng.Fori(0, EXPERTS) as e:
            for u in range(UNITS_E):
                sh.wait_apart(eng, s["ab_done"], e * UNITS_E + u + 1)
                eng.wait_ge(s["hid_made"], e * UNITS_E + u + 1)
                eng.activation(silu[:, u % 2], ps[:, 2 * (u % 2), :], ACT.Silu).then_inc(s["silued"], 1)
        nm.scalar(eng, run2)

    def vector(eng):
        eng.wait_ge(*before)
        nm.vector(eng, lambda t: sh.x[:, t, :], lambda t: xn[:, t, :], run)
        top.start(eng)
        eng.wait_ge(s["gated"], 1)
        top.did(eng.tensor_copy(gate, ps[:, 0, 0:NT * EXPERTS].rearrange("p (t e) -> p t e", t=NT)))
        top.wait(eng)
        top.pick(eng, gate, best[:, 0], one1)
        top.did(eng.scalar_tensor_tensor(gate, one1, -1e30, gate, ALU.mult, ALU.add))
        top.wait(eng)
        top.pick(eng, gate, best[:, 1], one2)
        top.did(eng.tensor_tensor(prob[:, 1], best[:, 1], best[:, 0], ALU.subtract))
        assert top.steps == ratio_at, top.steps
        for t in range(NT):
            eng.tensor_tensor(acc[:, t, :], acc[:, t, :], sh.x[:, t, :], ALU.add).then_inc(s["added"], 1)
        eng.wait_ge(s["ratio"], 1)
        top.did(eng.tensor_scalar(prob[:, 0], prob[:, 1], 1.0, None, ALU.add))
        top.wait(eng)
        top.did(eng.reciprocal(prob[:, 0], prob[:, 0]))
        top.wait(eng)
        top.did(eng.tensor_tensor(prob[:, 1], prob[:, 1], prob[:, 0], ALU.mult))
        top.wait(eng)
        top.did(eng.tensor_tensor(one1, one1, prob[:, 0].unsqueeze(2).to_broadcast(wide), ALU.mult))
        top.did(eng.tensor_tensor(one2, one2, prob[:, 1].unsqueeze(2).to_broadcast(wide), ALU.mult))
        top.wait(eng)
        top.did(eng.tensor_tensor(wt, one1, one2, ALU.add))
        top.wait(eng)
        eng.memset(hid[:, 0, 0, 0:1], 0.0).then_inc(s["hid_made"], 2)
        eng.wait_ge(s["hid_made"], 2)

        def product(e, c, m):
            u = c * HC + m
            sh.wait_apart(eng, s["silued"], e * UNITS_E + u + 1)
            eng.tensor_tensor(hid[:, c % 2, m, :], silu[:, u % 2], ps[:, 2 * (u % 2) + 1, :], ALU.mult)\
                .then_inc(s["hid_made"], 1)

        for m in range(2):
            product(0, 0, m)

        def body(e, r, more):
            for c in range(CH):
                product(e, c, 2)
                product(e, c, 3)
                if c + 1 < CH or more:
                    for m in range(2):
                        product(e + (c + 1) // CH, (c + 1) % CH, m)
                sh.wait_apart(eng, s["o_done"], e * CH + c + 1)
                eng.wait_ge(s["added"], e * NT + 4 * c + 4)
                for t in range(4):
                    n = 4 * c + t
                    eng.scalar_tensor_tensor(acc[:, n, :], ps[:, 4 + 2 * (c % 2) + t // 2, (t % 2) * D:(t % 2 + 1) * D],
                                             wt[:, n, bass.ds(e, 1)], acc[:, n, :], ALU.mult, ALU.add)\
                        .then_inc(s["added"], 1)
        loop(eng, body)
        eng.wait_ge(s["added"], (EXPERTS + 1) * NT)
        nm.vector(eng, lambda t: acc[:, t, :], lambda t: sh.x[:, t, :], run2)

    def tensor(eng):
        eng.wait_ge(*before)
        tn.tensor(eng, lambda t, c: xn[:, t, c * P:(c + 1) * P], trun, lambda e, t: e.wait_ge(nm.normed, run * NT + t + 1))
        eng.wait_ge(s["loaded"], 48)
        eng.wait_ge(tn.taken, 8 * trun + 8)
        for t in range(NT):
            for k in range(DC):
                mm = eng.matmul(ps[:, 0, t * EXPERTS:(t + 1) * EXPERTS], hT[:, k, t * P:(t + 1) * P], gw[:, k, :],
                                start=k == 0, stop=k == DC - 1)
        mm.then_inc(s["gated"], 1)
        eng.wait_ge(s["hid_made"], 2)

        def ab(e, r, c, m):
            u = c * HC + m
            if u == 0:
                eng.wait_ge(w_in[r], (e - r) * 24 + 48)
            eng.wait_ge(s["hid_made"], e * UNITS_E + u + 1)
            for w in range(2):
                for k in range(DC):
                    mm = eng.matmul(ps[:, 2 * (u % 2) + w, :], w12[:, r, w, k, m * P:(m + 1) * P],
                                    hT[:, k, c * BANK:(c + 1) * BANK], start=k == 0, stop=k == DC - 1)
            mm.then_inc(s["ab_done"], 1)

        for m in range(2):
            ab(0, 0, 0, m)

        def body(e, r, more):
            for c in range(CH):
                ab(e, r, c, 2)
                ab(e, r, c, 3)
                if c + 1 < CH:
                    ab(e, r, c + 1, 0)
                    ab(e, r, c + 1, 1)
                elif more:
                    ab(e + 1, 1 - r, 0, 0)
                    ab(e + 1, 1 - r, 0, 1)
                eng.wait_ge(s["hid_made"], e * UNITS_E + 4 * c + 4 + 2)
                if c >= 2 or not isinstance(e, int) or e > 0:
                    eng.wait_ge(s["added"], e * NT + 4 * c - 4 + NT)
                for t in range(4):
                    for m in range(HC):
                        mm = eng.matmul(ps[:, 4 + 2 * (c % 2) + t // 2, (t % 2) * D:(t % 2 + 1) * D],
                                        hid[:, c % 2, m, t * P:(t + 1) * P], w3[:, r, m, :],
                                        start=m == 0, stop=m == HC - 1)
                mm.then_inc(s["o_done"], 1)
        loop(eng, body)

    sh.done = (nm.normed, run2 * NT + NT)
    sh.top = mark
    return {"sync": sync, "scalar": scalar, "vector": vector, "tensor": tensor}




CK = 77


class Context:

    HC8 = P // DH

    def __init__(self, sh):
        self.sh = sh
        self.raw = sh.take("p (b d) -> p b d", B * D, b=B)
        self.rows = sh.take("p (c s) -> p c s", DC * B * CK, c=DC)
        self.of_head = sh.take(None, self.HC8)
        self.s = {k: sh.sem("ctx_" + k) for k in ("loaded", "turned", "ready", "heads")}
        self.ready = (self.s["ready"], 1)

    def stage(self):
        s, sh = self.s, self.sh

        def sync(eng):
            eng.wait_ge(*self.before)
            eng.dma_start(self.raw[0:CK], sh.ins["ctx_1024"].rearrange("b k d -> k b d")).then_inc(s["loaded"], 16)

        def pool(eng):
            eng.wait_ge(*self.before)
            eng.memset(self.of_head, 1.0).then_inc(s["heads"], 1)
            eng.wait_ge(s["heads"], 1)
            eng.affine_select(out=self.of_head, in_=self.of_head, compare_op=ALU.is_ge, fill=0.0, base=0,
                              pattern=[[-DH, self.HC8]], channel_multiplier=1).then_inc(s["heads"], 1)
            eng.wait_ge(s["heads"], 2)
            eng.affine_select(out=self.of_head, in_=self.of_head, compare_op=ALU.is_ge, fill=0.0, base=DH - 1,
                              pattern=[[DH, self.HC8]], channel_multiplier=-1).then_inc(s["heads"], 1)

        def tensor(eng):
            eng.wait_ge(*self.before)
            eng.wait_ge(*sh.constants)
            eng.wait_ge(s["loaded"], 16)
            for c in range(DC):
                for b in range(B):
                    at = (c * B + b) * CK
                    mm = eng.transpose(sh.psum[:, 0, at:at + CK], self.raw[0:CK, b, c * P:(c + 1) * P], sh.ident[0:CK, 0:CK])
            mm.then_inc(s["turned"], 1)

        def scalar(eng):
            eng.wait_ge(s["turned"], 1)
            eng.activation(self.rows.rearrange("p c s -> p (c s)"), sh.psum[:, 0, 0:DC * B * CK], ACT.Copy).then_inc(s["ready"], 1)

        self.before = sh.done
        sh.done = self.ready
        return {"sync": sync, "pool": pool, "tensor": tensor, "scalar": scalar}


def query_softmax_attention(sh):
    ins, nm, tn, ps, cx = sh.ins, sh.norm, sh.turn, sh.psum, sh.context
    before = sh.done
    mark = sh.top
    hT = sh.take("p (c s) -> p c s", DC * TOK, c=DC)
    qT = sh.take("p (c s) -> p c s", DC * TOK, c=DC)
    o = sh.take("p (t d) -> p t d", NT * D, t=NT)
    names = ("Wq", "Wk1", "Wk2", "Wv1", "Wv2", "Wo")
    w = {n: sh.take("p (c n) -> p c n", DC * D, c=DC) for n in names}
    rows = {n: sh.take(None, D) for n in ("bq", "bv1", "bv2", "bo")}
    cols = {n: sh.take(None, DC) for n in ("bq", "bk1", "bk2")}
    affine = {n: sh.take(None, D) for n in ("g0", "beta0", "g1", "beta1")}
    kT = sh.take("p (j c s) -> p j c s", 2 * DC * B * CK, j=2, c=DC)
    kh = sh.take("p (j c b h k) -> p j c b h k", 2 * DC * B * 8 * CK, j=2, c=DC, b=B, h=8)
    v = sh.take("p (j b h n) -> p j b h n", 2 * B * D, j=2, b=B, h=HEADS)
    vs = sh.take("p (r n) -> p r n", 3 * DH, r=3)
    ex = sh.take("p (r s) -> p r s", 3 * S, r=3)
    mx = sh.take("p (r k) -> p r k", 3 * 4, r=3)
    relu = sh.take("p (t d) -> p t d", NT * D, t=NT)
    s = {k: sh.sem("qx_" + k) for k in (
        "loaded", "proj", "moved", "k_ready", "v_proj", "v_ready", "s_done", "max", "exped", "v_scaled",
        "q_done", "av_done", "o_taken", "f_done", "relued", "step")}
    runs, t1, t2 = [nm.use() for _ in range(3)], tn.use(), tn.use()
    NLOAD = len(names) + len(rows) + len(cols) + len(affine)
    UNITS_X = [(b, h, j) for b in range(B) for h in range(HEADS) for j in range(2)]
    PER_B = 2 * HEADS

    def sync(eng):
        eng.wait_ge(*before)
        for n in names:
            eng.dma_start(w[n], ins["L0_xattn_" + n].rearrange("(c p) n -> p c n", p=P)).then_inc(s["loaded"], 16)
        for n, dst in rows.items():
            eng.dma_start(dst[0:1, :], ins["L0_xattn_" + n].rearrange("(o d) -> o d", o=1)).then_inc(s["loaded"], 16)
        for n, dst in cols.items():
            eng.dma_start(dst, feature_columns(ins["L0_xattn_" + n]), allow_slow_non_contiguous=True).then_inc(s["loaded"], 16)
        for n, dst in affine.items():
            eng.dma_start(dst, on_all_partitions(ins["L0_xattn_" + n])).then_inc(s["loaded"], 16)

    def scalar(eng):
        tn.scalar(eng, hT, t1)
        eng.wait_ge(s["loaded"], 16 * NLOAD)
        for n in range(8):
            m, c = n // 4, n % 4
            eng.wait_ge(s["proj"], n + 1)
            eng.activation(qT[:, m, c * BANK:(c + 1) * BANK], ps[:, n, :], ACT.Identity, bias=cols["bq"][:, m:m + 1])\
                .then_inc(s["moved"], 1)
        for n in range(4):
            j, m = n // 2, n % 2
            eng.wait_ge(s["proj"], 8 + n + 1)
            eng.activation(kT[:, j, m, :], ps[:, n, 0:B * CK], ACT.Identity, bias=cols[("bk1", "bk2")[j]][:, m:m + 1])\
                .then_inc(s["moved"], 1)
        for u, (b, h, j) in enumerate(UNITS_X):
            eng.wait_ge(s["max"], u + 1)
            if u >= 3:
                eng.wait_ge(s["av_done"], u - 2)
            eng.activation(ex[0:CK, u % 3, :], ps[0:CK, 2 * (u % 2):2 * (u % 2) + 2, :].rearrange("p b s -> p (b s)"),
                           ACT.Exp, bias=mx[0:CK, u % 3, 0:1], scale=1 / 16,
                           accum_out=mx[0:CK, u % 3, 1:2]).then_inc(s["exped"], 1)
            if u % PER_B == PER_B - 1:
                eng.wait_ge(s["av_done"], u + 1)
                for n in range(4):
                    eng.activation(o[:, b * BT + 2 * n:b * BT + 2 * n + 2, :].rearrange("p t d -> p (t d)"), ps[:, 4 + n, :],
                                   ACT.Copy).then_inc(s["o_taken"], 1)
        nm.scalar(eng, runs[0])
        tn.scalar(eng, hT, t2)
        for j in range(NT // 2):
            eng.wait_ge(s["f_done"], j + 1)
            eng.activation(relu[:, 2 * j:2 * j + 2, :].rearrange("p t d -> p (t d)"), ps[:, j, :], ACT.Relu).then_inc(s["relued"], 1)
        nm.scalar(eng, runs[1])
        nm.scalar(eng, runs[2])

    def vector(eng):
        steps = [0]

        def did(ins_):
            steps[0] += 1
            ins_.then_inc(s["step"], 1)
            eng.wait_ge(s["step"], steps[0])

        eng.wait_ge(cx.s["heads"], 3)
        for n in range(4):
            j, m = n // 2, n % 2
            eng.wait_ge(s["moved"], 8 + n + 1)
            for b in range(B):
                shape = [P, 8, CK]
                eng.tensor_tensor(kh[:, j, m, b], kT[:, j, m, b * CK:(b + 1) * CK].unsqueeze(1).to_broadcast(shape),
                                  cx.of_head.unsqueeze(2).to_broadcast(shape), ALU.mult).then_inc(s["k_ready"], 1)
        for n in range(4):
            eng.wait_ge(s["v_proj"], n + 1)
            eng.tensor_copy(v[0:CK, n // 2, n % 2].rearrange("p h n -> p (h n)"), ps[0:CK, 4 + n, 0:D]).then_inc(s["v_ready"], 1)
        eng.wait_ge(s["v_ready"], 4)

        def scale_v(u):
            b, h, j = UNITS_X[u]
            eng.wait_ge(s["exped"], u + 1)
            did(eng.reciprocal(mx[0:CK, u % 3, 2:3], mx[0:CK, u % 3, 1:2]))
            if u >= 3:
                eng.wait_ge(s["av_done"], u - 2)
            eng.tensor_scalar(vs[0:CK, u % 3, :], v[0:CK, j, b, h, :], mx[0:CK, u % 3, 2:3], None, ALU.mult).then_inc(s["v_scaled"], 1)

        for u, (b, h, j) in enumerate(UNITS_X):
            eng.wait_ge(s["s_done"], u + 1)
            if u >= 3:
                eng.wait_ge(s["exped"], u - 2)
            did(eng.tensor_reduce(mx[0:CK, u % 3, 3:4], ps[0:CK, 2 * (u % 2):2 * (u % 2) + 2, :], mybir.AxisListType.XY, ALU.max))
            eng.tensor_scalar(mx[0:CK, u % 3, 0:1], mx[0:CK, u % 3, 3:4], -1 / 16, None, ALU.mult).then_inc(s["max"], 1)
            if u:
                scale_v(u - 1)
        scale_v(len(UNITS_X) - 1)

        def tile(t):
            return o[:, t, :]

        def all_tokens(param, op):
            did(eng.tensor_tensor(o, o, affine[param].unsqueeze(1).to_broadcast([P, NT, D]), op))

        eng.wait_ge(s["o_taken"], 8)
        nm.vector(eng, tile, tile, runs[0])
        eng.wait_ge(nm.normed, (runs[0] + 1) * NT)
        all_tokens("g0", ALU.mult)
        all_tokens("beta0", ALU.add)
        for j in range(NT // 2):
            eng.wait_ge(s["relued"], j + 1)
            ins_ = eng.tensor_tensor(o[:, 2 * j:2 * j + 2, :], o[:, 2 * j:2 * j + 2, :], relu[:, 2 * j:2 * j + 2, :], ALU.add)
        did(ins_)
        nm.vector(eng, tile, tile, runs[1])
        eng.wait_ge(nm.normed, (runs[1] + 1) * NT)
        all_tokens("g1", ALU.mult)
        all_tokens("beta1", ALU.add)
        did(eng.tensor_tensor(o, o, sh.x, ALU.add))
        nm.vector(eng, tile, lambda t: sh.x[:, t, :], runs[2])
    AFFINE0 = 2 * len(UNITS_X) + 2

    def tensor(eng):
        eng.wait_ge(*before)
        tn.tensor(eng, lambda t, c: sh.x[:, t, c * P:(c + 1) * P], t1, lambda e, t: None)
        eng.wait_ge(s["loaded"], 16 * NLOAD)
        eng.wait_ge(tn.taken, 8 * t1 + 8)
        for n in range(8):
            m, c = n // 4, n % 4
            for k in range(DC):
                mm = eng.matmul(ps[:, n, :], w["Wq"][:, k, m * P:(m + 1) * P], hT[:, k, c * BANK:(c + 1) * BANK],
                                start=k == 0, stop=k == DC - 1)
            mm.then_inc(s["proj"], 1)
        for n in range(4):
            j, m = n // 2, n % 2
            eng.wait_ge(s["moved"], n + 1)
            for k in range(DC):
                mm = eng.matmul(ps[:, n, 0:B * CK], w[("Wk1", "Wk2")[j]][:, k, m * P:(m + 1) * P], cx.rows[:, k, :],
                                start=k == 0, stop=k == DC - 1)
            mm.then_inc(s["proj"], 1)
        eng.wait_ge(s["moved"], 12)
        for n in range(4):
            j, b = n // 2, n % 2
            for k in range(DC):
                eng.matmul(ps[0:CK, 4 + n, 0:D], kT[:, j, k, b * CK:(b + 1) * CK], w[("Wv1", "Wv2")[j]][:, k, :],
                           start=k == 0, stop=False)
            eng.matmul(ps[0:CK, 4 + n, 0:D], sh.ones_row[0:1, 0:CK], rows[("bv1", "bv2")[j]][0:1, :],
                       start=False, stop=True).then_inc(s["v_proj"], 1)
        eng.wait_ge(s["k_ready"], 8)

        def scores(u):
            b, h, j = UNITS_X[u]
            if u >= 2:
                eng.wait_ge(s["exped"], u - 1)
            for c in range(2):
                mm = eng.matmul(ps[0:CK, 2 * (u % 2) + c, :], kh[:, j, h // 8, b, h % 8, :],
                                qT[:, h // 8, b * S + c * BANK:b * S + (c + 1) * BANK], start=True, stop=True)
            mm.then_inc(s["s_done"], 1)

        def queries(b):
            eng.wait_ge(s["v_ready"], 4)
            if b:
                eng.wait_ge(s["o_taken"], 4)
            for t in range(BT):
                dst = ps[:, 4 + t // 2, (t % 2) * D:(t % 2 + 1) * D]
                for k in range(DC):
                    eng.matmul(dst, hT[:, k, (b * BT + t) * P:(b * BT + t + 1) * P], w["Wq"][:, k, :],
                               start=k == 0 and t % 2 == 0, stop=False, skip_group_check=True)
                eng.matmul(dst, sh.ones_row[0:1, :], rows["bq"][0:1, :], start=False, stop=False, skip_group_check=True)

        def products(u):
            b, h, j = UNITS_X[u]
            eng.wait_ge(s["exped"], u + 1)
            eng.wait_ge(s["v_scaled"], u + 1)
            for t in range(BT):
                mm = eng.matmul(ps[:, 4 + t // 2, (t % 2) * D + h * DH:(t % 2) * D + (h + 1) * DH],
                                ex[0:CK, u % 3, t * P:(t + 1) * P], vs[0:CK, u % 3, :], start=False, stop=h == HEADS - 1 and j == 1,
                                skip_group_check=True)
            mm.then_inc(s["av_done"], 1)

        scores(0)
        scores(1)
        for u, (b, h, j) in enumerate(UNITS_X):
            if u + 2 < len(UNITS_X):
                scores(u + 2)
            if h == 0 and j == 0:
                queries(b)
            products(u)
        eng.wait_ge(s["step"], AFFINE0)
        tn.tensor(eng, lambda t, c: o[:, t, c * P:(c + 1) * P], t2, lambda e, t: None)
        eng.wait_ge(tn.taken, 8 * t2 + 8)
        for t in range(NT):
            dst = ps[:, t // 2, (t % 2) * D:(t % 2 + 1) * D]
            for k in range(DC):
                eng.matmul(dst, hT[:, k, t * P:(t + 1) * P], w["Wo"][:, k, :], start=k == 0, stop=False)
            mm = eng.matmul(dst, sh.ones_row[0:1, :], rows["bo"][0:1, :], start=False, stop=True)
            if t % 2:
                mm.then_inc(s["f_done"], 1)

    sh.done = (nm.normed, runs[2] * NT + NT)
    sh.top = mark
    return {"sync": sync, "scalar": scalar, "vector": vector, "tensor": tensor}


def masked_cross_attention(sh):
    ins, nm, tn, ps, cx = sh.ins, sh.norm, sh.turn, sh.psum, sh.context
    before = sh.done
    mark = sh.top
    hT = sh.take("p (c s) -> p c s", DC * TOK, c=DC)
    o = sh.take("p (t d) -> p t d", NT * D, t=NT)
    names = ("W_Q", "W_K", "W_V", "W_O")
    w = {n: sh.take("p (c n) -> p c n", DC * D, c=DC) for n in names}
    mask_i = sh.take("p (t k) -> p t k", NT * CK, t=NT).bitcast(I32)
    mask = sh.take("p (t k) -> p t k", NT * CK, t=NT)
    kT = sh.take("p (c s) -> p c s", DC * B * CK, c=DC)
    kh = sh.take("p (b c h k) -> p b c h k", B * DC * 8 * CK, c=DC, b=B, h=8)
    VN = DH + 1
    v = sh.take("p (b h n) -> p b h n", B * HEADS * VN, b=B, h=HEADS)
    qT = sh.take("p (r c s) -> p r c s", 2 * DC * P, r=2, c=DC)
    sc = sh.take("p (r h k) -> p r h k", 2 * HEADS * CK, r=2, h=HEADS)
    mx = sh.take("p (r h) -> p r h", 2 * HEADS, r=2)
    pT = sh.take("p (r h s) -> p r h s", 2 * 8 * P, r=2, h=8)
    rc = sh.take("p (r h) -> p r h", 2 * HEADS, r=2)
    s = {k: sh.sem("kx_" + k) for k in (
        "loaded", "mask_ready", "proj", "moved", "k_ready", "v_proj", "v_ready", "q_done", "q_moved", "s_done",
        "masked", "less", "exped", "turned", "taken", "av_done", "recip", "scaled", "o_done", "x_done")}
    run, t1, t2 = nm.use(), tn.use(), tn.use()
    BAR = -1e29

    def sync(eng):
        eng.wait_ge(*before)
        for n in names:
            eng.dma_start(w[n], ins["L1_xattn_" + n].rearrange("(c p) n -> p c n", p=P)).then_inc(s["loaded"], 16)
        eng.dma_start(mask_i, ins["mask_Bx1xSxS2_ik0"].rearrange("b o (t p) k -> p (b o t) k", p=P)).then_inc(s["loaded"], 16)

    def tiles(eng, body):
        with eng.Fori(0, NT // 2 - 1) as pair:
            for r in range(2):
                body(pair * 2 + r, r, True)
        body(NT - 2, 0, True)
        body(NT - 1, 1, False)

    def scalar(eng):
        tn.scalar(eng, hT, t1)
        for m in range(DC):
            eng.wait_ge(s["proj"], m + 1)
            eng.activation(kT[:, m, :], ps[:, m, 0:B * CK], ACT.Copy).then_inc(s["moved"], 1)

        def take_q(t, r):
            sh.wait_apart(eng, s["q_done"], t + 1)
            eng.activation(qT[:, r].rearrange("p c s -> p (c s)"), ps[:, 7, 0:DC * P], ACT.Copy, scale=0.25).then_inc(s["q_moved"], 1)

        def take_turned(t, half):
            sh.wait_apart(eng, s["turned"], t * 2 + half + 1)
            eng.activation(pT[0:CK, half].rearrange("p h s -> p (h s)"), ps[0:CK, 4:6, :].rearrange("p b s -> p (b s)"),
                           ACT.Copy).then_inc(s["taken"], 1)

        def exponentials(t, r):
            sh.wait_apart(eng, s["less"], t + 1)
            eng.activation(sc[:, r], sc[:, r], ACT.Exp).then_inc(s["exped"], 1)

        take_q(0, 0)
        exponentials(0, 0)

        def body(t, r, more):
            if more:
                take_q(t + 1, 1 - r)
            take_turned(t, 0)
            take_turned(t, 1)
            if more:
                exponentials(t + 1, 1 - r)
        tiles(eng, body)
        tn.scalar(eng, hT, t2)
        nm.scalar(eng, run)

    def vector(eng):
        eng.wait_ge(s["loaded"], 80)
        eng.tensor_copy(mask, mask_i).then_inc(s["mask_ready"], 1)
        eng.wait_ge(s["mask_ready"], 1)
        eng.tensor_scalar(mask, mask, 0.0, -1e30, ALU.is_equal, ALU.mult).then_inc(s["mask_ready"], 1)
        eng.memset(v, 1.0).then_inc(s["mask_ready"], 1)
        eng.wait_ge(s["mask_ready"], 3)
        eng.wait_ge(cx.s["heads"], 3)
        for m in range(DC):
            eng.wait_ge(s["moved"], m + 1)
            for b in range(B):
                shape = [P, 8, CK]
                eng.tensor_tensor(kh[:, b, m], kT[:, m, b * CK:(b + 1) * CK].unsqueeze(1).to_broadcast(shape),
                                  cx.of_head.unsqueeze(2).to_broadcast(shape), ALU.mult).then_inc(s["k_ready"], 1)
        for b in range(B):
            eng.wait_ge(s["v_proj"], b + 1)
            eng.tensor_copy(v[0:CK, b, :, 0:DH], ps[0:CK, 2 + b, 0:D].rearrange("p (h n) -> p h n", h=HEADS)).then_inc(s["v_ready"], 1)

        def scores(t, r):
            sh.wait_apart(eng, s["s_done"], t + 1)
            quarters = [P, 4, 4, CK]
            eng.tensor_tensor(sc[:, r].rearrange("p (a h) k -> p a h k", a=4),
                              ps[:, 0:4, 0:4 * CK].rearrange("p a (h k) -> p a h k", h=4),
                              mask[:, bass.ds(t, 1), :].unsqueeze(1).to_broadcast(quarters), ALU.add).then_inc(s["masked"], 1)
            eng.wait_ge(s["masked"], t * 3 + 1)
            eng.tensor_reduce(mx[:, r], sc[:, r], AX_X, ALU.max).then_inc(s["masked"], 1)
            eng.wait_ge(s["masked"], t * 3 + 2)
            eng.tensor_scalar(mx[:, r], mx[:, r], BAR, None, ALU.max).then_inc(s["masked"], 1)
            eng.wait_ge(s["masked"], t * 3 + 3)
            eng.tensor_tensor(sc[:, r], sc[:, r], mx[:, r].unsqueeze(2).to_broadcast([P, HEADS, CK]), ALU.subtract)\
                .then_inc(s["less"], 1)

        eng.memset(rc[:, 0, 0:1], 0.0).then_inc(s["scaled"], 1)
        eng.wait_ge(s["scaled"], 1)
        scores(0, 0)

        def body(t, r, more):
            if more:
                scores(t + 1, 1 - r)
            sh.wait_apart(eng, s["av_done"], t + 1)
            src = ps[:, 6, 0:HEADS * VN].rearrange("p (h n) -> p h n", h=HEADS)
            eng.tensor_scalar(rc[:, r], src[:, :, DH], 1e-30, None, ALU.max).then_inc(s["recip"], 1)
            eng.wait_ge(s["recip"], t * 2 + 1)
            eng.reciprocal(rc[:, r], rc[:, r]).then_inc(s["recip"], 1)
            eng.wait_ge(s["recip"], t * 2 + 2)
            eng.tensor_tensor(o[:, bass.ds(t, 1), :].rearrange("p o (h n) -> p (o h) n", h=HEADS), src[:, :, 0:DH],
                              rc[:, r].unsqueeze(2).to_broadcast([P, HEADS, DH]), ALU.mult).then_inc(s["scaled"], 1)
        tiles(eng, body)
        for j in range(NT // 2):
            eng.wait_ge(s["o_done"], j + 1)
            pair = sh.x[:, 2 * j:2 * j + 2, :]
            eng.tensor_tensor(pair, pair, ps[:, j, :].rearrange("p (t d) -> p t d", t=2), ALU.add).then_inc(s["x_done"], 1)
        eng.wait_ge(s["x_done"], NT // 2)
        nm.vector(eng, lambda t: sh.x[:, t, :], lambda t: sh.x[:, t, :], run)

    def tensor(eng):
        eng.wait_ge(*before)
        tn.tensor(eng, lambda t, c: sh.x[:, t, c * P:(c + 1) * P], t1, lambda e, t: None)
        eng.wait_ge(s["loaded"], 80)
        eng.wait_ge(tn.taken, 8 * t1 + 8)
        for m in range(DC):
            for k in range(DC):
                mm = eng.matmul(ps[:, m, 0:B * CK], w["W_K"][:, k, m * P:(m + 1) * P], cx.rows[:, k, :],
                                start=k == 0, stop=k == DC - 1)
            mm.then_inc(s["proj"], 1)
        for b in range(B):
            for k in range(DC):
                mm = eng.matmul(ps[0:CK, 2 + b, 0:D], cx.rows[:, k, b * CK:(b + 1) * CK], w["W_V"][:, k, :],
                                start=k == 0, stop=k == DC - 1)
            mm.then_inc(s["v_proj"], 1)
        eng.wait_ge(s["k_ready"], 4)
        eng.wait_ge(s["v_ready"], 2)

        def queries(t):
            for m in range(DC):
                for k in range(DC):
                    mm = eng.matmul(ps[:, 7, m * P:(m + 1) * P], w["W_Q"][:, k, m * P:(m + 1) * P],
                                    hT[:, k, bass.ds(t * P, P)], start=k == 0, stop=k == DC - 1)
            mm.then_inc(s["q_done"], 1)

        def scores(t, r, b):
            eng.wait_ge(s["q_moved"], t + 1)
            if not isinstance(t, int) or t > 0:
                eng.wait_ge(s["masked"], t * 3 - 2)
            for a in range(4):
                mm = eng.matmul(ps[:, a, 0:4 * CK], qT[:, r, a // 2, :], kh_of(b, a), start=True, stop=True)
            mm.then_inc(s["s_done"], 1)

        def kh_of(b, a):
            one = kh[:, bass.ds(b, 1), a // 2, 4 * (a % 2):4 * (a % 2) + 4, :]
            return one.rearrange("p o h k -> p (o h k)")

        def turn(t, r, half):
            if half == 0:
                eng.wait_ge(s["exped"], t + 1)
            if half:
                eng.wait_ge(s["taken"], t * 2 + 1)
            for h in range(8):
                mm = eng.transpose(ps[0:CK, 4 + h // 4, (h % 4) * P:(h % 4 + 1) * P], sc[:, r, 8 * half + h, :], sh.ident)
            mm.then_inc(s["turned"], 1)

        def products(t, b):
            for half in range(2):
                eng.wait_ge(s["taken"], t * 2 + half + 1)
                if half == 0:
                    eng.wait_ge(s["scaled"], t + 1)
                for h in range(8):
                    n = 8 * half + h
                    mm = eng.matmul(ps[:, 6, n * VN:(n + 1) * VN], pT[0:CK, half, h, :],
                                    v[0:CK, bass.ds(b, 1), n, :].rearrange("p o n -> p (o n)"), start=True, stop=True)
            mm.then_inc(s["av_done"], 1)

        queries(0)
        scores(0, 0, 0)

        def tile(t, r, b, next_b, more):
            if more:
                queries(t + 1)
            turn(t, r, 0)
            if more:
                scores(t + 1, 1 - r, next_b)
            turn(t, r, 1)
            products(t, b)

        for b in range(B):
            with eng.Fori(b * BT // 2, (b + 1) * BT // 2 - 1) as pair:
                for r in range(2):
                    tile(pair * 2 + r, r, b, b, True)
            last = (b + 1) * BT - 1
            tile(last - 1, 0, b, b, True)
            tile(last, 1, b, min(b + 1, B - 1), last < NT - 1)
        eng.wait_ge(s["scaled"], NT + 1)
        tn.tensor(eng, lambda t, c: o[:, t, c * P:(c + 1) * P], t2, lambda e, t: None)
        eng.wait_ge(tn.taken, 8 * t2 + 8)
        for t in range(NT):
            dst = ps[:, t // 2, (t % 2) * D:(t % 2 + 1) * D]
            for k in range(DC):
                mm = eng.matmul(dst, hT[:, k, t * P:(t + 1) * P], w["W_O"][:, k, :], start=k == 0, stop=k == DC - 1)
            if t % 2:
                mm.then_inc(s["o_done"], 1)

    sh.done = (nm.normed, run * NT + NT)
    sh.top = mark
    return {"sync": sync, "scalar": scalar, "vector": vector, "tensor": tensor}


def gelu_attention(sh):
    ins, nm, tn, ps = sh.ins, sh.norm, sh.turn, sh.psum
    before = sh.done
    mark = sh.top
    WIDE = ins["L1_attn_Wv"].shape[1]
    DV = WIDE // HEADS
    GW = G * DV
    FC = WIDE // P
    o_tok = sh.take("p (t i n) -> p t i n", NT * WIDE, i=GROUPS, t=BT)
    early = o_tok.rearrange("p t i n -> p (t i n)")
    hT = early[:, 0:DC * TOK].rearrange("p (c s) -> p c s", c=DC)
    at = DC * TOK
    wk = early[:, at:at + DC * D].rearrange("p (c n) -> p c n", c=DC)
    at += DC * D
    wv = early[:, at:at + DC * WIDE].rearrange("p (c n) -> p c n", c=DC)
    at += DC * WIDE
    bv = early[:, at:at + WIDE]
    at += WIDE
    bk = early[:, at:at + DC]
    at += DC
    v_out = early[:, at:at + 4 * WIDE].rearrange("p (r n) -> p r n", r=4)
    assert at + 4 * WIDE <= NT * WIDE
    inner = sh.top
    parts_scratch = sh.nc.dram_tensor("l1_parts", [2, PARTS, GROUPS, G * DH, S], BF16, kind="Internal").ap()
    v_scratch = sh.nc.dram_tensor("l1_v", [GROUPS, S, GW], F32, kind="Internal").ap()
    loaded, wf_in = sh.sem("l1_loaded"), sh.sem("l1_wf_in")
    v_done, v_kept = sh.sem("l1_v_done"), sh.sem("l1_v_kept")
    v_sent = [sh.sem(f"l1_v_sent{r}") for r in range(4)]
    o_turned, o_done, x_done, gelu_done = (sh.sem("l1_" + k) for k in ("o_turned", "o_done", "x_done", "gelu_done"))
    run, trun = nm.use(), tn.use()
    tasks = [(0, m, b, None, None) for b in range(B) for m in range(2)] + \
            [(1, m, b, wk, bk) for b in range(B) for m in range(2)]
    sent, wp = write_parts(sh, "l1p", tasks, parts_scratch, None, hT, before)
    sh.top = inner

    def v_load(eng, i, dst, sem):
        for h in range(G):
            eng.dma_start(dst[:, :, h, 0:DV], v_scratch[bass.ds(i, 1), :, h * DV:(h + 1) * DV]
                          .rearrange("o (t p) n -> p (o t) n", p=P)).then_inc(sem, 16)
    v_load.count = 16 * G

    def out_tok(i, qc, h, heads):
        return lambda t: o_tok[:, qc * 4 + t, bass.ds(i, 1), h * DV:(h + 1) * DV]

    s, OUTS, att = causal_attention(sh, "l1", DV, 1.0, v_load, out_tok)
    sh.top = inner
    wf = sh.take("p (c n) -> p c n", FC * D, c=FC)
    bf = sh.take(None, D)
    oT = sh.take("p (r f s) -> p r f s", 2 * FC * P, r=2, f=FC)

    def sync(eng):
        eng.wait_ge(*before)
        eng.dma_start(wk, ins["L1_attn_Wk"].rearrange("(c p) n -> p c n", p=P)).then_inc(loaded, 16)
        eng.dma_start(wv, ins["L1_attn_Wv"].rearrange("(c p) n -> p c n", p=P)).then_inc(loaded, 16)
        eng.dma_start(bk, feature_columns(ins["L1_attn_bk"]), allow_slow_non_contiguous=True).then_inc(loaded, 16)
        eng.dma_start(bv, on_all_partitions(ins["L1_attn_bv"])).then_inc(loaded, 16)
        wp["sync"](eng)
        for t in range(NT):
            eng.wait_ge(v_kept, 2 * t + 2)
            dst = v_scratch[t // BT * NG:(t // BT + 1) * NG, t % BT * P:(t % BT + 1) * P].rearrange("g p n -> p g n")
            eng.dma_start(dst, v_out[:, t % 4].rearrange("p (g n) -> p g n", g=NG)).then_inc(v_sent[t % 4], 16)

        def first_wait(eng):
            for both in sent:
                eng.wait_ge(*both)
            for sem in v_sent:
                eng.wait_ge(sem, 16 * NT // 4)
        att["sync"](eng, parts_scratch, first_wait)
        eng.wait_ge(s["scaled"], 4 + 4 * OUTS * GROUPS)
        eng.dma_start(wf, ins["L1_attn_Wf"].rearrange("(c p) n -> p c n", p=P)).then_inc(wf_in, 16)
        eng.dma_start(bf[0:1, :], ins["L1_attn_bf"].rearrange("(o d) -> o d", o=1)).then_inc(wf_in, 16)

    def pool(eng):
        wp["pool"](eng)
        att["pool"](eng, sent)

    def scalar(eng):
        tn.scalar(eng, hT, trun)
        eng.wait_ge(tn.taken, 8 * trun + 8)
        eng.wait_ge(loaded, 64)
        wp["scalar"](eng)
        att["scalar"](eng)
        for t in range(NT):
            eng.wait_ge(o_turned, t + 1)
            if t >= 2:
                eng.wait_ge(o_done, t - 1)
            eng.activation(oT[:, t % 2].rearrange("p f s -> p (f s)"),
                           ps[:, 2 * (t % 2):2 * (t % 2) + 2, :].rearrange("p b s -> p (b s)"), ACT.Gelu).then_inc(gelu_done, 1)
        nm.scalar(eng, run)

    def vector(eng):
        wp["vector"](eng)
        for j in range(2 * NT):
            t, half = j // 2, j % 2
            eng.wait_ge(v_done, j + 1)
            if t >= 4:
                eng.wait_ge(v_sent[t % 4], 16 * (t // 4))
            cols = slice(half * BANK, (half + 1) * BANK)
            eng.tensor_tensor(v_out[:, t % 4, cols], ps[:, j % 8, :], bv[:, cols], ALU.add).then_inc(v_kept, 1)
        for sem in v_sent:
            eng.wait_ge(sem, 16 * NT // 4)
        att["vector"](eng)
        for t in range(NT):
            eng.wait_ge(o_done, t + 1)
            tile = sh.x[:, t, :]
            eng.scalar_tensor_tensor(tile, tile, 2.0, ps[:, 4 + t % 2, 0:D], ALU.mult, ALU.add).then_inc(x_done, 1)
        eng.wait_ge(x_done, NT)
        nm.vector(eng, lambda t: sh.x[:, t, :], lambda t: sh.x[:, t, :], run)

    def tensor(eng):
        eng.wait_ge(*before)
        tn.tensor(eng, lambda t, c: sh.x[:, t, c * P:(c + 1) * P], trun, lambda e, t: None)
        eng.wait_ge(loaded, 64)
        eng.wait_ge(tn.taken, 8 * trun + 8)
        wp["tensor"](eng)
        eng.wait_ge(wp["taken"], len(tasks))
        for j in range(2 * NT):
            t, half = j // 2, j % 2
            if j >= 8:
                eng.wait_ge(v_kept, j - 7)
            for k in range(DC):
                mm = eng.matmul(ps[:, j % 8, :], hT[:, k, t * P:(t + 1) * P], wv[:, k, half * BANK:(half + 1) * BANK],
                                start=k == 0, stop=k == DC - 1)
            mm.then_inc(v_done, 1)
        eng.wait_ge(v_kept, 2 * NT)
        eng.wait_ge(*sh.masks.ready)
        att["tensor"](eng)
        eng.wait_ge(s["scaled"], 4 + 4 * OUTS * GROUPS)

        def turn(t):
            if t >= 2:
                eng.wait_ge(gelu_done, t - 1)
            for f in range(FC):
                src = o_tok[:, t % BT, (t // BT) * NG + f // 2, (f % 2) * P:(f % 2 + 1) * P]
                mm = eng.transpose(ps[:, 2 * (t % 2) + f // 4, (f % 4) * P:(f % 4 + 1) * P], src, sh.ident)
            mm.then_inc(o_turned, 1)

        turn(0)
        eng.wait_ge(wf_in, 32)
        for t in range(NT):
            if t + 1 < NT:
                turn(t + 1)
            eng.wait_ge(gelu_done, t + 1)
            if t >= 2:
                eng.wait_ge(x_done, t - 1)
            dst = ps[:, 4 + t % 2, 0:D]
            for f in range(FC):
                eng.matmul(dst, oT[:, t % 2, f, :], wf[:, f, :], start=f == 0, stop=False)
            eng.matmul(dst, sh.ones_row[0:1, :], bf[0:1, :], start=False, stop=True).then_inc(o_done, 1)

    sh.done = (nm.normed, run * NT + NT)
    sh.top = mark
    return {"sync": sync, "pool": pool, "scalar": scalar, "vector": vector, "tensor": tensor}


def routed_ffn(sh):
    ins, nm, tn, ps = sh.ins, sh.norm, sh.turn, sh.psum
    before = sh.done
    mark = sh.top
    GP, PER = 2, 4
    LG = GP + EXPERTS
    hT = sh.take("p (c s) -> p c s", DC * TOK, c=DC)
    w12 = sh.take("p (r w c n) -> p r w c n", 2 * 2 * DC * HID, r=2, w=2, c=DC)
    w3 = sh.take("p (r c n) -> p r c n", 3 * HC * D, r=3, c=HC)
    silu = sh.take("p (r s) -> p r s", 2 * BANK, r=2)
    hid = sh.take("p (r m s) -> p r m s", 2 * HC * TOK, r=2, m=HC)
    gw = sh.take("p (c e) -> p c e", DC * LG, c=DC)
    bias = sh.take(None, 12)
    lg = sh.take("p (t e) -> p t e", NT * LG, t=NT)
    ev = sh.take("p (t e) -> p t e", NT * EXPERTS, t=NT)
    ex = sh.take("p (t e) -> p t e", NT * EXPERTS, t=NT)
    one1 = sh.take("p (t e) -> p t e", NT * EXPERTS, t=NT)
    one2 = sh.take("p (t e) -> p t e", NT * EXPERTS, t=NT)
    wt = sh.take("p (t e) -> p t e", NT * EXPERTS, t=NT)
    small = sh.take("p (k t) -> p k t", 8 * NT, k=8)
    diff, sel0, sel1, gp, z, best1, best2 = (small[:, k] for k in range(7))
    top = TopTwo(sh, "rt", EXPERTS)
    s = {k: sh.sem("rt_" + k) for k in ("loaded", "logits", "exped", "ab_done", "silued", "hid_made", "o_done", "added")}
    w_in = [sh.sem(f"rt_w_in{r}") for r in range(3)]
    h_in = sh.sem("rt_h_in")
    run, trun = nm.use(), tn.use()
    wide = [P, NT, EXPERTS]
    UNITS_L = 2 * CH * HC
    exp_at = EXPERTS + 1 + 4 + 2 + 5 + 1

    def loop(eng, body):
        with eng.Fori(0, EXPERTS // 2 - 1) as pair:
            for r in range(2):
                body(pair * 2 + r, r)
        body(EXPERTS - 2, 0)
        body(EXPERTS - 1, 1)

    def sync(eng):
        eng.wait_ge(*before)
        for k, (name, n) in enumerate((("wg", GP), ("we", EXPERTS))):
            eng.dma_start(gw[:, :, k * GP:k * GP + n], ins["L1_ffn_" + name].rearrange("(c p) e -> p c e", p=P),
                          allow_slow_non_contiguous=True).then_inc(s["loaded"], 16)
        for k, (name, n) in enumerate((("gb", GP), ("eb", EXPERTS))):
            eng.dma_start(bias[0:1, k * GP:k * GP + n], ins["L1_ffn_" + name].rearrange("(o e) -> o e", o=1)).then_inc(s["loaded"], 16)
        for i, name in enumerate(("w_in", "w1")):
            for w in range(2):
                eng.dma_start(w12[:, i, w], ins["L1_ffn_" + name][:, w * HID:(w + 1) * HID]
                              .rearrange("(c p) n -> p c n", p=P)).then_inc(h_in, 16)
        eng.dma_start(w3[:, 2], ins["L1_ffn_w_out"].rearrange("(c p) n -> p c n", p=P)).then_inc(w_in[2], 16)

        def load(e, r):
            eng.dma_start(w3[:, r], ins["L1_ffn_w2"][bass.ds(e, 1)].rearrange("o (c p) n -> p (o c) n", p=P))\
                .then_inc(w_in[r], 16)

        load(0, 0)
        load(1, 1)

        def body(e, r):
            if not isinstance(e, int):
                eng.wait_ge(s["o_done"], (e + 2) * CH)
                load(e + 2, r)
        loop(eng, body)

    def scalar(eng):
        tn.scalar(eng, hT, trun)
        eng.wait_ge(top.step, exp_at)
        eng.activation(ex, ex, ACT.Exp).then_inc(s["exped"], 1)
        eng.activation(gp, gp, ACT.Exp).then_inc(s["exped"], 1)
        for u in range(UNITS_L):
            eng.wait_ge(s["ab_done"], u + 1)
            eng.wait_ge(s["hid_made"], u + 1)
            eng.activation(silu[:, u % 2], ps[:, 2 * (u % 2), :], ACT.Silu).then_inc(s["silued"], 1)
        nm.scalar(eng, run)

    def vector(eng):
        eng.wait_ge(*before)
        top.start(eng)
        eng.wait_ge(s["logits"], 1)
        top.did(eng.tensor_copy(lg, ps[:, 0, 0:NT * LG].rearrange("p (t e) -> p t e", t=NT)))
        top.wait(eng)
        top.did(eng.tensor_tensor(diff, lg[:, :, 0], lg[:, :, 1], ALU.subtract))
        top.wait(eng)
        top.did(eng.tensor_scalar(sel0, diff, 0.0, None, ALU.is_ge))
        top.did(eng.tensor_scalar(sel1, diff, 0.0, None, ALU.is_lt))
        top.did(eng.scalar_tensor_tensor(gp, diff, -1.0, diff, ALU.mult, ALU.min))
        top.wait(eng)
        for g, other in enumerate((sel1, sel0)):
            e0 = g * PER
            top.did(eng.scalar_tensor_tensor(ev[:, :, e0:e0 + PER], other.unsqueeze(2).to_broadcast([P, NT, PER]), -1e30,
                                             lg[:, :, GP + e0:GP + e0 + PER], ALU.mult, ALU.add))
        top.wait(eng)
        top.pick(eng, ev, best1, one1)
        top.did(eng.tensor_tensor(ex, ev, best1.unsqueeze(2).to_broadcast(wide), ALU.subtract))
        assert top.steps == exp_at, top.steps
        top.did(eng.scalar_tensor_tensor(ev, one1, -1e30, ev, ALU.mult, ALU.add))
        top.wait(eng)
        top.pick(eng, ev, best2, one2)
        top.did(eng.tensor_tensor(one1, one1, one2, ALU.add))
        eng.wait_ge(s["exped"], 2)
        top.did(eng.tensor_reduce(z, ex, AX_X, ALU.add))
        top.did(eng.tensor_scalar(gp, gp, 1.0, None, ALU.add))
        top.wait(eng)
        top.did(eng.tensor_tensor(z, z, gp, ALU.mult))
        top.wait(eng)
        top.did(eng.reciprocal(z, z))
        top.did(eng.tensor_tensor(one1, one1, ex, ALU.mult))
        top.wait(eng)
        top.did(eng.tensor_tensor(wt, one1, z.unsqueeze(2).to_broadcast(wide), ALU.mult))
        top.wait(eng)
        eng.memset(hid[:, 0, 0, 0:1], 0.0).then_inc(s["hid_made"], 2)
        eng.wait_ge(s["hid_made"], 2)
        for u in range(UNITS_L):
            i, c, m = u // (CH * HC), u // HC % CH, u % HC
            eng.wait_ge(s["silued"], u + 1)
            eng.tensor_tensor(hid[:, i, m, c * BANK:(c + 1) * BANK], silu[:, u % 2], ps[:, 2 * (u % 2) + 1, :], ALU.mult)\
                .then_inc(s["hid_made"], 1)

        def out(c, t):
            return ps[:, 4 + 2 * (c % 2) + t // 2, (t % 2) * D:(t % 2 + 1) * D]

        for c in range(CH):
            eng.wait_ge(s["o_done"], c + 1)
            for t in range(4):
                n = 4 * c + t
                eng.tensor_tensor(sh.x[:, n, :], sh.x[:, n, :], out(c, t), ALU.add).then_inc(s["added"], 1)

        def body(e, r):
            for c in range(CH):
                sh.wait_apart(eng, s["o_done"], (e + 1) * CH + c + 1)
                eng.wait_ge(s["added"], e * NT + 4 * c + 4)
                for t in range(4):
                    n = 4 * c + t
                    eng.scalar_tensor_tensor(sh.x[:, n, :], out(c, t), wt[:, n, bass.ds(e, 1)], sh.x[:, n, :],
                                             ALU.mult, ALU.add).then_inc(s["added"], 1)
        loop(eng, body)
        eng.wait_ge(s["added"], (EXPERTS + 1) * NT)
        nm.vector(eng, lambda t: sh.x[:, t, :], lambda t: sh.x[:, t, :], run)

    def tensor(eng):
        eng.wait_ge(*before)
        tn.tensor(eng, lambda t, c: sh.x[:, t, c * P:(c + 1) * P], trun, lambda e, t: None)
        eng.wait_ge(s["loaded"], 64)
        eng.wait_ge(tn.taken, 8 * trun + 8)
        for t in range(NT):
            dst = ps[:, 0, t * LG:(t + 1) * LG]
            for k in range(DC):
                eng.matmul(dst, hT[:, k, t * P:(t + 1) * P], gw[:, k, :], start=k == 0, stop=False)
            mm = eng.matmul(dst, sh.ones_row[0:1, :], bias[0:1, 0:LG], start=False, stop=True)
        mm.then_inc(s["logits"], 1)
        eng.wait_ge(h_in, 64)
        for u in range(UNITS_L):
            i, c, m = u // (CH * HC), u // HC % CH, u % HC
            eng.wait_ge(s["hid_made"], u + 1)
            for w in range(2):
                for k in range(DC):
                    mm = eng.matmul(ps[:, 2 * (u % 2) + w, :], w12[:, i, w, k, m * P:(m + 1) * P],
                                    hT[:, k, c * BANK:(c + 1) * BANK], start=k == 0, stop=k == DC - 1)
            mm.then_inc(s["ab_done"], 1)

        def products(e, c, i, slot):
            if c >= 2 or not isinstance(e, int) or e >= 0:
                eng.wait_ge(s["added"], (e + 1) * NT + 4 * c - 4)
            for t in range(4):
                for m in range(HC):
                    mm = eng.matmul(ps[:, 4 + 2 * (c % 2) + t // 2, (t % 2) * D:(t % 2 + 1) * D],
                                    hid[:, i, m, c * BANK + t * P:c * BANK + (t + 1) * P], w3[:, slot, m, :],
                                    start=m == 0, stop=m == HC - 1)
            mm.then_inc(s["o_done"], 1)

        eng.wait_ge(w_in[2], 16)
        eng.wait_ge(s["hid_made"], CH * HC + 2)
        for c in range(CH):
            products(-1, c, 0, 2)
        eng.wait_ge(s["hid_made"], UNITS_L + 2)

        def body(e, r):
            eng.wait_ge(w_in[r], (e - r) * 8 + 16)
            for c in range(CH):
                products(e, c, 1, r)
        loop(eng, body)

    sh.done = (nm.normed, run * NT + NT)
    sh.top = mark
    return {"sync": sync, "scalar": scalar, "vector": vector, "tensor": tensor}




def norms(sh):
    sh.norm_all()
    return {}


def causal_masks(sh):
    sh.masks = Masks(sh)
    return {"pool": sh.masks.pool}


def context_rows(sh):
    sh.context = Context(sh)
    return sh.context.stage()


def store_x(sh):
    stored = sh.sem("stored")
    last = sh.done

    def sync(eng):
        eng.wait_ge(*last)
        eng.dma_start(sh.out.rearrange("b (t p) d -> p (b t) d", p=P), sh.x).then_inc(stored, 16)
        eng.wait_ge(stored, 16)
    return {"sync": sync}


def run_phase(sh, stages):
    parts = [stage(sh) for stage in stages]
    with sh.nc.Block() as block:

        @block.sync
        def _(sp):
            for part in parts:
                if "sync" in part:
                    part["sync"](sp)

        @block.gpsimd
        def _(pool):
            for part in parts:
                if "pool" in part:
                    part["pool"](pool)

        @block.scalar
        def _(act):
            for part in parts:
                if "scalar" in part:
                    part["scalar"](act)

        @block.vector
        def _(dve):
            for part in parts:
                if "vector" in part:
                    part["vector"](dve)

        @block.tensor
        def _(pe):
            for part in parts:
                if "tensor" in part:
                    part["tensor"](pe)


def program(nc, ins, out, phases):
    with ExitStack() as ctx:
        sh = Shared(nc, ctx, ins, out)
        room = sh.top
        for n, stages in enumerate(phases):
            if n:
                nc.clear_and_free_semaphores(sh.phase_sems)
                nc.all_engine_barrier()
                sh.done = sh.constants
            sh.phase, sh.phase_sems, sh.top = n, [], room
            run_phase(sh, stages)


def build(nc, ins, out):
    program(nc, ins, out, [
        [constants, norms, mamba, mamba_out, context_rows, query_softmax_attention],
        [norms, causal_masks, kept, self_attention, experts],
        [norms, causal_masks, gelu_attention, context_rows, masked_cross_attention, routed_ffn, store_x],
    ])


_TRANSPOSED = ("L1_xattn_W_Q", "L1_xattn_W_K", "L1_xattn_W_V", "L1_xattn_W_O",
               "L1_ffn_w_in", "L1_ffn_w_out", "L1_ffn_w1", "L1_ffn_w2", "L1_ffn_wg", "L1_ffn_we")


def kernel(**inputs):
    import numpy as _np
    import concourse.bacc as _bacc
    from concourse import mybir as _mybir
    from concourse.bass_utils import run_bass_kernel_spmd as _run

    nc = _bacc.Bacc("TRN2", target_bir_lowering=False, num_devices=1)
    arrays, ins = {}, {}
    for name, value in inputs.items():
        a = _np.asarray(value)
        if name in _TRANSPOSED:
            a = a.swapaxes(-1, -2)
        arrays[name] = _np.ascontiguousarray(a)
        ins[name] = nc.dram_tensor(name, list(a.shape), _mybir.dt.from_np(a.dtype), kind="ExternalInput").ap()
    out = nc.dram_tensor("out", [B, S, D], F32, kind="ExternalOutput").ap()
    build(nc, ins, out)
    if not nc.is_finalized():
        nc.finalize()
    return _run(nc, [arrays], [0]).results[0]["out"]
```

```python
from contextlib import ExitStack

import concourse.bass as bass
from concourse import mybir

F32 = mybir.dt.float32
BF16 = mybir.dt.bfloat16
I32 = mybir.dt.int32
FR = mybir.dt.float32r
ALU = mybir.AluOpType
ACT = mybir.ActivationFunctionType
AX_X = mybir.AxisListType.X

P = 128
D = 256
DC = D // P
B = 2
S = 1024
TOK = B * S
NT = TOK // P
BT = S // P
BANK = 512
EPS = 1e-5
BASE = NT * D + 3 * P
ARENA = 52480 - BASE


class Shared:

    def __init__(self, nc, ctx, ins, out):
        self.nc, self.ctx, self.ins, self.out = nc, ctx, ins, out
        self.arena = ctx.enter_context(nc.sbuf_tensor("base", [P, BASE], F32))
        self.psum = ctx.enter_context(nc.psum_tensor("psum", [P, 8, BANK], F32))
        self.top = 0
        self.x = self.take("p (t d) -> p t d", NT * D, t=NT)
        self.ident = self.take(None, P)
        self.ident_bf = self.take(None, P // 2).bitcast(BF16)
        self.ones_row = self.take(None, P)
        self.ones_bf = self.take(None, P // 2).bitcast(BF16)
        assert self.top == BASE
        self.x_before = nc.dram_tensor("x_before", [P, NT * D], F32, kind="Internal").ap()
        self.phase, self.phase_sems = 0, []
        self.const_ready = ctx.enter_context(nc.semaphore("const_ready"))
        self.constants = (self.const_ready, 8)
        self.done = self.constants

    def norm_all(self):
        self.norm = Norm(self, "norm", NT)
        self.norm_runs = 0
        self.turn = Turn(self)

    def take(self, pattern, count, **sizes):
        view = self.arena[:, self.top:self.top + count]
        assert view.shape[1] == count, (self.top, count)
        self.top += count
        return view.rearrange(pattern, **sizes) if pattern else view

    def start_phase(self, n, ctx, rounded):
        self.phase, self.phase_sems, self.top, self.rounded_top = n, [], 0, 0
        self.arena = ctx.enter_context(self.nc.sbuf_tensor(f"arena{n}", [P, ARENA - rounded], F32))
        if rounded:
            self.rounded = ctx.enter_context(self.nc.sbuf_tensor(f"rounded{n}", [P, rounded], FR))

    def take_parts(self, pattern, count, **sizes):
        views = []
        for _ in range(2):
            view = self.rounded[:, self.rounded_top:self.rounded_top + count]
            assert view.shape[1] == count, (self.rounded_top, count)
            self.rounded_top += count
            views.append(view.rearrange(pattern, **sizes))
        return views

    def wait_apart(self, eng, sem, value):
        eng.wait_ge(self.const_ready, 1)
        eng.wait_ge(sem, value)

    def sem(self, name):
        handle = self.nc.alloc_semaphore(name=f"phase{self.phase}_{name}")
        self.phase_sems.append(handle)
        return handle


def constants(sh):
    def pool(eng):
        eng.memset(sh.ident, 0.0).then_inc(sh.const_ready, 1)
        eng.memset(sh.ident_bf, 0.0).then_inc(sh.const_ready, 1)
        eng.memset(sh.ones_row, 1.0).then_inc(sh.const_ready, 1)
        eng.memset(sh.ones_bf, 1.0).then_inc(sh.const_ready, 1)
        eng.wait_ge(sh.const_ready, 4)
        eng.affine_select(out=sh.ident, in_=sh.ident, compare_op=ALU.not_equal, fill=1.0, base=0,
                          pattern=[[-1, P]], channel_multiplier=1).then_inc(sh.const_ready, 2)
        eng.affine_select(out=sh.ident_bf, in_=sh.ident_bf, compare_op=ALU.not_equal, fill=1.0, base=0,
                          pattern=[[-1, P]], channel_multiplier=1).then_inc(sh.const_ready, 2)
    return {"pool": pool}


class Norm:

    def __init__(self, sh, name, tiles):
        self.sh = sh
        self.tiles = tiles
        self.bn = sh.take("p (t k) -> p t k", tiles * 6, t=tiles)
        self.mv = sh.take("p (t k) -> p t k", tiles * 2, t=tiles)
        self.std = sh.take(None, tiles)
        self.rstd = sh.take(None, tiles)
        self.stats = sh.sem(name + "_stats")
        self.std_ready = sh.sem(name + "_std")
        self.normed = sh.sem(name + "_normed")

    def stats_tile(self, eng, src, t):
        eng.bn_stats(self.bn[:, t, :], src).then_inc(self.stats, 1)

    def aggregate(self, eng, rep=0):
        n = self.tiles
        eng.wait_ge(self.stats, rep * (2 * n + 2) + n)
        eng.memset(self.rstd[:, 0:1], 0.0)
        for t in range(n):
            eng.bn_aggr(self.mv[:, t, :], self.bn[:, t, :]).then_inc(self.stats, 1)
        eng.wait_ge(self.stats, rep * (2 * n + 2) + 2 * n)
        eng.tensor_scalar(self.std, self.mv[:, :, 1], EPS, None, ALU.add).then_inc(self.stats, 1)

    def vector(self, eng, src, dst, rep=0, wait_std=True):
        n = self.tiles
        for t in range(n):
            self.stats_tile(eng, src(t), t)
        self.aggregate(eng, rep)
        self.normalize(eng, src, dst, rep)

    def normalize(self, eng, src, dst, rep=0):
        n = self.tiles
        eng.wait_ge(self.std_ready, rep + 1)
        eng.reciprocal(self.rstd, self.std).then_inc(self.stats, 1)
        eng.wait_ge(self.stats, rep * (2 * n + 2) + 2 * n + 2)
        for t in range(n):
            eng.tensor_scalar(dst(t), src(t), self.mv[:, t, 0:1], self.rstd[:, t:t + 1],
                              ALU.subtract, ALU.mult).then_inc(self.normed, 1)

    def scalar(self, eng, rep=0):
        n = self.tiles
        eng.wait_ge(self.stats, rep * (2 * n + 2) + 2 * n + 1)
        eng.activation(self.std, self.std, ACT.Sqrt).then_inc(self.std_ready, 1)

    def use(self):
        self.sh.norm_runs += 1
        return self.sh.norm_runs - 1


class Turn:

    def __init__(self, sh):
        self.sh = sh
        self.turned, self.taken = sh.sem("turned"), sh.sem("turn_taken")
        self.runs = 0

    def use(self):
        self.runs += 1
        return self.runs - 1

    def tensor(self, eng, src, run, ready):
        for c in range(DC):
            for q in range(NT // 4):
                for t in range(4):
                    if c == 0:
                        ready(eng, 4 * q + t)
                    mm = eng.transpose(self.sh.psum[:, 4 * c + q, t * P:(t + 1) * P],
                                       src(4 * q + t, c), self.sh.ident)
                mm.then_inc(self.turned, 1)

    def scalar(self, eng, dst, run, scale=None, bias=None):
        for c in range(DC):
            for q in range(NT // 4):
                eng.wait_ge(self.turned, 8 * run + 4 * c + q + 1)
                if scale is None:
                    ins = eng.activation(dst[:, c, q * BANK:(q + 1) * BANK], self.sh.psum[:, 4 * c + q, :], ACT.Copy)
                else:
                    ins = eng.activation(dst[:, c, q * BANK:(q + 1) * BANK], self.sh.psum[:, 4 * c + q, :],
                                         ACT.Identity, bias=bias[:, c:c + 1], scale=scale[:, c:c + 1])
                ins.then_inc(self.taken, 1)


def feature_columns(ap):
    return ap.rearrange("(c p) -> p c", p=P)


def on_all_partitions(ap, n=P):
    return ap.rearrange("(o d) -> o d", o=1).broadcast_to([n, ap.shape[0]])



def high_part(eng, high, src):
    return eng.tensor_copy(high, src)


def low_part(eng, low, high, src):
    return eng.tensor_tensor(low, src, high.bitcast(F32), ALU.subtract)


def product_of_parts(eng, dst, a, b, first, last):
    eng.matmul(dst, a[0], b[0], start=first, stop=False)
    eng.matmul(dst, a[0], b[1], start=False, stop=False)
    return eng.matmul(dst, a[1], b[0], start=False, stop=last)


def mamba(sh):
    nc, ins, ps = sh.nc, sh.ins, sh.psum
    NB, E, NS, R, KC = 4, 512, 16, 64, 4
    M = E // P
    H = S // BANK
    U = NS * M
    mark = sh.top
    w_in = sh.take("p (c n) -> p c n", DC * 2 * E, c=DC)
    w_x = sh.take("p (m n) -> p m n", M * (R + 2 * NS), m=M)
    w_dt = sh.take(None, E)
    w_out = sh.take("p (m n) -> p m n", M * D, m=M)
    n_w = sh.take("p (i c) -> p i c", (NB + 1) * DC, i=NB + 1)
    n_b = sh.take("p (i c) -> p i c", (NB + 1) * DC, i=NB + 1)
    n_now = sh.take("p (k c) -> p k c", 2 * DC, k=2)
    cw = sh.take("p (m k) -> p m k", M * KC, m=M)
    cb = sh.take(None, M)
    dtb = sh.take(None, M)
    skip = sh.take(None, M)
    a_log = sh.take("p (m n) -> p m n", M * NS, m=M)
    a_exp = sh.take("p (m n) -> p m n", M * NS, m=M)
    a_neg = sh.take("p (m n) -> p m n", M * NS, m=M)
    skip_diag = sh.take("p (m q) -> p m q", M * P, m=M)
    PAD = KC - 1
    u_in = sh.take("p (m s) -> p m s", M * (PAD + S), m=M)
    sz = sh.take("p (m s) -> p m s", M * S, m=M)
    uc = sh.take("p (m s) -> p m s", M * S, m=M)
    dt = sh.take("p (m s) -> p m s", M * S, m=M)
    dtu = sh.take("p (m s) -> p m s", M * S, m=M)
    dt_low = sh.take(None, S)
    bc = u_in[:, 0, PAD:PAD + S]
    rest = u_in[:, 1, PAD:PAD + S]
    mid0 = u_in[:, 2, PAD:PAD + S // 2].bitcast(BF16)
    parts = sh.take(None, S // 2).bitcast(BF16)
    sel = sh.take("p (n q) -> p n q", 2 * NS * P // 2, n=2 * NS).bitcast(BF16)
    decay = sh.take("p (r m s) -> p r m s", 2 * M * BANK, r=2, m=M)
    drive = sh.take("p (r m s) -> p r m s", 2 * M * BANK, r=2, m=M)
    h = sh.take("p (r m s) -> p r m s", 2 * M * BANK, r=2, m=M)
    hc = sh.take("p (r m s) -> p r m s", 2 * M * BANK, r=2, m=M)

    def hn(t):
        at = PAD + t % (BT // 2) * D
        return u_in[:, t // (BT // 2), at:at + D]

    hT = hc[:, 1].rearrange("p m s -> p (m s)").rearrange("p (c s) -> p c s", c=DC)
    b_sb = sh.take("p (r s) -> p r s", 2 * BANK, r=2)
    spare = sh.take(None, 1)
    carry = sh.take("p (n m) -> p n m", NS * M, n=NS)
    log_y = drive.rearrange("p r m s -> p (r m s)").rearrange("p (m s) -> p m s", m=M)
    rem = decay.rearrange("p r m s -> p (r m s)").rearrange("p (m s) -> p m s", m=M)
    norm = Norm(sh, "mb_norm", BT)

    x_loaded, n_loaded, n_picked = sh.sem("mb_x_loaded"), sh.sem("mb_n_loaded"), sh.sem("mb_n_picked")
    w_loaded, w_out_loaded = sh.sem("mb_w_loaded"), sh.sem("mb_w_out_loaded")
    sel_ready = sh.sem("mb_sel_ready")
    diag_ready, a_exped, a_ready = sh.sem("mb_diag_ready"), sh.sem("mb_a_exped"), sh.sem("mb_a_ready")
    turned = sh.sem("mb_turned")
    ht_ready = sh.sem("mb_ht_ready")
    u_done, u_copied = sh.sem("mb_u_done"), sh.sem("mb_u_copied")
    z_done, z_gated = sh.sem("mb_z_done"), sh.sem("mb_z_gated")
    tapped, conv = sh.sem("mb_tapped"), sh.sem("mb_conv")
    uc_ready = sh.sem("mb_uc_ready")
    xp_done, xp_copied = sh.sem("mb_xp_done"), sh.sem("mb_xp_copied")
    dt_done, v_ready = sh.sem("mb_dt_done"), sh.sem("mb_v_ready")
    neg_ready, ey_ready, rem_ready = sh.sem("mb_neg"), sh.sem("mb_ey"), sh.sem("mb_rem")
    corr_ready, log_ready, soft_ready = sh.sem("mb_corr"), sh.sem("mb_log"), sh.sem("mb_soft")
    dt_ready, dtu_ready = sh.sem("mb_dt_ready"), sh.sem("mb_dtu_ready")
    b_spread, c_spread, b_copied = sh.sem("mb_b_spread"), sh.sem("mb_c_spread"), sh.sem("mb_b_copied")
    decay_ready, drive_ready = sh.sem("mb_decay"), sh.sem("mb_drive")
    scanned, weighted, summed = sh.sem("mb_scanned"), sh.sem("mb_weighted"), sh.sem("mb_summed")
    y_gated = sh.sem("mb_y_gated")
    o_done, x_done = sh.sem("mb_o_done"), sh.sem("mb_x_done")
    carried = sh.sem("mb_carried")
    NW = 8
    PASSES = NB * B
    CT = KC - 1
    ZM = 3
    CREDIT = 2 * M

    def sync(eng):
        eng.dma_start(sh.x, ins["x"].rearrange("b (t p) d -> p (b t) d", p=P)).then_inc(x_loaded, 16)

        for dst, name in ((n_w, "norm_w"), (n_b, "norm_b")):
            eng.dma_start(dst[:, 0:NB], ins["L0_attn_" + name].rearrange("i (c p) -> p i c", p=P),
                          allow_slow_non_contiguous=True).then_inc(n_loaded, 16)

        def load(i):
            for dst, src in (
                (w_in, ins["L0_attn_in_proj_w"][i].rearrange("(c p) n -> p c n", p=P)),
                (w_x, ins["L0_attn_xproj_w"][i].rearrange("(m p) n -> p m n", p=P)),
                (w_dt[0:R, :], ins["L0_attn_dtproj_w"][i]),
                (cw, ins["L0_attn_conv_w"][i].rearrange("(m p) k -> p m k", p=P)),
                (cb, ins["L0_attn_conv_b"][i].rearrange("(m p) -> p m", p=P)),
                (dtb, ins["L0_attn_dtproj_b"][i].rearrange("(m p) -> p m", p=P)),
                (skip, ins["L0_attn_skip_D"][i].rearrange("(m p) -> p m", p=P)),
                (a_log, ins["L0_attn_A_log"][i].rearrange("(m p) n -> p m n", p=P)),
            ):
                eng.dma_start(dst, src, allow_slow_non_contiguous=True).then_inc(w_loaded, 16)

        def load_out(i):
            eng.dma_start(w_out, ins["L0_attn_out_proj_w"][i].rearrange("(m p) n -> p m n", p=P)).then_inc(w_out_loaded, 16)

        load(0)
        load_out(0)
        with eng.Fori(0, NB - 1) as i:
            eng.wait_ge(decay_ready, i * (B * H * NS * M) + ((B - 1) * H * NS * M + 1))
            load(i + 1)
            eng.wait_ge(x_done, (i + 1) * (B * BT // 2))
            load_out(i + 1)

    def pool(eng):
        eng.memset(n_w[:, NB], 0.0).then_inc(n_loaded, 1)
        eng.memset(n_b[:, NB], 0.0).then_inc(n_loaded, 1)
        eng.memset(u_in[:, :, 0:PAD], 0.0).then_inc(sel_ready, 1)
        eng.memset(b_sb[:, 0, 0:1], 0.0).then_inc(drive_ready, CREDIT)
        eng.memset(sel, 0.0).then_inc(sel_ready, 1)
        for part in range(3):
            eng.wait_ge(sel_ready, part + 2)
            eng.affine_select(out=sel, in_=sel, compare_op=ALU.not_equal, fill=1.0, base=-32 * part,
                              pattern=[[-1, 2 * NS], [0, P]], channel_multiplier=1).then_inc(sel_ready, 1)
        with eng.Fori(0, NB) as i:
            with eng.Fori(0, B) as b:
                k = i * B + b
                eng.wait_ge(w_loaded, (i + 1) * (16 * NW))
                eng.wait_ge(uc_ready, k * M + 1)
                for m in range(M):
                    eng.tensor_tensor(skip_diag[:, m, :], sh.ident, skip[:, m:m + 1].to_broadcast([P, P]),
                                      ALU.mult).then_inc(diag_ready, 1)
                for m in range(M):
                    eng.wait_ge(rem_ready, k * M + m + 1)
                    eng.tensor_tensor(rem[:, m, :], dtu[:, m, :], rem[:, m, :], ALU.subtract)\
                        .then_inc(corr_ready, 1)
                sh.wait_apart(eng, dtu_ready, k * M + M)
                for s in range(H):
                    with eng.Fori(0, NS // 2) as pair:
                        for r in range(2):
                            n = (k * H + s) * NS + pair * 2 + r
                            eng.wait_ge(b_copied, n + 1)
                            for m in range(M):
                                eng.wait_ge(scanned, n * M + m + 1)
                                eng.tensor_tensor(drive[:, r, m, :], dtu[:, m, s * BANK:(s + 1) * BANK],
                                                  b_sb[:, r, :], ALU.mult).then_inc(drive_ready, 1)

    def scalar(eng):
        def normalized_rows(k, i):
            norm.scalar(eng, k)
            for j, of_all in enumerate((n_w, n_b)):
                eng.activation(n_now[:, j], of_all[:, bass.ds(i, 1), :].rearrange("p o c -> p (o c)"), ACT.Copy)\
                    .then_inc(n_picked, 1)
            eng.wait_ge(n_picked, k * 2 + 2)
            for c in range(DC):
                for s in range(H):
                    eng.wait_ge(turned, k * (DC * H) + c * H + s + 1)
                    eng.activation(hT[:, c, s * BANK:(s + 1) * BANK], ps[:, 4 + c * H + s, :], ACT.Identity,
                                   bias=n_now[:, 1, c:c + 1], scale=n_now[:, 0, c:c + 1]).then_inc(ht_ready, 1)

        eng.wait_ge(n_loaded, 34)
        normalized_rows(0, 0)
        with eng.Fori(0, NB) as i:
            with eng.Fori(0, B) as b:
                k = i * B + b
                eng.wait_ge(w_loaded, (i + 1) * (16 * NW))
                for m in range(M):
                    for s in range(H):
                        eng.wait_ge(u_done, k * (M * H) + m * H + s + 1)
                        eng.activation(u_in[:, m, PAD + s * BANK:PAD + (s + 1) * BANK],
                                       ps[:, (m * H + s) % 8, :], ACT.Copy).then_inc(u_copied, 1)
                    eng.wait_ge(u_copied, k * (M * H) + (m + 1) * H)
                    eng.activation(uc[:, m, :], u_in[:, m, PAD:PAD + S], ACT.Identity, bias=cb[:, m:m + 1],
                                   scale=cw[:, m, PAD:PAD + 1]).then_inc(tapped, 1)

                def gate(m):
                    for s in range(H):
                        eng.wait_ge(z_done, k * (M * H) + m * H + s + 1)
                        eng.activation(sz[:, m, s * BANK:(s + 1) * BANK], ps[:, (m * H + s) % (ZM * H), :],
                                       ACT.Silu).then_inc(z_gated, 1)

                for m in range(M):
                    if m < ZM:
                        gate(m)
                    eng.wait_ge(conv, k * (CT * M) + (m + 1) * CT)
                    eng.activation(uc[:, m, :], uc[:, m, :], ACT.Silu).then_inc(uc_ready, 1)
                for m in range(M):
                    for s in range(H):
                        eng.wait_ge(dt_done, k * (M * H) + m * H + s + 1)
                        eng.activation(dt[:, m, s * BANK:(s + 1) * BANK], ps[:, (m * H + s) % 8, :],
                                       ACT.Identity, bias=dtb[:, m:m + 1]).then_inc(v_ready, 1)
                for m in range(M):
                    eng.wait_ge(neg_ready, k * M + m + 1)
                    eng.activation(dtu[:, m, :], dtu[:, m, :], ACT.Exp).then_inc(ey_ready, 1)
                eng.activation(a_exp, a_log, ACT.Exp).then_inc(a_exped, 1)
                for m in range(M):
                    eng.wait_ge(ey_ready, k * M + m + 1)
                    eng.activation(log_y[:, m, :], dtu[:, m, :], ACT.Ln, bias=1.0).then_inc(log_ready, 1)
                for m in range(ZM, M):
                    gate(m)
                eng.wait_ge(dtu_ready, k * M + M)
                for s in range(H):
                    def copy_b(n, r):
                        eng.wait_ge(b_spread, n + 1)
                        eng.wait_ge(drive_ready, (n + 1) * M)
                        eng.activation(b_sb[:, r, :], ps[:, 4 + r, :], ACT.Copy).then_inc(b_copied, 1)

                    def decays(n, state, r):
                        for m in range(M):
                            eng.wait_ge(scanned, n * M + m + 1)
                            eng.activation(decay[:, r, m, :], dt[:, m, s * BANK:(s + 1) * BANK], ACT.Exp,
                                           scale=a_neg[:, m, bass.ds(state, 1)]).then_inc(decay_ready, 1)

                    with eng.Fori(0, NS // 2) as pair:
                        for r in range(2):
                            n = (k * H + s) * NS + pair * 2 + r
                            copy_b(n, r)
                            decays(n, pair * 2 + r, r)
                normalized_rows(k + 1, i + b)

    def vector(eng):
        eng.memset(carry[:, 0, :], 0.0).then_inc(scanned, CREDIT)
        eng.wait_ge(x_loaded, 16)
        eng.wait_ge(sel_ready, 1)
        norm.vector(eng, lambda t: sh.x[:, t, :], hn, 0)
        with eng.Fori(0, NB) as i:
            with eng.Fori(0, B) as b:
                k = i * B + b
                for m in range(M):
                    eng.wait_ge(tapped, k * M + m + 1)
                    for tap in range(KC - 2, -1, -1):
                        n = k * (CT * M) + m * CT + (CT - 1 - tap)
                        if tap < KC - 2:
                            eng.wait_ge(conv, n)
                        eng.scalar_tensor_tensor(out=uc[:, m, :], in0=u_in[:, m, tap:tap + S],
                                                 scalar=cw[:, m, tap:tap + 1], in1=uc[:, m, :],
                                                 op0=ALU.mult, op1=ALU.add).then_inc(conv, 1)
                eng.wait_ge(conv, k * (CT * M) + CT * M)
                for s in range(H):
                    cols = slice(s * BANK, (s + 1) * BANK)
                    eng.wait_ge(xp_done, k * H + s + 1)
                    eng.tensor_copy(dt_low[0:R, cols], ps[0:R, 6 + s, :]).then_inc(xp_copied, 1)
                    eng.tensor_copy(bc[0:32, cols], ps[R:R + 32, 6 + s, :]).then_inc(xp_copied, 1)
                XP = 2 * H + 6
                eng.wait_ge(xp_copied, k * XP + 2 * H)
                eng.tensor_copy(parts[0:32, :], bc[0:32, :]).then_inc(xp_copied, 1)
                eng.wait_ge(xp_copied, k * XP + 2 * H + 1)
                eng.tensor_tensor(rest[0:32, :], bc[0:32, :], parts[0:32, :], ALU.subtract).then_inc(xp_copied, 1)
                eng.wait_ge(xp_copied, k * XP + 2 * H + 2)
                eng.tensor_copy(mid0[0:32, :], rest[0:32, :]).then_inc(xp_copied, 1)
                eng.wait_ge(xp_copied, k * XP + 2 * H + 3)
                eng.tensor_copy(parts[32:64, :], mid0[0:32, :]).then_inc(xp_copied, 1)
                eng.tensor_tensor(rest[0:32, :], rest[0:32, :], mid0[0:32, :], ALU.subtract).then_inc(xp_copied, 1)
                eng.wait_ge(xp_copied, k * XP + 2 * H + 5)
                eng.tensor_copy(parts[64:96, :], rest[0:32, :]).then_inc(xp_copied, 1)
                for m in range(M):
                    eng.wait_ge(v_ready, k * (M * H) + (m + 1) * H)
                    eng.scalar_tensor_tensor(out=dtu[:, m, :], in0=dt[:, m, :], scalar=-1.0, in1=dt[:, m, :],
                                             op0=ALU.mult, op1=ALU.min).then_inc(neg_ready, 1)
                for m in range(M):
                    eng.wait_ge(ey_ready, k * M + m + 1)
                    eng.tensor_scalar(rem[:, m, :], dtu[:, m, :], 1.0, 1.0, ALU.add, ALU.subtract)\
                        .then_inc(rem_ready, 1)
                for m in range(M):
                    eng.wait_ge(log_ready, k * M + m + 1)
                    eng.scalar_tensor_tensor(out=dt[:, m, :], in0=dt[:, m, :], scalar=0.0, in1=log_y[:, m, :],
                                             op0=ALU.max, op1=ALU.add).then_inc(soft_ready, 1)
                for m in range(M):
                    eng.wait_ge(soft_ready, k * M + m + 1)
                    eng.wait_ge(corr_ready, k * M + m + 1)
                    eng.tensor_tensor(dt[:, m, :], dt[:, m, :], rem[:, m, :], ALU.add).then_inc(dt_ready, 1)
                eng.wait_ge(a_exped, k + 1)
                eng.tensor_scalar(a_neg, a_exp, -1.0, None, ALU.mult).then_inc(a_ready, 1)
                for m in range(M):
                    eng.wait_ge(dt_ready, k * M + m + 1)
                    eng.tensor_tensor(dtu[:, m, :], dt[:, m, :], uc[:, m, :], ALU.mult).then_inc(dtu_ready, 1)

                def state_step(s, n, state, r):
                    def scan(m):
                        eng.wait_ge(decay_ready, n * M + m + 1)
                        eng.wait_ge(drive_ready, CREDIT + n * M + m + 1)
                        first = 0.0 if s == 0 else carry[:, bass.ds(state, 1), m]
                        eng.tensor_tensor_scan(h[:, r, m, :], decay[:, r, m, :], drive[:, r, m, :], first,
                                               ALU.mult, ALU.add).then_inc(scanned, 1)

                    def weigh(m):
                        if m == 0:
                            eng.wait_ge(c_spread, n + 1)
                        eng.wait_ge(scanned, CREDIT + n * M + m + 1)
                        eng.tensor_tensor(hc[:, r, m, :], h[:, r, m, :], ps[:, 6 + r, :], ALU.mult)\
                            .then_inc(weighted, 1)

                    scan(0)
                    for m in range(1, M):
                        scan(m)
                        weigh(m - 1)
                    weigh(M - 1)
                    if s < H - 1:
                        eng.tensor_copy(carry[:, bass.ds(state, 1), :].rearrange("p o m -> p (o m)"),
                                        h[:, r, :, BANK - 1]).then_inc(carried, 1)

                for s in range(H):
                    if s > 0:
                        eng.wait_ge(carried, k * (NS * (H - 1)) + NS * s)
                        eng.memset(spare, 0.0)
                    with eng.Fori(0, NS // 2) as pair:
                        for r in range(2):
                            state_step(s, (k * H + s) * NS + pair * 2 + r, pair * 2 + r, r)
                    for m in range(M):
                        eng.wait_ge(summed, (k * H + s) * M + m + 1)
                        cols = slice(s * BANK, (s + 1) * BANK)
                        eng.tensor_tensor(sz[:, m, cols], ps[:, m, :], sz[:, m, cols], ALU.mult)\
                            .then_inc(y_gated, 1)
                norm.vector(eng, lambda t: sh.x[:, bass.ds(BT - b * BT + t, 1), :].rearrange("p o d -> p (o d)"),
                            hn, k + 1)
                for j in range(BT // 2):
                    eng.wait_ge(o_done, k * (BT // 2) + j + 1)
                    tiles = sh.x[:, bass.ds(b * BT + 2 * j, 2), :]
                    eng.tensor_tensor(tiles, tiles, ps[:, j, :].rearrange("p (t d) -> p t d", t=2), ALU.add)\
                        .then_inc(x_done, 1)
        eng.wait_ge(ht_ready, (PASSES + 1) * (DC * H))
        eng.memset(spare, 0.0).then_inc(x_done, 1)

    def tensor(eng):
        eng.wait_ge(*sh.constants)
        eng.wait_ge(sel_ready, 5)

        def turn(k):
            for c in range(DC):
                for s in range(H):
                    for t in range(BT // H):
                        if c == 0:
                            eng.wait_ge(norm.normed, k * BT + s * (BT // H) + t + 1)
                        mm = eng.transpose(ps[:, 4 + c * H + s, t * P:(t + 1) * P],
                                           hn(s * (BT // H) + t)[:, c * P:(c + 1) * P], sh.ident)
                    mm.then_inc(turned, 1)

        turn(0)
        with eng.Fori(0, NB) as i:
            with eng.Fori(0, B) as b:
                k = i * B + b
                eng.wait_ge(ht_ready, k * (DC * H) + DC * H)
                eng.wait_ge(w_loaded, (i + 1) * (16 * NW))
                def in_projection(z, m):
                    for s in range(H):
                        j = m * H + s
                        bank = j % (ZM * H) if z else j
                        if z and m < ZM:
                            eng.wait_ge(u_copied, k * (M * H) + j + 1)
                        elif z:
                            eng.wait_ge(v_ready, k * (M * H) + bank + 1)
                        for c in range(DC):
                            mm = eng.matmul(ps[:, bank, :], w_in[:, c, z * E + m * P:z * E + (m + 1) * P],
                                            hT[:, c, s * BANK:(s + 1) * BANK], start=c == 0, stop=c == DC - 1)
                        mm.then_inc(z_done if z else u_done, 1)

                for m in range(M):
                    in_projection(0, m)
                for m in range(ZM):
                    in_projection(1, m)
                eng.wait_ge(u_copied, k * (M * H) + M * H)
                for m in range(M):
                    eng.wait_ge(uc_ready, k * M + m + 1)
                    for s in range(H):
                        mm = eng.matmul(ps[0:R + 2 * NS, 6 + s, :], w_x[:, m, :], uc[:, m, s * BANK:(s + 1) * BANK],
                                        start=m == 0, stop=m == M - 1)
                        if m == M - 1:
                            mm.then_inc(xp_done, 1)
                eng.wait_ge(xp_copied, k * (2 * H + 6) + 2 * H)
                eng.wait_ge(z_gated, k * (M * H) + ZM * H)
                for m in range(M):
                    for s in range(H):
                        eng.matmul(ps[:, (m * H + s) % 8, :], w_dt[0:R, m * P:(m + 1) * P],
                                   dt_low[0:R, s * BANK:(s + 1) * BANK], start=True, stop=True).then_inc(dt_done, 1)
                for m in range(ZM, M):
                    in_projection(1, m)
                eng.wait_ge(z_gated, k * (M * H) + M * H)
                eng.wait_ge(v_ready, k * (M * H) + M * H)
                eng.wait_ge(xp_copied, k * (2 * H + 6) + 2 * H + 6)
                eng.wait_ge(diag_ready, k * M + M)

                def spread(kind, s, state, r):
                    bank = 4 + 2 * kind + r
                    eng.matmul(ps[:, bank, :], sel[0:96, kind * NS + state, :], parts[0:96, s * BANK:(s + 1) * BANK],
                               start=True, stop=True).then_inc(c_spread if kind else b_spread, 1)

                def add_state(n, r, last):
                    for m in range(M):
                        eng.wait_ge(weighted, n * M + m + 1)
                        mm = eng.matmul(ps[:, m, :], sh.ident, hc[:, r, m, :], start=False, stop=last)
                        if last:
                            mm.then_inc(summed, 1)

                for s in range(H):
                    base = (k * H + s) * NS
                    for r in range(2):
                        spread(0, s, r, r)
                        spread(1, s, r, r)
                    if s > 0:
                        eng.wait_ge(y_gated, (k * H + s) * M)
                    for m in range(M):
                        eng.matmul(ps[:, m, :], skip_diag[:, m, :], uc[:, m, s * BANK:(s + 1) * BANK],
                                   start=True, stop=False)
                    with eng.Fori(0, NS // 2 - 1) as pair:
                        for r in range(2):
                            n = base + pair * 2 + r
                            eng.wait_ge(b_copied, n + 1)
                            spread(0, s, pair * 2 + 2 + r, r)
                            add_state(n, r, False)
                            spread(1, s, pair * 2 + 2 + r, r)
                    for r in range(2):
                        add_state(base + NS - 2 + r, r, r == 1)
                eng.wait_ge(w_out_loaded, (i + 1) * 16)
                eng.wait_ge(y_gated, (k + 1) * (H * M))
                for t in range(BT):
                    for m in range(M):
                        mm = eng.matmul(ps[:, t // 2, (t % 2) * D:(t % 2 + 1) * D], sz[:, m, t * P:(t + 1) * P],
                                        w_out[:, m, :], start=m == 0, stop=m == M - 1)
                    if t % 2:
                        mm.then_inc(o_done, 1)
                    if t == BT // 2 + 1:
                        eng.wait_ge(b_copied, (k + 1) * (H * NS))
                        turn(k + 1)
                eng.wait_ge(x_done, (k + 1) * (BT // 2))

    sh.done = (x_done, PASSES * BT // 2 + 1)
    sh.top = mark
    return {"sync": sync, "pool": pool, "scalar": scalar, "vector": vector, "tensor": tensor}


def mamba_out(sh):
    ins, nm = sh.ins, sh.norm
    mark = sh.top
    x0 = sh.take("p (t d) -> p t d", NT * D, t=NT)
    fw, fb = sh.take(None, D), sh.take(None, D)
    loaded, added = sh.sem("fn_loaded"), sh.sem("fn_added")
    run1, run2 = nm.use(), nm.use()
    before = sh.done

    def sync(eng):
        eng.wait_ge(*before)
        eng.dma_start(x0, ins["x"].rearrange("b (t p) d -> p (b t) d", p=P)).then_inc(loaded, 16)
        eng.dma_start(fw, on_all_partitions(ins["L0_attn_fn_w"])).then_inc(loaded, 16)
        eng.dma_start(fb, on_all_partitions(ins["L0_attn_fn_b"])).then_inc(loaded, 16)

    def tile(t):
        return sh.x[:, t, :]

    def scalar(eng):
        nm.scalar(eng, run1)
        nm.scalar(eng, run2)

    def vector(eng):
        eng.wait_ge(*before)
        nm.vector(eng, tile, tile, run1)
        eng.wait_ge(loaded, 48)
        eng.wait_ge(nm.normed, run1 * NT + NT)
        wide = [P, NT, D]
        for n, (v, op) in enumerate(((fw.unsqueeze(1).to_broadcast(wide), ALU.mult),
                                     (fb.unsqueeze(1).to_broadcast(wide), ALU.add), (x0, ALU.add))):
            if n:
                eng.wait_ge(added, n)
            eng.tensor_tensor(sh.x, sh.x, v, op).then_inc(added, 1)
        eng.wait_ge(added, 3)
        nm.vector(eng, tile, tile, run2)

    sh.done = (nm.normed, run2 * NT + NT)
    sh.top = mark
    return {"sync": sync, "scalar": scalar, "vector": vector}


HEADS, DH = 16, 16
G = 4
NG = HEADS // G
GROUPS = B * NG
PARTS = 3
Q_PARTS = (0, 1, 2, 0, 1, 0)
K_PARTS = (0, 0, 0, 1, 1, 2)
STACK = DH * len(Q_PARTS)
UNITS = [(h, t, kc) for t in range(BT) for h in range(G) for kc in range(t // 4 + 1)]


class Masks:

    def __init__(self, sh):
        self.sh = sh
        self.mask_q = sh.take(None, P // 2).bitcast(BF16)
        self.mask_k = sh.take(None, P // 2).bitcast(BF16)
        self.made = sh.sem("masks_made")
        self.ready = (self.made, 4)

    def pool(self, eng):
        made = self.made
        eng.memset(self.mask_q, 0.0).then_inc(made, 1)
        eng.memset(self.mask_k, 0.0).then_inc(made, 1)
        eng.wait_ge(made, 2)
        eng.affine_select(out=self.mask_q, in_=self.mask_q, compare_op=ALU.is_ge, fill=-1e30,
                          base=0, pattern=[[-1, P]], channel_multiplier=1).then_inc(made, 1)
        eng.affine_select(out=self.mask_k, in_=self.mask_k, compare_op=ALU.is_ge, fill=-1e30,
                          base=0, pattern=[[1, P]], channel_multiplier=-1).then_inc(made, 1)


def causal_attention(sh, name, dv, scale, v_load, out_tok):
    ps, nc = sh.psum, sh.nc
    packed = dv == DH
    VW = 32 if packed else 80
    ONE = DH if packed else dv
    OUTW = P if packed else VW
    RE = 4
    qs = sh.take(None, 2 * G * S // 2).bitcast(BF16).rearrange("p (r h s) -> p r h s", r=2, h=G)
    ks = sh.take(None, 2 * G * S // 2).bitcast(BF16).rearrange("p (r h s) -> p r h s", r=2, h=G)
    v = sh.take("p (r t h n) -> p r t h n", 2 * BT * G * VW, r=2, t=BT, h=G)
    mx = sh.take("p (k t h) -> p k t h", 2 * BT * G, k=2, t=BT)
    mr = sh.take("p (k t h) -> p k t h", 2 * BT * G, k=2, t=BT)
    mp = sh.take(None, BT * G * PARTS // 2).bitcast(BF16).rearrange("p (t h j) -> p t h j", t=BT, j=PARTS)
    mt = sh.take(None, S // 2).bitcast(BF16)
    ex = sh.take("p (r h s) -> p r h s", RE * 2 * BANK, r=RE, h=2)
    oa = sh.take("p (r s) -> p r s", 2 * BANK, r=2)
    rc = sh.take("p (r t h) -> p r t h", 2 * 4 * G, r=2, t=4)
    s = {k: sh.sem(f"{name}_{k}") for k in (
        "init", "s_done", "max_taken", "max_done", "mt_done", "mt_taken", "rows_in",
        "st_done", "exped", "av_done", "acc_taken", "turned", "recip", "scaled")}
    stacked = [sh.sem(f"{name}_stacked{r}") for r in range(2)]
    v_in = [sh.sem(f"{name}_v_in{r}") for r in range(2)]
    U1 = len(UNITS)
    if packed:
        units2 = [(qc, [(2 * hp, kt), (2 * hp + 1, kt)], qc) for qc in range(2) for kt in range(4 * qc + 4)
                  for hp in range(2)]
    else:
        units2 = [(qc, [(h, kt), (h, kt + 1)], qc * G + h) for qc in range(2) for h in range(G)
                  for kt in range(0, 4 * qc + 4, 2)]
    U2 = len(units2)
    OUTS = units2[-1][2] + 1
    last_of = {o: max(u for u in range(U2) if units2[u][2] == o) for o in range(OUTS)}
    A0, B0, ACC = 0, 2, 6
    STACK_DMAS = 12
    LAG = 2
    EARLY = U2 * 6 // 8
    TURN = min(EARLY + 1, U2 - 2)
    assert last_of[OUTS - 1] + 4 >= EARLY
    MAXES = 5

    def span(qc, kt):
        first = max(kt * P - qc * BANK, 0)
        return first, BANK - first

    def sync(eng, scratch, stacks_wait, v_wait):
        def load_stacks(i, r):
            for side, (dst, which) in enumerate(((qs, Q_PARTS), (ks, K_PARTS))):
                for blk, part in enumerate(which):
                    src = scratch[side, part, bass.ds(i, 1)].rearrange("o (h d) s -> d (o h) s", h=G)
                    eng.dma_start(dst[blk * DH:(blk + 1) * DH, r], src).then_inc(stacked[r], 16)

        def load(i, r):
            load_stacks(i, r)
            v_load(eng, i, v[:, r], v_in[r])

        def rows(i, r):
            eng.wait_ge(s["mt_taken"], i * 2 + 2)
            for h in range(G):
                eng.dma_start(qs[STACK:STACK + PARTS, r, h, :], mt[PARTS * h:PARTS * (h + 1), :])\
                    .then_inc(s["rows_in"], 16)

        eng.wait_ge(s["init"], 4)
        stacks_wait(eng)
        load_stacks(0, 0)
        load_stacks(1, 1)
        v_wait(eng)
        v_load(eng, 0, v[:, 0], v_in[0])
        v_load(eng, 1, v[:, 1], v_in[1])
        rows(0, 0)

        def body(i, r, more):
            if more:
                rows(i + 1, 1 - r)
            if not isinstance(i, int):
                eng.wait_ge(s["av_done"], (i + 1) * U2)
                load(i + 2, r)

        loop(eng, body)

    def loop(eng, body):
        with eng.Fori(0, GROUPS // 2 - 1) as pair:
            for r in range(2):
                body(pair * 2 + r, r, True)
        body(GROUPS - 2, 0, True)
        body(GROUPS - 1, 1, False)

    def pool(eng, start):
        for wait in start:
            eng.wait_ge(*wait)
        eng.memset(ks[STACK:STACK + PARTS], -1.0).then_inc(s["init"], 1)
        eng.wait_ge(s["init"], 1)
        eng.memset(v, 0.0).then_inc(s["init"], 1)
        eng.wait_ge(s["init"], 2)
        eng.memset(mp, 0.0).then_inc(s["init"], 1)
        eng.wait_ge(s["init"], 3)
        eng.memset(v[:, :, :, :, ONE:ONE + 1], 1.0).then_inc(s["init"], 1)

    def take_rows(eng, i):
        eng.wait_ge(s["mt_done"], i + 1)
        if not isinstance(i, int) or i > 0:
            eng.wait_ge(s["rows_in"], i * (16 * G))
        for c in range(2):
            eng.activation(mt[0:12, c * BANK:(c + 1) * BANK], ps[0:12, A0 + c, :], ACT.Copy)\
                .then_inc(s["mt_taken"], 1)

    def scalar(eng):
        def exponentials(i, r, more):
            for u, (qc, blocks, o) in enumerate(units2):
                eng.wait_ge(s["st_done"], i * U2 + u + 1)
                if u >= RE:
                    eng.wait_ge(s["av_done"], i * U2 + u - RE + 1)
                bank = B0 + 2 * (u % 2)
                widths = [span(qc, kt)[1] for _, kt in blocks]
                if widths[0] == widths[1]:
                    eng.activation(ex[:, u % RE, :, 0:widths[0]], ps[:, bank:bank + 2, 0:widths[0]], ACT.Exp,
                                   scale=scale).then_inc(s["exped"], 2)
                else:
                    for k, w in enumerate(widths):
                        eng.activation(ex[:, u % RE, k, 0:w], ps[:, bank + k, 0:w], ACT.Exp,
                                       scale=scale).then_inc(s["exped"], 1)
                for done in [n for n in range(OUTS) if min(last_of[n] + LAG + 1, U2 - 1) == u]:
                    take_output(i, done)
                if more and u == TURN + 1:
                    take_rows(eng, i + 1)

        def take_output(i, o):
            eng.wait_ge(s["av_done"], i * U2 + last_of[o] + 1)
            eng.activation(oa[0:OUTW, o % 2, :], ps[0:OUTW, ACC + o % 2, :], ACT.Copy).then_inc(s["acc_taken"], 1)

        take_rows(eng, 0)
        loop(eng, exponentials)

    def vector(eng):
        def maxima(i, lo, hi):
            for u in range(lo, hi):
                h, t, kc = UNITS[u]
                w = min((t + 1) * P - kc * BANK, BANK)
                eng.wait_ge(s["s_done"], i * U1 + u + 1)
                eng.tensor_reduce(mx[:, kc, t, h:h + 1], ps[:, A0 + u % 2, 0:w], AX_X, ALU.max)\
                    .then_inc(s["max_taken"], 1)

        def max_parts(i):
            eng.wait_ge(s["max_taken"], (i + 1) * U1)
            eng.tensor_tensor(mx[:, 0, 4:8, :], mx[:, 0, 4:8, :], mx[:, 1, 4:8, :], ALU.max).then_inc(s["max_done"], 1)
            eng.wait_ge(s["max_done"], i * MAXES + 1)
            eng.tensor_copy(mp[:, :, :, 0], mx[:, 0]).then_inc(s["max_done"], 1)
            eng.wait_ge(s["max_done"], i * MAXES + 2)
            eng.tensor_tensor(mr[:, 0], mx[:, 0], mp[:, :, :, 0], ALU.subtract).then_inc(s["max_done"], 1)
            eng.wait_ge(s["max_done"], i * MAXES + 3)
            eng.tensor_copy(mp[:, :, :, 1], mr[:, 0]).then_inc(s["max_done"], 1)
            eng.wait_ge(s["max_done"], i * MAXES + 4)
            eng.tensor_tensor(mp[:, :, :, 2], mr[:, 0], mp[:, :, :, 1], ALU.subtract).then_inc(s["max_done"], 1)

        def output(i, o):
            n = i * OUTS + o
            eng.wait_ge(s["turned"], n + 1)
            heads = G if packed else 1
            src = ps[:, ACC + o % 2, 0:4 * OUTW].rearrange("p (t h n) -> p t h n", t=4, h=heads)
            eng.reciprocal(rc[:, o % 2, :, 0:heads], src[:, :, :, ONE]).then_inc(s["recip"], 1)
            eng.wait_ge(s["recip"], n + 1)
            qc, h = (o, 0) if packed else (o // G, o % G)
            dst = out_tok(i, qc, h, heads)
            for t in range(4):
                eng.tensor_tensor(dst(t), src[:, t, :, 0:dv], rc[:, o % 2, t, 0:heads].unsqueeze(2)
                                  .to_broadcast([P, heads, dv]), ALU.mult).then_inc(s["scaled"], 1)

        eng.wait_ge(s["init"], 4)
        eng.memset(rc, 0.0).then_inc(s["scaled"], 4)
        maxima(0, 0, U1)
        max_parts(0)

        def body(i, r, more):
            lo = 0
            for o in range(OUTS):
                if more:
                    hi = min((last_of[o] + LAG + 3) * U1 // EARLY, U1)
                    maxima(i + 1, lo, hi)
                    if lo < U1 and hi == U1:
                        max_parts(i + 1)
                    lo = hi
                output(i, o)

        loop(eng, body)

    def tensor(eng):
        def score(i, r, u):
            h, t, kc = UNITS[u]
            w = min((t + 1) * P - kc * BANK, BANK)
            diagonal = kc == t // 4
            bank = A0 + u % 2
            if u == 0:
                eng.wait_ge(stacked[r], (i - r) * (8 * STACK_DMAS) + 16 * STACK_DMAS)
                if not isinstance(i, int) or i > 0:
                    eng.wait_ge(s["mt_taken"], i * 2)
            if u >= 2:
                eng.wait_ge(s["max_taken"], i * U1 + u - 1)
            mm = eng.matmul(ps[:, bank, 0:w], qs[0:STACK, r, h, t * P:(t + 1) * P],
                            ks[0:STACK, r, h, kc * BANK:kc * BANK + w], start=True, stop=not diagonal)
            if diagonal:
                mm = eng.matmul(ps[:, bank, w - P:w], sh.ident_bf, sh.masks.mask_q, start=False, stop=True)
            mm.then_inc(s["s_done"], 1)

        def turn_max(i):
            eng.wait_ge(s["max_done"], i * MAXES + 5)
            for c in range(2):
                for t in range(4):
                    mm = eng.matmul(ps[0:12, A0 + c, t * P:(t + 1) * P], mp[:, 4 * c + t].rearrange("p h j -> p (h j)"), sh.ident_bf,
                                    start=True, stop=True)
            mm.then_inc(s["mt_done"], 1)

        def products(i, r, u, between):
            qc, blocks, o = units2[u]
            eng.wait_ge(s["exped"], i * (2 * U2) + 2 * u + 2)
            if u == 0 or units2[u - 1][2] != o:
                eng.wait_ge(s["scaled"], 4 + i * (4 * OUTS) + 4 * max(o - 1, 0))
            for k, (h, kt) in enumerate(blocks):
                first, w = span(qc, kt)
                rows = slice(32 * h, 32 * h + 32) if packed else slice(0, VW)
                mm = eng.matmul(ps[rows, ACC + o % 2, first:BANK], v[:, r, kt, h, :], ex[:, u % RE, k, 0:w],
                                start=kt == 0, stop=kt == 4 * qc + 3)
                if k == 0 and between:
                    between(2)
            mm.then_inc(s["av_done"], 1)

        def turn_output(i, o):
            eng.wait_ge(s["acc_taken"], i * OUTS + o + 1)
            for t in range(4):
                mm = eng.transpose(ps[:, ACC + o % 2, t * OUTW:(t + 1) * OUTW], oa[0:OUTW, o % 2, t * P:(t + 1) * P],
                                   sh.ident[0:OUTW, 0:OUTW])
            mm.then_inc(s["turned"], 1)

        for u in range(U1):
            score(0, 0, u)
        turn_max(0)

        def body(i, r, more):
            lo = 0
            eng.wait_ge(s["rows_in"], (i + 1) * (16 * G))
            eng.wait_ge(v_in[r], (i - r) * (v_load.count // 2) + v_load.count)
            for u, (qc, blocks, o) in enumerate(units2):
                bank = B0 + 2 * (u % 2)
                if u >= 2:
                    eng.wait_ge(s["exped"], i * (2 * U2) + 2 * u - 2)
                hi = min((u + 1) * U1 // EARLY, U1) if more else 0
                cuts = [lo + (hi - lo) * q // 4 for q in range(5)] if more else [0] * 5

                def between(q):
                    for n in range(cuts[q], cuts[q + 1]):
                        score(i + 1, 1 - r, n)

                for k, (h, kt) in enumerate(blocks):
                    first, w = span(qc, kt)
                    diagonal = kt >= 4 * qc
                    mm = eng.matmul(ps[:, bank + k, 0:w], ks[0:STACK + PARTS, r, h, kt * P:(kt + 1) * P],
                                    qs[0:STACK + PARTS, r, h, qc * BANK + first:(qc + 1) * BANK],
                                    start=True, stop=not diagonal)
                    if diagonal:
                        mm = eng.matmul(ps[:, bank + k, 0:P], sh.ident_bf, sh.masks.mask_k, start=False, stop=True)
                    if k == 0:
                        between(0)
                mm.then_inc(s["st_done"], 1)
                between(1)
                if u >= LAG:
                    products(i, r, u - LAG, between)
                else:
                    between(2)
                between(3)
                lo = hi
                if more and u == TURN:
                    turn_max(i + 1)
                for n in range(OUTS):
                    if last_of[n] + LAG + 2 == u:
                        turn_output(i, n)
            for u in range(U2 - LAG, U2):
                products(i, r, u, None)
            for n in range(OUTS):
                if last_of[n] + LAG + 2 > U2 - 1:
                    turn_output(i, n)

        loop(eng, body)

    ns = {"sync": sync, "pool": pool, "scalar": scalar, "vector": vector, "tensor": tensor}
    return s, OUTS, ns


def write_parts(sh, name, tasks, scratch, weights, hT, start):
    ps = sh.psum
    st = sh.take("p (r s) -> p r s", 2 * S, r=2)
    rest = sh.take("p (r s) -> p r s", 2 * S, r=2)
    SLOTS = 4
    part = [sh.take(None, SLOTS * S // 2).bitcast(BF16).rearrange("p (r s) -> p r s", r=SLOTS) for _ in range(PARTS)]
    s = {k: sh.sem(f"{name}_{k}") for k in ("projected", "taken", "part0", "rest", "part1", "part2")}
    sent = [sh.sem(f"{name}_sent{r}") for r in range(SLOTS)]
    N = len(tasks)

    def tensor(eng):
        for n, (side, m, b, w, bias) in enumerate(t for t in tasks if t[3] is not None):
            if n >= 4:
                eng.wait_ge(s["taken"], n - 3 + (N - n_proj))
            for c in range(2):
                for k in range(DC):
                    mm = eng.matmul(ps[:, 2 * (n % 4) + c, :], w[:, k, m * P:(m + 1) * P],
                                    hT[:, k, b * S + c * BANK:b * S + (c + 1) * BANK], start=k == 0, stop=k == DC - 1)
            mm.then_inc(s["projected"], 1)

    def scalar(eng):
        proj = 0
        for n, (side, m, b, w, bias) in enumerate(tasks):
            if n >= 2:
                eng.wait_ge(s["rest"], n - 1)
            if n >= SLOTS:
                eng.wait_ge(sent[n % SLOTS], (n // SLOTS) * 48)
            if w is not None:
                proj += 1
                eng.wait_ge(s["projected"], proj)
                src = ps[:, 2 * ((proj - 1) % 4):2 * ((proj - 1) % 4) + 2, :].rearrange("p c s -> p (c s)")
            else:
                src = hT[:, m, b * S:(b + 1) * S]
            if bias is None:
                eng.activation(st[:, n % 2, :], src, ACT.Copy).then_inc(s["taken"], 1)
            else:
                eng.activation(st[:, n % 2, :], src, ACT.Identity, bias=bias[:, m:m + 1]).then_inc(s["taken"], 1)
            eng.wait_ge(s["taken"], n + 1)
            eng.activation(part[0][:, n % SLOTS, :], st[:, n % 2, :], ACT.Copy).then_inc(s["part0"], 1)

    def vector(eng):
        for n in range(N):
            eng.wait_ge(s["part0"], n + 1)
            if n >= 2:
                eng.wait_ge(s["part2"], n - 1)
            if n >= SLOTS:
                eng.wait_ge(sent[n % SLOTS], (n // SLOTS) * 48)
            eng.tensor_tensor(rest[:, n % 2, :], st[:, n % 2, :], part[0][:, n % SLOTS, :], ALU.subtract)\
                .then_inc(s["rest"], 1)
            eng.wait_ge(s["rest"], n + 1)
            eng.tensor_copy(part[1][:, n % SLOTS, :], rest[:, n % 2, :]).then_inc(s["part1"], 1)

    def pool(eng):
        for n in range(N):
            eng.wait_ge(s["part1"], n + 1)
            if n >= SLOTS:
                eng.wait_ge(sent[n % SLOTS], (n // SLOTS) * 48)
            eng.tensor_tensor(part[2][:, n % SLOTS, :], rest[:, n % 2, :], part[1][:, n % SLOTS, :], ALU.subtract)\
                .then_inc(s["part2"], 1)

    def sync(eng):
        for n, (side, m, b, w, bias) in enumerate(tasks):
            eng.wait_ge(s["part2"], n + 1)
            for j in range(PARTS):
                dst = scratch[side, j, b * NG + 2 * m:b * NG + 2 * m + 2].rearrange("g r s -> (g r) s")
                eng.dma_start(dst, part[j][:, n % SLOTS, :]).then_inc(sent[n % SLOTS], 16)

    n_proj = sum(t[3] is not None for t in tasks)
    return [(sem, 48 * (N // SLOTS)) for sem in sent], {"taken": s["taken"], "sync": sync, "scalar": scalar, "vector": vector, "pool": pool, "tensor": tensor}


def self_attention(sh):
    ins, nm, tn, ps = sh.ins, sh.norm, sh.turn, sh.psum
    before = sh.done
    mark = sh.top
    hT = sh.take("p (c s) -> p c s", DC * TOK, c=DC)
    v_all = sh.take("p (i t n) -> p i t n", NT * D, i=GROUPS, t=BT)
    o_tok = sh.take("p (t i n) -> p t i n", NT * D, i=GROUPS, t=BT)
    xn = o_tok.rearrange("p t i n -> p (t i n)").rearrange("p (t d) -> p t d", t=NT)
    w_all = sh.take("p (k c n) -> p k c n", 4 * DC * D, k=4, c=DC)
    bo = sh.take(None, 2 * D)
    ls, lb = sh.take(None, DC), sh.take(None, DC)
    scratch = sh.nc.dram_tensor("f0_parts", [2, PARTS, GROUPS, G * DH, S], BF16, kind="Internal").ap()
    loaded, kept = sh.sem("f0_loaded"), sh.sem("f0_kept")
    v_done, v_kept = sh.sem("f0_v_done"), sh.sem("f0_v_kept")
    o_done, x_done = sh.sem("f0_o_done"), sh.sem("f0_x_done")
    run, trun, trun2 = nm.use(), tn.use(), tn.use()
    tasks = [(side, m, b, w_all[:, side], None) for b in range(B) for m in range(2) for side in range(2)]
    sent, wp = write_parts(sh, "f0p", tasks, scratch, w_all, hT, before)

    def v_load(eng, i, dst, sem):
        for h in range(G):
            eng.dma_start(dst[:, :, h, 0:DH], v_all[:, bass.ds(i, 1), :, h * DH:(h + 1) * DH]
                          .rearrange("p o t n -> p (o t) n")).then_inc(sem, 16)
    v_load.count = 16 * G

    def out_tok(i, qc, h, heads):
        return lambda t: o_tok[:, qc * 4 + t, bass.ds(i, 1), :].rearrange("p o (h n) -> p (o h) n", h=heads)

    s, OUTS, att = causal_attention(sh, "f0", DH, DH ** -0.5, v_load, out_tok)

    def sync(eng):
        eng.wait_ge(*before)
        eng.dma_start(sh.x_before, sh.x.rearrange("p t d -> p (t d)")).then_inc(kept, 16)
        for k, w in enumerate(("wq", "wk", "wv", "wo")):
            eng.dma_start(w_all[:, k], ins["L0_ffn_" + w].rearrange("(c p) n -> p c n", p=P)).then_inc(loaded, 16)
        for k in range(2):
            eng.dma_start(bo[0:1, k * D:(k + 1) * D], ins["L0_ffn_bo"].rearrange("(o d) -> o d", o=1)).then_inc(loaded, 16)
        eng.dma_start(ls, feature_columns(ins["L0_ffn_ln1_scale"]), allow_slow_non_contiguous=True).then_inc(loaded, 16)
        eng.dma_start(lb, feature_columns(ins["L0_ffn_ln1_shift"]), allow_slow_non_contiguous=True).then_inc(loaded, 16)
        wp["sync"](eng)

        def stacks_wait(eng):
            for slot in sent:
                eng.wait_ge(*slot)
        att["sync"](eng, scratch, stacks_wait, lambda eng: eng.wait_ge(v_kept, 8))

    def pool(eng):
        att["pool"](eng, [before, sh.masks.ready])
        wp["pool"](eng)

    def scalar(eng):
        nm.scalar(eng, run)
        eng.wait_ge(loaded, 16 * 8)
        tn.scalar(eng, hT, trun, scale=ls, bias=lb)
        wp["scalar"](eng)
        att["scalar"](eng)
        tn.scalar(eng, hT, trun2)

    def vector(eng):
        eng.wait_ge(*before)
        nm.vector(eng, lambda t: sh.x[:, t, :], lambda t: xn[:, t, :], run)
        wp["vector"](eng)
        for j in range(8):
            eng.wait_ge(v_done, j + 1)
            dst = v_all[:, (j // 4) * NG:(j // 4 + 1) * NG, 2 * (j % 4):2 * (j % 4) + 2, :].rearrange("p g t n -> p t g n")
            src = ps[:, j, :].rearrange("p (t g n) -> p t g n", t=2, g=NG)
            for t in range(2):
                ins_ = eng.tensor_copy(dst[:, t], src[:, t])
            ins_.then_inc(v_kept, 1)
        att["vector"](eng)
        eng.wait_ge(kept, 16)
        for j in range(NT // 2):
            eng.wait_ge(o_done, j + 1)
            tiles = sh.x[:, 2 * j:2 * j + 2, :]
            eng.tensor_tensor(tiles, tiles, ps[:, j, :].rearrange("p (t d) -> p t d", t=2), ALU.add)\
                .then_inc(x_done, 1)

    def tensor(eng):
        eng.wait_ge(*before)
        tn.tensor(eng, lambda t, c: xn[:, t, c * P:(c + 1) * P], trun, lambda e, t: e.wait_ge(nm.normed, run * NT + t + 1))
        eng.wait_ge(loaded, 16 * 8)
        eng.wait_ge(tn.taken, 8 * trun + 8)
        wp["tensor"](eng)
        eng.wait_ge(wp_taken, len(tasks))
        for t in range(NT):
            for k in range(DC):
                mm = eng.matmul(ps[:, t // 2, (t % 2) * D:(t % 2 + 1) * D], hT[:, k, t * P:(t + 1) * P], w_all[:, 2, k, :],
                                start=k == 0, stop=k == DC - 1)
            if t % 2:
                mm.then_inc(v_done, 1)
        eng.wait_ge(v_kept, 8)
        eng.wait_ge(*sh.masks.ready)
        att["tensor"](eng)
        eng.wait_ge(s["scaled"], 4 + 4 * OUTS * GROUPS)
        tn.tensor(eng, lambda t, c: o_tok[:, t % BT, (t // BT) * NG + 2 * c:(t // BT) * NG + 2 * c + 2, :]
                  .rearrange("p i n -> p (i n)"), trun2,
                  lambda e, t: None)
        eng.wait_ge(tn.taken, 8 * trun2 + 8)
        for t in range(NT):
            dst = ps[:, t // 2, (t % 2) * D:(t % 2 + 1) * D]
            for k in range(DC):
                eng.matmul(dst, hT[:, k, t * P:(t + 1) * P], w_all[:, 3, k, :], start=k == 0, stop=False)
            mm = eng.matmul(dst, sh.ones_row[0:1, :], bo[0:1, 0:D], start=False, stop=True)
            if t % 2:
                mm.then_inc(o_done, 1)

    wp_taken = wp["taken"]
    sh.done = (x_done, NT // 2)
    sh.top = mark
    return {"sync": sync, "pool": pool, "scalar": scalar, "vector": vector, "tensor": tensor}



EXPERTS, HID = 8, 512
HC = HID // P
CH = TOK // BANK


class TopTwo:

    def __init__(self, sh, name, n):
        self.n = n
        self.order = sh.take(None, n)
        self.a = sh.take("p (t e) -> p t e", NT * n, t=NT)
        self.low = sh.take(None, NT)
        self.step = sh.sem(name + "_step")
        self.steps = 0

    def did(self, ins):
        self.steps += 1
        ins.then_inc(self.step, 1)

    def wait(self, eng):
        eng.wait_ge(self.step, self.steps)

    def start(self, eng):
        for e in range(self.n):
            self.did(eng.memset(self.order[:, e:e + 1], float(self.n - e)))
        self.wait(eng)

    def pick(self, eng, values, best, one):
        wide = [P, NT, self.n]
        self.did(eng.tensor_reduce(best, values, AX_X, ALU.max))
        self.wait(eng)
        self.did(eng.tensor_tensor(self.a, values, best.unsqueeze(2).to_broadcast(wide), ALU.is_equal))
        self.wait(eng)
        self.did(eng.tensor_tensor(self.a, self.a, self.order.unsqueeze(1).to_broadcast(wide), ALU.mult))
        self.wait(eng)
        self.did(eng.tensor_reduce(self.low, self.a, AX_X, ALU.max))
        self.wait(eng)
        self.did(eng.tensor_tensor(one, self.a, self.low.unsqueeze(2).to_broadcast(wide), ALU.is_equal))
        self.wait(eng)


def experts(sh):
    ins, nm, tn, ps = sh.ins, sh.norm, sh.turn, sh.psum
    before = sh.done
    mark = sh.top
    acc = sh.take("p (t d) -> p t d", NT * D, t=NT)
    E2 = EXPERTS // 2
    hT = sh.take("p (c s) -> p c s", DC * TOK, c=DC)
    xn = sh.take("p (t d) -> p t d", NT * D, t=NT)
    WN = 2 * DC * HID + HC * D
    RING = 4
    w_raw = xn.rearrange("p t d -> p (t d)")[:, 0:WN]
    w_parts = sh.take_parts("p (r n) -> p r n", 2 * WN, r=2)
    w12 = [v[:, :, 0:2 * DC * HID].rearrange("p r (w c n) -> p r w c n", w=2, c=DC) for v in w_parts]
    w3 = [v[:, :, 2 * DC * HID:].rearrange("p r (c n) -> p r c n", c=HC) for v in w_parts]
    silu = sh.take("p (r s) -> p r s", 2 * BANK, r=2)
    hid_raw = sh.take("p (r s) -> p r s", RING * BANK, r=RING)
    hid = sh.take_parts("p (r m s) -> p r m s", 2 * HC * BANK, r=2, m=HC)
    hT_parts = sh.take_parts("p (c s) -> p c s", DC * TOK, c=DC)
    gw = sh.take("p (c e) -> p c e", DC * EXPERTS, c=DC)
    ls, lb = sh.take(None, DC), sh.take(None, DC)
    gate = sh.take("p (t e) -> p t e", NT * EXPERTS, t=NT)
    one1 = sh.take("p (t e) -> p t e", NT * EXPERTS, t=NT)
    one2 = sh.take("p (t e) -> p t e", NT * EXPERTS, t=NT)
    wt = sh.take("p (t e) -> p t e", NT * EXPERTS, t=NT)
    best, prob = sh.take("p (k t) -> p k t", 2 * NT, k=2), sh.take("p (k t) -> p k t", 2 * NT, k=2)
    top = TopTwo(sh, "moe", EXPERTS)
    s = {k: sh.sem("moe_" + k) for k in ("loaded", "gated", "ratio", "ab_done", "silued", "hid_made", "o_done", "added",
                                      "hT_high", "hT_low", "hid_high", "hid_low", "w_high", "w_low")}
    w_in, acc_in = sh.sem("moe_w_in"), sh.sem("moe_acc_in")
    run, run2, trun = nm.use(), nm.use(), tn.use()
    UNITS_E = CH * HC
    ratio_at = EXPERTS + 1 + 5 + 1 + 5 + 1
    wide = [P, NT, EXPERTS]

    def loop(eng, body):
        with eng.Fori(0, E2 - 1) as pair:
            for r in range(2):
                body(pair * 2 + r, r, True)
        body(EXPERTS - 2, 0, True)
        body(EXPERTS - 1, 1, False)

    def sync(eng):
        eng.wait_ge(*before)
        eng.dma_start(gw, ins["L0_ffn_gate_w"].rearrange("(c p) e -> p c e", p=P)).then_inc(s["loaded"], 16)
        eng.dma_start(ls, feature_columns(ins["L0_ffn_ln2_scale"]), allow_slow_non_contiguous=True).then_inc(s["loaded"], 16)
        eng.dma_start(lb, feature_columns(ins["L0_ffn_ln2_shift"]), allow_slow_non_contiguous=True).then_inc(s["loaded"], 16)

        eng.dma_start(acc.rearrange("p t d -> p (t d)"), sh.x_before).then_inc(acc_in, 16)

        def load(e):
            w12_raw = w_raw[:, 0:2 * DC * HID].rearrange("p (w c n) -> p w c n", w=2, c=DC)
            w3_raw = w_raw[:, 2 * DC * HID:].rearrange("p (c n) -> p c n", c=HC)
            for k in range(2):
                eng.dma_start(w12_raw[:, k], ins[("L0_ffn_w1", "L0_ffn_w2")[k]][bass.ds(e, 1)]
                              .rearrange("o (c p) n -> p (o c) n", p=P)).then_inc(w_in, 16)
            eng.dma_start(w3_raw, ins["L0_ffn_w3"][bass.ds(e, 1)].rearrange("o (c p) n -> p (o c) n", p=P))\
                .then_inc(w_in, 16)

        eng.wait_ge(tn.turned, 8 * trun + 8)
        load(0)
        with eng.Fori(1, EXPERTS) as e:
            eng.wait_ge(s["w_low"], e)
            load(e)

    def scalar(eng):
        nm.scalar(eng, run)
        eng.wait_ge(s["loaded"], 48)
        tn.scalar(eng, hT, trun, scale=ls, bias=lb)
        eng.wait_ge(top.step, ratio_at)
        eng.activation(prob[:, 1], prob[:, 1], ACT.Exp).then_inc(s["ratio"], 1)
        with eng.Fori(0, EXPERTS) as e:
            for u in range(UNITS_E):
                sh.wait_apart(eng, s["ab_done"], e * UNITS_E + u + 1)
                eng.wait_ge(s["hid_made"], e * UNITS_E + u + 1)
                eng.activation(silu[:, u % 2], ps[:, 2 * (u % 2), :], ACT.Silu).then_inc(s["silued"], 1)
        nm.scalar(eng, run2)

    def pool(eng):
        def weights_low(e, r):
            eng.wait_ge(s["w_high"], e + 1)
            low_part(eng, w_parts[1][:, r], w_parts[0][:, r], w_raw).then_inc(s["w_low"], 1)

        def hidden_low(e, c, m):
            eng.wait_ge(s["hid_high"], e * UNITS_E + c * HC + m + 1)
            low_part(eng, hid[1][:, c % 2, m, :], hid[0][:, c % 2, m, :], hid_raw[:, m % RING, :]).then_inc(s["hid_low"], 1)

        eng.wait_ge(*before)
        eng.memset(hid_raw[:, 0, 0:1], 0.0).then_inc(s["hid_low"], RING)
        weights_low(0, 0)

        def body(e, r, more):
            for c in range(CH):
                if c == 2 and more:
                    weights_low(e + 1, 1 - r)
                for m in range(HC):
                    hidden_low(e, c, m)
        loop(eng, body)

    def vector(eng):
        def weights_high(e, r):
            sh.wait_apart(eng, w_in, e * 48 + 48)
            high_part(eng, w_parts[0][:, r], w_raw).then_inc(s["w_high"], 1)

        eng.wait_ge(*before)
        nm.vector(eng, lambda t: sh.x[:, t, :], lambda t: xn[:, t, :], run)
        top.start(eng)
        eng.wait_ge(tn.taken, 8 * trun + 8)
        high_part(eng, hT_parts[0], hT).then_inc(s["hT_high"], 1)
        weights_high(0, 0)
        eng.wait_ge(s["hT_high"], 1)
        low_part(eng, hT_parts[1], hT_parts[0], hT).then_inc(s["hT_low"], 1)
        eng.wait_ge(s["gated"], 1)
        top.did(eng.tensor_copy(gate, ps[:, 0, 0:NT * EXPERTS].rearrange("p (t e) -> p t e", t=NT)))
        top.wait(eng)
        top.pick(eng, gate, best[:, 0], one1)
        top.did(eng.scalar_tensor_tensor(gate, one1, -1e30, gate, ALU.mult, ALU.add))
        top.wait(eng)
        top.pick(eng, gate, best[:, 1], one2)
        top.did(eng.tensor_tensor(prob[:, 1], best[:, 1], best[:, 0], ALU.subtract))
        assert top.steps == ratio_at, top.steps
        eng.wait_ge(acc_in, 16)
        for t in range(NT):
            eng.tensor_tensor(acc[:, t, :], acc[:, t, :], sh.x[:, t, :], ALU.add).then_inc(s["added"], 1)
        eng.wait_ge(s["ratio"], 1)
        top.did(eng.tensor_scalar(prob[:, 0], prob[:, 1], 1.0, None, ALU.add))
        top.wait(eng)
        top.did(eng.reciprocal(prob[:, 0], prob[:, 0]))
        top.wait(eng)
        top.did(eng.tensor_tensor(prob[:, 1], prob[:, 1], prob[:, 0], ALU.mult))
        top.wait(eng)
        top.did(eng.tensor_tensor(one1, one1, prob[:, 0].unsqueeze(2).to_broadcast(wide), ALU.mult))
        top.did(eng.tensor_tensor(one2, one2, prob[:, 1].unsqueeze(2).to_broadcast(wide), ALU.mult))
        top.wait(eng)
        top.did(eng.tensor_tensor(wt, one1, one2, ALU.add))
        top.wait(eng)
        eng.memset(best[:, 0, 0:1], 0.0).then_inc(s["hid_made"], 2)
        eng.wait_ge(s["hid_made"], 2)

        def product(e, c, m):
            u = c * HC + m
            sh.wait_apart(eng, s["silued"], e * UNITS_E + u + 1)
            eng.wait_ge(s["hid_low"], e * UNITS_E + u + 1)
            eng.tensor_tensor(hid_raw[:, m % RING, :], silu[:, u % 2], ps[:, 2 * (u % 2) + 1, :], ALU.mult)\
                .then_inc(s["hid_made"], 1)
            eng.wait_ge(s["hid_made"], e * UNITS_E + u + 3)
            high_part(eng, hid[0][:, c % 2, m, :], hid_raw[:, m % RING, :]).then_inc(s["hid_high"], 1)

        for m in range(2):
            product(0, 0, m)

        def body(e, r, more):
            for c in range(CH):
                product(e, c, 2)
                product(e, c, 3)
                if c == 1 and more:
                    weights_high(e + 1, 1 - r)
                if c + 1 < CH or more:
                    for m in range(2):
                        product(e + (c + 1) // CH, (c + 1) % CH, m)
                sh.wait_apart(eng, s["o_done"], e * CH + c + 1)
                eng.wait_ge(s["added"], e * NT + 4 * c + 4)
                for t in range(4):
                    n = 4 * c + t
                    eng.scalar_tensor_tensor(acc[:, n, :], ps[:, 4 + 2 * (c % 2) + t // 2, (t % 2) * D:(t % 2 + 1) * D],
                                             wt[:, n, bass.ds(e, 1)], acc[:, n, :], ALU.mult, ALU.add)\
                        .then_inc(s["added"], 1)
        loop(eng, body)
        eng.wait_ge(s["added"], (EXPERTS + 1) * NT)
        nm.vector(eng, lambda t: acc[:, t, :], lambda t: sh.x[:, t, :], run2)

    def tensor(eng):
        eng.wait_ge(*before)
        tn.tensor(eng, lambda t, c: xn[:, t, c * P:(c + 1) * P], trun, lambda e, t: e.wait_ge(nm.normed, run * NT + t + 1))
        eng.wait_ge(s["loaded"], 48)
        eng.wait_ge(tn.taken, 8 * trun + 8)
        for t in range(NT):
            for k in range(DC):
                mm = eng.matmul(ps[:, 0, t * EXPERTS:(t + 1) * EXPERTS], hT[:, k, t * P:(t + 1) * P], gw[:, k, :],
                                start=k == 0, stop=k == DC - 1)
        mm.then_inc(s["gated"], 1)
        eng.wait_ge(s["hid_made"], 2)
        eng.wait_ge(s["hT_low"], 1)

        def ab(e, r, c, m):
            u = c * HC + m
            if u == 0:
                eng.wait_ge(s["w_low"], e + 1)
            eng.wait_ge(s["hid_made"], e * UNITS_E + u + 1)
            for w in range(2):
                for k in range(DC):
                    mm = product_of_parts(eng, ps[:, 2 * (u % 2) + w, :],
                                          [v[:, r, w, k, m * P:(m + 1) * P] for v in w12],
                                          [v[:, k, c * BANK:(c + 1) * BANK] for v in hT_parts], k == 0, k == DC - 1)
            mm.then_inc(s["ab_done"], 1)

        for m in range(2):
            ab(0, 0, 0, m)

        def body(e, r, more):
            for c in range(CH):
                ab(e, r, c, 2)
                ab(e, r, c, 3)
                if c + 1 < CH:
                    ab(e, r, c + 1, 0)
                    ab(e, r, c + 1, 1)
                elif more:
                    ab(e + 1, 1 - r, 0, 0)
                    ab(e + 1, 1 - r, 0, 1)
                eng.wait_ge(s["hid_low"], e * UNITS_E + 4 * c + 4 + RING)
                if c >= 2 or not isinstance(e, int) or e > 0:
                    eng.wait_ge(s["added"], e * NT + 4 * c - 4 + NT)
                for t in range(4):
                    for m in range(HC):
                        mm = product_of_parts(eng, ps[:, 4 + 2 * (c % 2) + t // 2, (t % 2) * D:(t % 2 + 1) * D],
                                              [v[:, c % 2, m, t * P:(t + 1) * P] for v in hid],
                                              [v[:, r, m, :] for v in w3], m == 0, m == HC - 1)
                mm.then_inc(s["o_done"], 1)
        loop(eng, body)

    sh.done = (nm.normed, run2 * NT + NT)
    sh.top = mark
    return {"sync": sync, "pool": pool, "scalar": scalar, "vector": vector, "tensor": tensor}


CK = 77


class Context:

    HC8 = P // DH

    def __init__(self, sh):
        self.sh = sh
        self.raw = sh.take("p (b d) -> p b d", B * D, b=B)
        self.rows = sh.take("p (c s) -> p c s", DC * B * CK, c=DC)
        self.of_head = sh.take(None, self.HC8)
        self.s = {k: sh.sem("ctx_" + k) for k in ("loaded", "turned", "ready", "heads")}
        self.ready = (self.s["ready"], 1)

    def stage(self):
        s, sh = self.s, self.sh

        def sync(eng):
            eng.wait_ge(*self.before)
            eng.dma_start(self.raw[0:CK], sh.ins["ctx_1024"].rearrange("b k d -> k b d")).then_inc(s["loaded"], 16)

        def pool(eng):
            eng.wait_ge(*self.before)
            eng.memset(self.of_head, 1.0).then_inc(s["heads"], 1)
            eng.wait_ge(s["heads"], 1)
            eng.affine_select(out=self.of_head, in_=self.of_head, compare_op=ALU.is_ge, fill=0.0, base=0,
                              pattern=[[-DH, self.HC8]], channel_multiplier=1).then_inc(s["heads"], 1)
            eng.wait_ge(s["heads"], 2)
            eng.affine_select(out=self.of_head, in_=self.of_head, compare_op=ALU.is_ge, fill=0.0, base=DH - 1,
                              pattern=[[DH, self.HC8]], channel_multiplier=-1).then_inc(s["heads"], 1)

        def tensor(eng):
            eng.wait_ge(*self.before)
            eng.wait_ge(*sh.constants)
            eng.wait_ge(s["loaded"], 16)
            for c in range(DC):
                for b in range(B):
                    at = (c * B + b) * CK
                    mm = eng.transpose(sh.psum[:, 0, at:at + CK], self.raw[0:CK, b, c * P:(c + 1) * P], sh.ident[0:CK, 0:CK])
            mm.then_inc(s["turned"], 1)

        def scalar(eng):
            eng.wait_ge(s["turned"], 1)
            eng.activation(self.rows.rearrange("p c s -> p (c s)"), sh.psum[:, 0, 0:DC * B * CK], ACT.Copy).then_inc(s["ready"], 1)

        self.before = sh.done
        sh.done = self.ready
        return {"sync": sync, "pool": pool, "tensor": tensor, "scalar": scalar}


def query_softmax_attention(sh):
    ins, nm, tn, ps, cx = sh.ins, sh.norm, sh.turn, sh.psum, sh.context
    before = sh.done
    mark = sh.top
    hT = sh.take("p (c s) -> p c s", DC * TOK, c=DC)
    qT = sh.take("p (c s) -> p c s", DC * TOK, c=DC)
    o = sh.take("p (t d) -> p t d", NT * D, t=NT)
    names = ("Wq", "Wk1", "Wk2", "Wv1", "Wv2", "Wo")
    w = {n: sh.take("p (c n) -> p c n", DC * D, c=DC) for n in names}
    rows = {n: sh.take(None, D) for n in ("bq", "bv1", "bv2", "bo")}
    cols = {n: sh.take(None, DC) for n in ("bq", "bk1", "bk2")}
    affine = {n: sh.take(None, D) for n in ("g0", "beta0", "g1", "beta1")}
    kT = sh.take("p (j c s) -> p j c s", 2 * DC * B * CK, j=2, c=DC)
    kh = sh.take("p (j c b h k) -> p j c b h k", 2 * DC * B * 8 * CK, j=2, c=DC, b=B, h=8)
    v = sh.take("p (j b h n) -> p j b h n", 2 * B * D, j=2, b=B, h=HEADS)
    vs = sh.take("p (r n) -> p r n", 3 * DH, r=3)
    ex = sh.take("p (r s) -> p r s", 3 * S, r=3)
    mx = sh.take("p (r k) -> p r k", 3 * 4, r=3)
    relu = sh.take("p (t d) -> p t d", NT * D, t=NT)
    s = {k: sh.sem("qx_" + k) for k in (
        "loaded", "proj", "moved", "k_ready", "v_proj", "v_ready", "s_done", "max", "exped", "v_scaled",
        "q_done", "av_done", "o_taken", "f_done", "relued", "step")}
    runs, t1, t2 = [nm.use() for _ in range(3)], tn.use(), tn.use()
    NLOAD = len(names) + len(rows) + len(cols) + len(affine)
    UNITS_X = [(b, h, j) for b in range(B) for h in range(HEADS) for j in range(2)]
    PER_B = 2 * HEADS

    def sync(eng):
        eng.wait_ge(*before)
        for n in names:
            eng.dma_start(w[n], ins["L0_xattn_" + n].rearrange("(c p) n -> p c n", p=P)).then_inc(s["loaded"], 16)
        for n, dst in rows.items():
            eng.dma_start(dst[0:1, :], ins["L0_xattn_" + n].rearrange("(o d) -> o d", o=1)).then_inc(s["loaded"], 16)
        for n, dst in cols.items():
            eng.dma_start(dst, feature_columns(ins["L0_xattn_" + n]), allow_slow_non_contiguous=True).then_inc(s["loaded"], 16)
        for n, dst in affine.items():
            eng.dma_start(dst, on_all_partitions(ins["L0_xattn_" + n])).then_inc(s["loaded"], 16)

    def scalar(eng):
        tn.scalar(eng, hT, t1)
        eng.wait_ge(s["loaded"], 16 * NLOAD)
        for n in range(4):
            j, m = n // 2, n % 2
            eng.wait_ge(s["proj"], n + 1)
            eng.activation(kT[:, j, m, :], ps[:, n, 0:B * CK], ACT.Identity, bias=cols[("bk1", "bk2")[j]][:, m:m + 1])\
                .then_inc(s["moved"], 1)
        for n in range(8):
            m, c = n // 4, n % 4
            eng.wait_ge(s["proj"], 4 + n + 1)
            eng.activation(qT[:, m, c * BANK:(c + 1) * BANK], ps[:, n, :], ACT.Identity, bias=cols["bq"][:, m:m + 1])\
                .then_inc(s["moved"], 1)
        for u, (b, h, j) in enumerate(UNITS_X):
            eng.wait_ge(s["max"], u + 1)
            if u >= 3:
                eng.wait_ge(s["av_done"], u - 2)
            eng.activation(ex[0:CK, u % 3, :], ps[0:CK, 2 * (u % 2):2 * (u % 2) + 2, :].rearrange("p b s -> p (b s)"),
                           ACT.Exp, bias=mx[0:CK, u % 3, 0:1], scale=1 / 16,
                           accum_out=mx[0:CK, u % 3, 1:2]).then_inc(s["exped"], 1)
            if u % PER_B == PER_B - 1:
                eng.wait_ge(s["av_done"], u + 1)
                for n in range(4):
                    eng.activation(o[:, b * BT + 2 * n:b * BT + 2 * n + 2, :].rearrange("p t d -> p (t d)"), ps[:, 4 + n, :],
                                   ACT.Copy).then_inc(s["o_taken"], 1)
        nm.scalar(eng, runs[0])
        tn.scalar(eng, hT, t2)
        for j in range(NT // 2):
            eng.wait_ge(s["f_done"], j + 1)
            eng.activation(relu[:, 2 * j:2 * j + 2, :].rearrange("p t d -> p (t d)"), ps[:, j, :], ACT.Relu).then_inc(s["relued"], 1)
        nm.scalar(eng, runs[1])
        nm.scalar(eng, runs[2])

    def vector(eng):
        steps = [0]

        def did(ins_):
            steps[0] += 1
            ins_.then_inc(s["step"], 1)
            eng.wait_ge(s["step"], steps[0])

        eng.wait_ge(cx.s["heads"], 3)
        for n in range(4):
            j, m = n // 2, n % 2
            eng.wait_ge(s["moved"], n + 1)
            for b in range(B):
                shape = [P, 8, CK]
                eng.tensor_tensor(kh[:, j, m, b], kT[:, j, m, b * CK:(b + 1) * CK].unsqueeze(1).to_broadcast(shape),
                                  cx.of_head.unsqueeze(2).to_broadcast(shape), ALU.mult).then_inc(s["k_ready"], 1)
        for n in range(4):
            eng.wait_ge(s["v_proj"], n + 1)
            eng.tensor_copy(v[0:CK, n // 2, n % 2].rearrange("p h n -> p (h n)"), ps[0:CK, 4 + n, 0:D]).then_inc(s["v_ready"], 1)
        eng.wait_ge(s["v_ready"], 4)

        def scale_v(u):
            b, h, j = UNITS_X[u]
            eng.wait_ge(s["exped"], u + 1)
            did(eng.reciprocal(mx[0:CK, u % 3, 2:3], mx[0:CK, u % 3, 1:2]))
            if u >= 3:
                eng.wait_ge(s["av_done"], u - 2)
            eng.tensor_scalar(vs[0:CK, u % 3, :], v[0:CK, j, b, h, :], mx[0:CK, u % 3, 2:3], None, ALU.mult).then_inc(s["v_scaled"], 1)

        for u, (b, h, j) in enumerate(UNITS_X):
            eng.wait_ge(s["s_done"], u + 1)
            if u >= 3:
                eng.wait_ge(s["exped"], u - 2)
            did(eng.tensor_reduce(mx[0:CK, u % 3, 3:4], ps[0:CK, 2 * (u % 2):2 * (u % 2) + 2, :], mybir.AxisListType.XY, ALU.max))
            eng.tensor_scalar(mx[0:CK, u % 3, 0:1], mx[0:CK, u % 3, 3:4], -1 / 16, None, ALU.mult).then_inc(s["max"], 1)
            if u:
                scale_v(u - 1)
        scale_v(len(UNITS_X) - 1)

        def tile(t):
            return o[:, t, :]

        def all_tokens(param, op):
            did(eng.tensor_tensor(o, o, affine[param].unsqueeze(1).to_broadcast([P, NT, D]), op))

        eng.wait_ge(s["o_taken"], 8)
        nm.vector(eng, tile, tile, runs[0])
        eng.wait_ge(nm.normed, (runs[0] + 1) * NT)
        all_tokens("g0", ALU.mult)
        all_tokens("beta0", ALU.add)
        for j in range(NT // 2):
            eng.wait_ge(s["relued"], j + 1)
            ins_ = eng.tensor_tensor(o[:, 2 * j:2 * j + 2, :], o[:, 2 * j:2 * j + 2, :], relu[:, 2 * j:2 * j + 2, :], ALU.add)
        did(ins_)
        nm.vector(eng, tile, tile, runs[1])
        eng.wait_ge(nm.normed, (runs[1] + 1) * NT)
        all_tokens("g1", ALU.mult)
        all_tokens("beta1", ALU.add)
        did(eng.tensor_tensor(o, o, sh.x, ALU.add))
        nm.vector(eng, tile, lambda t: sh.x[:, t, :], runs[2])
    AFFINE0 = 2 * len(UNITS_X) + 2

    def tensor(eng):
        eng.wait_ge(*before)
        tn.tensor(eng, lambda t, c: sh.x[:, t, c * P:(c + 1) * P], t1, lambda e, t: None)
        eng.wait_ge(s["loaded"], 16 * NLOAD)
        eng.wait_ge(tn.taken, 8 * t1 + 8)
        for n in range(4):
            j, m = n // 2, n % 2
            for k in range(DC):
                mm = eng.matmul(ps[:, n, 0:B * CK], w[("Wk1", "Wk2")[j]][:, k, m * P:(m + 1) * P], cx.rows[:, k, :],
                                start=k == 0, stop=k == DC - 1)
            mm.then_inc(s["proj"], 1)

        def q_rows(n):
            m, c = n // 4, n % 4
            for k in range(DC):
                mm = eng.matmul(ps[:, n, :], w["Wq"][:, k, m * P:(m + 1) * P], hT[:, k, c * BANK:(c + 1) * BANK],
                                start=k == 0, stop=k == DC - 1)
            mm.then_inc(s["proj"], 1)

        for n in range(4):
            eng.wait_ge(s["moved"], n + 1)
            q_rows(n)
        for n in range(4):
            j, b = n // 2, n % 2
            for k in range(DC):
                eng.matmul(ps[0:CK, 4 + n, 0:D], kT[:, j, k, b * CK:(b + 1) * CK], w[("Wv1", "Wv2")[j]][:, k, :],
                           start=k == 0, stop=False)
            eng.matmul(ps[0:CK, 4 + n, 0:D], sh.ones_row[0:1, 0:CK], rows[("bv1", "bv2")[j]][0:1, :],
                       start=False, stop=True).then_inc(s["v_proj"], 1)
        for n in range(4, 8):
            eng.wait_ge(s["v_ready"], n - 3)
            q_rows(n)
        eng.wait_ge(s["moved"], 12)
        eng.wait_ge(s["k_ready"], 8)

        def scores(u):
            b, h, j = UNITS_X[u]
            if u >= 2:
                eng.wait_ge(s["exped"], u - 1)
            for c in range(2):
                mm = eng.matmul(ps[0:CK, 2 * (u % 2) + c, :], kh[:, j, h // 8, b, h % 8, :],
                                qT[:, h // 8, b * S + c * BANK:b * S + (c + 1) * BANK], start=True, stop=True)
            mm.then_inc(s["s_done"], 1)

        def queries(b):
            eng.wait_ge(s["v_ready"], 4)
            if b:
                eng.wait_ge(s["o_taken"], 4)
            for t in range(BT):
                dst = ps[:, 4 + t // 2, (t % 2) * D:(t % 2 + 1) * D]
                for k in range(DC):
                    eng.matmul(dst, hT[:, k, (b * BT + t) * P:(b * BT + t + 1) * P], w["Wq"][:, k, :],
                               start=k == 0 and t % 2 == 0, stop=False, skip_group_check=True)
                eng.matmul(dst, sh.ones_row[0:1, :], rows["bq"][0:1, :], start=False, stop=False, skip_group_check=True)

        def products(u):
            b, h, j = UNITS_X[u]
            eng.wait_ge(s["exped"], u + 1)
            eng.wait_ge(s["v_scaled"], u + 1)
            for t in range(BT):
                mm = eng.matmul(ps[:, 4 + t // 2, (t % 2) * D + h * DH:(t % 2) * D + (h + 1) * DH],
                                ex[0:CK, u % 3, t * P:(t + 1) * P], vs[0:CK, u % 3, :], start=False, stop=h == HEADS - 1 and j == 1,
                                skip_group_check=True)
            mm.then_inc(s["av_done"], 1)

        scores(0)
        scores(1)
        for u, (b, h, j) in enumerate(UNITS_X):
            if u + 2 < len(UNITS_X):
                scores(u + 2)
            if h == 0 and j == 0:
                queries(b)
            products(u)
        eng.wait_ge(s["step"], AFFINE0)
        tn.tensor(eng, lambda t, c: o[:, t, c * P:(c + 1) * P], t2, lambda e, t: None)
        eng.wait_ge(tn.taken, 8 * t2 + 8)
        for t in range(NT):
            dst = ps[:, t // 2, (t % 2) * D:(t % 2 + 1) * D]
            for k in range(DC):
                eng.matmul(dst, hT[:, k, t * P:(t + 1) * P], w["Wo"][:, k, :], start=k == 0, stop=False)
            mm = eng.matmul(dst, sh.ones_row[0:1, :], rows["bo"][0:1, :], start=False, stop=True)
            if t % 2:
                mm.then_inc(s["f_done"], 1)

    sh.done = (nm.normed, runs[2] * NT + NT)
    sh.top = mark
    return {"sync": sync, "scalar": scalar, "vector": vector, "tensor": tensor}


def masked_cross_attention(sh):
    ins, nm, tn, ps, cx = sh.ins, sh.norm, sh.turn, sh.psum, sh.context
    before = sh.done
    mark = sh.top
    hT = sh.take("p (c s) -> p c s", DC * TOK, c=DC)
    o = sh.take("p (t d) -> p t d", NT * D, t=NT)
    names = ("W_Q", "W_K", "W_V", "W_O")
    w = {n: sh.take("p (c n) -> p c n", DC * D, c=DC) for n in names}
    mask_i = sh.take("p (t k) -> p t k", NT * CK, t=NT).bitcast(I32)
    mask = sh.take("p (t k) -> p t k", NT * CK, t=NT)
    kT = sh.take("p (c s) -> p c s", DC * B * CK, c=DC)
    kh = sh.take("p (b c h k) -> p b c h k", B * DC * 8 * CK, c=DC, b=B, h=8)
    VN = DH + 1
    v = sh.take("p (b h n) -> p b h n", B * HEADS * VN, b=B, h=HEADS)
    qT = sh.take("p (r c s) -> p r c s", 2 * DC * P, r=2, c=DC)
    sc = sh.take("p (r h k) -> p r h k", 2 * HEADS * CK, r=2, h=HEADS)
    mx = sh.take("p (r h) -> p r h", 2 * HEADS, r=2)
    pT = sh.take("p (r h s) -> p r h s", 2 * 8 * P, r=2, h=8)
    rc = sh.take("p (r h) -> p r h", 2 * HEADS, r=2)
    s = {k: sh.sem("kx_" + k) for k in (
        "loaded", "mask_ready", "proj", "moved", "k_ready", "v_proj", "v_ready", "q_done", "q_moved", "s_done",
        "masked", "less", "exped", "turned", "taken", "av_done", "recip", "scaled", "o_done", "x_done")}
    run, t1, t2 = nm.use(), tn.use(), tn.use()
    BAR = -1e29

    def sync(eng):
        eng.wait_ge(*before)
        for n in names:
            eng.dma_start(w[n], ins["L1_xattn_" + n].rearrange("(c p) n -> p c n", p=P)).then_inc(s["loaded"], 16)
        eng.dma_start(mask_i, ins["mask_Bx1xSxS2_ik0"].rearrange("b o (t p) k -> p (b o t) k", p=P)).then_inc(s["loaded"], 16)

    def tiles(eng, body):
        with eng.Fori(0, NT // 2 - 1) as pair:
            for r in range(2):
                body(pair * 2 + r, r, True)
        body(NT - 2, 0, True)
        body(NT - 1, 1, False)

    def scalar(eng):
        tn.scalar(eng, hT, t1)
        for m in range(DC):
            eng.wait_ge(s["proj"], m + 1)
            eng.activation(kT[:, m, :], ps[:, m, 0:B * CK], ACT.Copy).then_inc(s["moved"], 1)

        def take_q(t, r):
            sh.wait_apart(eng, s["q_done"], t + 1)
            eng.activation(qT[:, r].rearrange("p c s -> p (c s)"), ps[:, 7, 0:DC * P], ACT.Copy, scale=0.25).then_inc(s["q_moved"], 1)

        def take_turned(t, half):
            sh.wait_apart(eng, s["turned"], t * 2 + half + 1)
            eng.activation(pT[0:CK, half].rearrange("p h s -> p (h s)"), ps[0:CK, 4:6, :].rearrange("p b s -> p (b s)"),
                           ACT.Copy).then_inc(s["taken"], 1)

        def exponentials(t, r):
            sh.wait_apart(eng, s["less"], t + 1)
            eng.activation(sc[:, r], sc[:, r], ACT.Exp).then_inc(s["exped"], 1)

        take_q(0, 0)
        exponentials(0, 0)

        def body(t, r, more):
            if more:
                take_q(t + 1, 1 - r)
            take_turned(t, 0)
            take_turned(t, 1)
            if more:
                exponentials(t + 1, 1 - r)
        tiles(eng, body)
        tn.scalar(eng, hT, t2)
        nm.scalar(eng, run)

    def vector(eng):
        eng.wait_ge(s["loaded"], 80)
        eng.tensor_copy(mask, mask_i).then_inc(s["mask_ready"], 1)
        eng.wait_ge(s["mask_ready"], 1)
        eng.tensor_scalar(mask, mask, 0.0, -1e30, ALU.is_equal, ALU.mult).then_inc(s["mask_ready"], 1)
        eng.memset(v, 1.0).then_inc(s["mask_ready"], 1)
        eng.wait_ge(s["mask_ready"], 3)
        eng.wait_ge(cx.s["heads"], 3)
        for m in range(DC):
            eng.wait_ge(s["moved"], m + 1)
            for b in range(B):
                shape = [P, 8, CK]
                eng.tensor_tensor(kh[:, b, m], kT[:, m, b * CK:(b + 1) * CK].unsqueeze(1).to_broadcast(shape),
                                  cx.of_head.unsqueeze(2).to_broadcast(shape), ALU.mult).then_inc(s["k_ready"], 1)
        for b in range(B):
            eng.wait_ge(s["v_proj"], b + 1)
            eng.tensor_copy(v[0:CK, b, :, 0:DH], ps[0:CK, 2 + b, 0:D].rearrange("p (h n) -> p h n", h=HEADS)).then_inc(s["v_ready"], 1)

        def scores(t, r):
            sh.wait_apart(eng, s["s_done"], t + 1)
            quarters = [P, 4, 4, CK]
            eng.tensor_tensor(sc[:, r].rearrange("p (a h) k -> p a h k", a=4),
                              ps[:, 0:4, 0:4 * CK].rearrange("p a (h k) -> p a h k", h=4),
                              mask[:, bass.ds(t, 1), :].unsqueeze(1).to_broadcast(quarters), ALU.add).then_inc(s["masked"], 1)
            eng.wait_ge(s["masked"], t * 3 + 1)
            eng.tensor_reduce(mx[:, r], sc[:, r], AX_X, ALU.max).then_inc(s["masked"], 1)
            eng.wait_ge(s["masked"], t * 3 + 2)
            eng.tensor_scalar(mx[:, r], mx[:, r], BAR, None, ALU.max).then_inc(s["masked"], 1)
            eng.wait_ge(s["masked"], t * 3 + 3)
            eng.tensor_tensor(sc[:, r], sc[:, r], mx[:, r].unsqueeze(2).to_broadcast([P, HEADS, CK]), ALU.subtract)\
                .then_inc(s["less"], 1)

        eng.memset(rc[:, 0, 0:1], 0.0).then_inc(s["scaled"], 1)
        eng.wait_ge(s["scaled"], 1)
        scores(0, 0)

        def body(t, r, more):
            if more:
                scores(t + 1, 1 - r)
            sh.wait_apart(eng, s["av_done"], t + 1)
            src = ps[:, 6, 0:HEADS * VN].rearrange("p (h n) -> p h n", h=HEADS)
            eng.tensor_scalar(rc[:, r], src[:, :, DH], 1e-30, None, ALU.max).then_inc(s["recip"], 1)
            eng.wait_ge(s["recip"], t * 2 + 1)
            eng.reciprocal(rc[:, r], rc[:, r]).then_inc(s["recip"], 1)
            eng.wait_ge(s["recip"], t * 2 + 2)
            eng.tensor_tensor(o[:, bass.ds(t, 1), :].rearrange("p o (h n) -> p (o h) n", h=HEADS), src[:, :, 0:DH],
                              rc[:, r].unsqueeze(2).to_broadcast([P, HEADS, DH]), ALU.mult).then_inc(s["scaled"], 1)
        tiles(eng, body)
        for j in range(NT // 2):
            eng.wait_ge(s["o_done"], j + 1)
            pair = sh.x[:, 2 * j:2 * j + 2, :]
            eng.tensor_tensor(pair, pair, ps[:, j, :].rearrange("p (t d) -> p t d", t=2), ALU.add).then_inc(s["x_done"], 1)
        eng.wait_ge(s["x_done"], NT // 2)
        nm.vector(eng, lambda t: sh.x[:, t, :], lambda t: sh.x[:, t, :], run)

    def tensor(eng):
        eng.wait_ge(*before)
        tn.tensor(eng, lambda t, c: sh.x[:, t, c * P:(c + 1) * P], t1, lambda e, t: None)
        eng.wait_ge(s["loaded"], 80)
        eng.wait_ge(tn.taken, 8 * t1 + 8)
        for m in range(DC):
            for k in range(DC):
                mm = eng.matmul(ps[:, m, 0:B * CK], w["W_K"][:, k, m * P:(m + 1) * P], cx.rows[:, k, :],
                                start=k == 0, stop=k == DC - 1)
            mm.then_inc(s["proj"], 1)
        for b in range(B):
            for k in range(DC):
                mm = eng.matmul(ps[0:CK, 2 + b, 0:D], cx.rows[:, k, b * CK:(b + 1) * CK], w["W_V"][:, k, :],
                                start=k == 0, stop=k == DC - 1)
            mm.then_inc(s["v_proj"], 1)
        eng.wait_ge(s["k_ready"], 4)
        eng.wait_ge(s["v_ready"], 2)

        def queries(t):
            for m in range(DC):
                for k in range(DC):
                    mm = eng.matmul(ps[:, 7, m * P:(m + 1) * P], w["W_Q"][:, k, m * P:(m + 1) * P],
                                    hT[:, k, bass.ds(t * P, P)], start=k == 0, stop=k == DC - 1)
            mm.then_inc(s["q_done"], 1)

        def scores(t, r, b):
            eng.wait_ge(s["q_moved"], t + 1)
            if not isinstance(t, int) or t > 0:
                eng.wait_ge(s["masked"], t * 3 - 2)
            for a in range(4):
                mm = eng.matmul(ps[:, a, 0:4 * CK], qT[:, r, a // 2, :], kh_of(b, a), start=True, stop=True)
            mm.then_inc(s["s_done"], 1)

        def kh_of(b, a):
            one = kh[:, bass.ds(b, 1), a // 2, 4 * (a % 2):4 * (a % 2) + 4, :]
            return one.rearrange("p o h k -> p (o h k)")

        def turn(t, r, half):
            if half == 0:
                eng.wait_ge(s["exped"], t + 1)
            if half:
                eng.wait_ge(s["taken"], t * 2 + 1)
            for h in range(8):
                mm = eng.transpose(ps[0:CK, 4 + h // 4, (h % 4) * P:(h % 4 + 1) * P], sc[:, r, 8 * half + h, :], sh.ident)
            mm.then_inc(s["turned"], 1)

        def products(t, b):
            for half in range(2):
                eng.wait_ge(s["taken"], t * 2 + half + 1)
                if half == 0:
                    eng.wait_ge(s["scaled"], t + 1)
                for h in range(8):
                    n = 8 * half + h
                    mm = eng.matmul(ps[:, 6, n * VN:(n + 1) * VN], pT[0:CK, half, h, :],
                                    v[0:CK, bass.ds(b, 1), n, :].rearrange("p o n -> p (o n)"), start=True, stop=True)
            mm.then_inc(s["av_done"], 1)

        queries(0)
        scores(0, 0, 0)

        def tile(t, r, b, next_b, more):
            if more:
                queries(t + 1)
            turn(t, r, 0)
            if more:
                scores(t + 1, 1 - r, next_b)
            turn(t, r, 1)
            products(t, b)

        for b in range(B):
            with eng.Fori(b * BT // 2, (b + 1) * BT // 2 - 1) as pair:
                for r in range(2):
                    tile(pair * 2 + r, r, b, b, True)
            last = (b + 1) * BT - 1
            tile(last - 1, 0, b, b, True)
            tile(last, 1, b, min(b + 1, B - 1), last < NT - 1)
        eng.wait_ge(s["scaled"], NT + 1)
        tn.tensor(eng, lambda t, c: o[:, t, c * P:(c + 1) * P], t2, lambda e, t: None)
        eng.wait_ge(tn.taken, 8 * t2 + 8)
        for t in range(NT):
            dst = ps[:, t // 2, (t % 2) * D:(t % 2 + 1) * D]
            for k in range(DC):
                mm = eng.matmul(dst, hT[:, k, t * P:(t + 1) * P], w["W_O"][:, k, :], start=k == 0, stop=k == DC - 1)
            if t % 2:
                mm.then_inc(s["o_done"], 1)

    sh.done = (nm.normed, run * NT + NT)
    sh.top = mark
    return {"sync": sync, "scalar": scalar, "vector": vector, "tensor": tensor}


def gelu_attention(sh):
    ins, nm, tn, ps = sh.ins, sh.norm, sh.turn, sh.psum
    before = sh.done
    mark = sh.top
    WIDE = ins["L1_attn_Wv"].shape[1]
    DV = WIDE // HEADS
    GW = G * DV
    FC = WIDE // P
    o_tok = sh.take("p (t i n) -> p t i n", NT * WIDE, i=GROUPS, t=BT)
    early = o_tok.rearrange("p t i n -> p (t i n)")
    hT = early[:, 0:DC * TOK].rearrange("p (c s) -> p c s", c=DC)
    at = DC * TOK
    wk = early[:, at:at + DC * D].rearrange("p (c n) -> p c n", c=DC)
    at += DC * D
    wv = early[:, at:at + DC * WIDE].rearrange("p (c n) -> p c n", c=DC)
    at += DC * WIDE
    bv = early[:, at:at + WIDE]
    at += WIDE
    bk = early[:, at:at + DC]
    at += DC
    v_out = early[:, at:at + 4 * WIDE].rearrange("p (r n) -> p r n", r=4)
    assert at + 4 * WIDE <= NT * WIDE
    inner = sh.top
    parts_scratch = sh.nc.dram_tensor("l1_parts", [2, PARTS, GROUPS, G * DH, S], BF16, kind="Internal").ap()
    v_scratch = sh.nc.dram_tensor("l1_v", [GROUPS, S, GW], F32, kind="Internal").ap()
    loaded, wf_in = sh.sem("l1_loaded"), sh.sem("l1_wf_in")
    v_done, v_kept = sh.sem("l1_v_done"), sh.sem("l1_v_kept")
    v_sent = [sh.sem(f"l1_v_sent{r}") for r in range(4)]
    o_turned, o_done, x_done, gelu_done = (sh.sem("l1_" + k) for k in ("o_turned", "o_done", "x_done", "gelu_done"))
    run, trun = nm.use(), tn.use()
    tasks = [(0, m, b, None, None) for b in range(B) for m in range(2)] + \
            [(1, m, b, wk, bk) for b in range(B) for m in range(2)]
    sent, wp = write_parts(sh, "l1p", tasks, parts_scratch, None, hT, before)

    def v_load(eng, i, dst, sem):
        for h in range(G):
            eng.dma_start(dst[:, :, h, 0:DV], v_scratch[bass.ds(i, 1), :, h * DV:(h + 1) * DV]
                          .rearrange("o (t p) n -> p (o t) n", p=P)).then_inc(sem, 16)
    v_load.count = 16 * G

    def out_tok(i, qc, h, heads):
        return lambda t: o_tok[:, qc * 4 + t, bass.ds(i, 1), h * DV:(h + 1) * DV]

    s, OUTS, att = causal_attention(sh, "l1", DV, 1.0, v_load, out_tok)
    sh.top = inner
    wf = sh.take("p (c n) -> p c n", FC * D, c=FC)
    bf = sh.take(None, D)
    oT = sh.take("p (r f s) -> p r f s", 2 * FC * P, r=2, f=FC)

    def sync(eng):
        eng.wait_ge(*before)
        eng.dma_start(wk, ins["L1_attn_Wk"].rearrange("(c p) n -> p c n", p=P)).then_inc(loaded, 16)
        eng.dma_start(wv, ins["L1_attn_Wv"].rearrange("(c p) n -> p c n", p=P)).then_inc(loaded, 16)
        eng.dma_start(bk, feature_columns(ins["L1_attn_bk"]), allow_slow_non_contiguous=True).then_inc(loaded, 16)
        eng.dma_start(bv, on_all_partitions(ins["L1_attn_bv"])).then_inc(loaded, 16)
        wp["sync"](eng)

        def stacks_wait(eng):
            for slot in sent:
                eng.wait_ge(*slot)

        def send_v(eng):
            for t in range(NT):
                eng.wait_ge(v_kept, 2 * t + 2)
                dst = v_scratch[t // BT * NG:(t // BT + 1) * NG, t % BT * P:(t % BT + 1) * P].rearrange("g p n -> p g n")
                eng.dma_start(dst, v_out[:, t % 4].rearrange("p (g n) -> p g n", g=NG)).then_inc(v_sent[t % 4], 16)
            for sem in v_sent:
                eng.wait_ge(sem, 16 * NT // 4)
        att["sync"](eng, parts_scratch, stacks_wait, send_v)
        eng.wait_ge(s["scaled"], 4 + 4 * OUTS * GROUPS)
        eng.dma_start(wf, ins["L1_attn_Wf"].rearrange("(c p) n -> p c n", p=P)).then_inc(wf_in, 16)
        eng.dma_start(bf[0:1, :], ins["L1_attn_bf"].rearrange("(o d) -> o d", o=1)).then_inc(wf_in, 16)

    def pool(eng):
        att["pool"](eng, [before, sh.masks.ready])
        wp["pool"](eng)

    def scalar(eng):
        tn.scalar(eng, hT, trun)
        eng.wait_ge(tn.taken, 8 * trun + 8)
        eng.wait_ge(loaded, 64)
        wp["scalar"](eng)
        att["scalar"](eng)
        for t in range(NT):
            eng.wait_ge(o_turned, t + 1)
            if t >= 2:
                eng.wait_ge(o_done, t - 1)
            eng.activation(oT[:, t % 2].rearrange("p f s -> p (f s)"),
                           ps[:, 2 * (t % 2):2 * (t % 2) + 2, :].rearrange("p b s -> p (b s)"), ACT.Gelu).then_inc(gelu_done, 1)
        nm.scalar(eng, run)

    def vector(eng):
        wp["vector"](eng)
        for j in range(2 * NT):
            t, half = j // 2, j % 2
            eng.wait_ge(v_done, j + 1)
            if t >= 4:
                eng.wait_ge(v_sent[t % 4], 16 * (t // 4))
            cols = slice(half * BANK, (half + 1) * BANK)
            eng.tensor_tensor(v_out[:, t % 4, cols], ps[:, j % 8, :], bv[:, cols], ALU.add).then_inc(v_kept, 1)
        for sem in v_sent:
            eng.wait_ge(sem, 16 * NT // 4)
        att["vector"](eng)
        for t in range(NT):
            eng.wait_ge(o_done, t + 1)
            tile = sh.x[:, t, :]
            eng.scalar_tensor_tensor(tile, tile, 2.0, ps[:, 4 + t % 2, 0:D], ALU.mult, ALU.add).then_inc(x_done, 1)
        eng.wait_ge(x_done, NT)
        nm.vector(eng, lambda t: sh.x[:, t, :], lambda t: sh.x[:, t, :], run)

    def tensor(eng):
        eng.wait_ge(*before)
        tn.tensor(eng, lambda t, c: sh.x[:, t, c * P:(c + 1) * P], trun, lambda e, t: None)
        eng.wait_ge(loaded, 64)
        eng.wait_ge(tn.taken, 8 * trun + 8)
        wp["tensor"](eng)
        eng.wait_ge(wp["taken"], len(tasks))
        for j in range(2 * NT):
            t, half = j // 2, j % 2
            if j >= 8:
                eng.wait_ge(v_kept, j - 7)
            for k in range(DC):
                mm = eng.matmul(ps[:, j % 8, :], hT[:, k, t * P:(t + 1) * P], wv[:, k, half * BANK:(half + 1) * BANK],
                                start=k == 0, stop=k == DC - 1)
            mm.then_inc(v_done, 1)
        eng.wait_ge(v_kept, 2 * NT)
        eng.wait_ge(*sh.masks.ready)
        att["tensor"](eng)
        eng.wait_ge(s["scaled"], 4 + 4 * OUTS * GROUPS)

        def turn(t):
            if t >= 2:
                eng.wait_ge(gelu_done, t - 1)
            for f in range(FC):
                src = o_tok[:, t % BT, (t // BT) * NG + f // 2, (f % 2) * P:(f % 2 + 1) * P]
                mm = eng.transpose(ps[:, 2 * (t % 2) + f // 4, (f % 4) * P:(f % 4 + 1) * P], src, sh.ident)
            mm.then_inc(o_turned, 1)

        turn(0)
        eng.wait_ge(wf_in, 32)
        for t in range(NT):
            if t + 1 < NT:
                turn(t + 1)
            eng.wait_ge(gelu_done, t + 1)
            if t >= 2:
                eng.wait_ge(x_done, t - 1)
            dst = ps[:, 4 + t % 2, 0:D]
            for f in range(FC):
                eng.matmul(dst, oT[:, t % 2, f, :], wf[:, f, :], start=f == 0, stop=False)
            eng.matmul(dst, sh.ones_row[0:1, :], bf[0:1, :], start=False, stop=True).then_inc(o_done, 1)

    sh.done = (nm.normed, run * NT + NT)
    sh.top = mark
    return {"sync": sync, "pool": pool, "scalar": scalar, "vector": vector, "tensor": tensor}


def routed_ffn(sh):
    ins, nm, tn, ps = sh.ins, sh.norm, sh.turn, sh.psum
    before = sh.done
    mark = sh.top
    GP, PER = 2, 4
    LG = GP + EXPERTS
    hT = sh.take("p (c s) -> p c s", DC * TOK, c=DC)
    RING = 2
    w12_raw = sh.take("p (r w c n) -> p r w c n", 2 * 2 * DC * HID, r=2, w=2, c=DC)
    w12 = sh.take_parts("p (r w c n) -> p r w c n", 2 * 2 * DC * HID, r=2, w=2, c=DC)
    w3 = sh.take_parts("p (r c n) -> p r c n", 2 * HC * D, r=2, c=HC)
    hT_parts = sh.take_parts("p (c s) -> p c s", DC * TOK, c=DC)
    room = hT.rearrange("p c s -> p (c s)")
    w3_raw = room[:, 0:HC * D].rearrange("p (c n) -> p c n", c=HC)
    hid_raw = room[:, HC * D:HC * D + RING * BANK].rearrange("p (r s) -> p r s", r=RING)
    silu = sh.take("p (r s) -> p r s", 2 * BANK, r=2)
    hid = sh.take_parts("p (m s) -> p m s", HC * TOK, m=HC)

    def hid_at(u):
        i, c, m = u // (CH * HC), u // HC % CH, u % HC
        at = c if i else 2 + c % 2
        return [v[:, m, at * BANK:(at + 1) * BANK] for v in hid]

    gw = sh.take("p (c e) -> p c e", DC * LG, c=DC)
    bias = sh.take(None, 12)
    lg = sh.take("p (t e) -> p t e", NT * LG, t=NT)
    ev = sh.take("p (t e) -> p t e", NT * EXPERTS, t=NT)
    ex = sh.take("p (t e) -> p t e", NT * EXPERTS, t=NT)
    one1 = sh.take("p (t e) -> p t e", NT * EXPERTS, t=NT)
    one2 = sh.take("p (t e) -> p t e", NT * EXPERTS, t=NT)
    wt = sh.take("p (t e) -> p t e", NT * EXPERTS, t=NT)
    small = sh.take("p (k t) -> p k t", 8 * NT, k=8)
    diff, sel0, sel1, gp, z, best1, best2 = (small[:, k] for k in range(7))
    top = TopTwo(sh, "rt", EXPERTS)
    s = {k: sh.sem("rt_" + k) for k in ("loaded", "logits", "exped", "ab_done", "silued", "hid_made", "o_done", "added",
                                     "high", "low", "hid_high", "hid_low", "w_high", "w_low")}
    w_in = sh.sem("rt_w_in")
    h_in = sh.sem("rt_h_in")
    run, trun = nm.use(), tn.use()
    wide = [P, NT, EXPERTS]
    UNITS_L = 2 * CH * HC
    exp_at = EXPERTS + 1 + 4 + 2 + 5 + 1

    def loop(eng, body):
        with eng.Fori(0, EXPERTS // 2 - 1) as pair:
            for r in range(2):
                body(pair * 2 + r, r)
        body(EXPERTS - 2, 0)
        body(EXPERTS - 1, 1)

    def sync(eng):
        eng.wait_ge(*before)
        for k, (name, n) in enumerate((("wg", GP), ("we", EXPERTS))):
            eng.dma_start(gw[:, :, k * GP:k * GP + n], ins["L1_ffn_" + name].rearrange("(c p) e -> p c e", p=P),
                          allow_slow_non_contiguous=True).then_inc(s["loaded"], 16)
        for k, (name, n) in enumerate((("gb", GP), ("eb", EXPERTS))):
            eng.dma_start(bias[0:1, k * GP:k * GP + n], ins["L1_ffn_" + name].rearrange("(o e) -> o e", o=1)).then_inc(s["loaded"], 16)
        for i, name in enumerate(("w_in", "w1")):
            for w in range(2):
                eng.dma_start(w12_raw[:, i, w], ins["L1_ffn_" + name][:, w * HID:(w + 1) * HID]
                              .rearrange("(c p) n -> p c n", p=P)).then_inc(h_in, 16)
        eng.wait_ge(s["high"], 6)
        eng.wait_ge(s["logits"], 1)
        eng.dma_start(w3_raw, ins["L1_ffn_w_out"].rearrange("(c p) n -> p c n", p=P)).then_inc(w_in, 16)
        with eng.Fori(0, EXPERTS) as e:
            eng.wait_ge(s["w_low"], e + 1)
            eng.dma_start(w3_raw, ins["L1_ffn_w2"][bass.ds(e, 1)].rearrange("o (c p) n -> p (o c) n", p=P))\
                .then_inc(w_in, 16)

    def scalar(eng):
        tn.scalar(eng, hT, trun)
        eng.wait_ge(top.step, exp_at)
        eng.activation(ex, ex, ACT.Exp).then_inc(s["exped"], 1)
        eng.activation(gp, gp, ACT.Exp).then_inc(s["exped"], 1)
        for u in range(UNITS_L):
            eng.wait_ge(s["ab_done"], u + 1)
            eng.wait_ge(s["hid_made"], u + 1)
            eng.activation(silu[:, u % 2], ps[:, 2 * (u % 2), :], ACT.Silu).then_inc(s["silued"], 1)
        nm.scalar(eng, run)

    def pool(eng):
        for i in range(2):
            eng.wait_ge(s["high"], 2 * i + 2)
            for w in range(2):
                low_part(eng, w12[1][:, i, w], w12[0][:, i, w], w12_raw[:, i, w]).then_inc(s["low"], 1)
        eng.wait_ge(s["w_high"], 1)
        low_part(eng, w3[1][:, 0], w3[0][:, 0], w3_raw).then_inc(s["w_low"], 1)
        for u in range(UNITS_L):
            eng.wait_ge(s["hid_high"], u + 1)
            high, low = hid_at(u)
            low_part(eng, low, high, hid_raw[:, u % RING]).then_inc(s["hid_low"], 1)
        with eng.Fori(0, EXPERTS // 2) as pair:
            for r in range(2):
                eng.wait_ge(s["w_high"], pair * 2 + r + 2)
                low_part(eng, w3[1][:, 1 - r], w3[0][:, 1 - r], w3_raw).then_inc(s["w_low"], 1)

    def vector(eng):
        eng.wait_ge(*before)
        eng.wait_ge(h_in, 64)
        for i in range(2):
            for w in range(2):
                high_part(eng, w12[0][:, i, w], w12_raw[:, i, w]).then_inc(s["high"], 1)
        top.start(eng)
        eng.wait_ge(tn.taken, 8 * trun + 8)
        high_part(eng, hT_parts[0], hT).then_inc(s["high"], 1)
        eng.wait_ge(s["high"], 5)
        low_part(eng, hT_parts[1], hT_parts[0], hT).then_inc(s["high"], 1)
        eng.wait_ge(s["logits"], 1)
        top.did(eng.tensor_copy(lg, ps[:, 0, 0:NT * LG].rearrange("p (t e) -> p t e", t=NT)))
        top.wait(eng)
        top.did(eng.tensor_tensor(diff, lg[:, :, 0], lg[:, :, 1], ALU.subtract))
        top.wait(eng)
        top.did(eng.tensor_scalar(sel0, diff, 0.0, None, ALU.is_ge))
        top.did(eng.tensor_scalar(sel1, diff, 0.0, None, ALU.is_lt))
        top.did(eng.scalar_tensor_tensor(gp, diff, -1.0, diff, ALU.mult, ALU.min))
        top.wait(eng)
        for g, other in enumerate((sel1, sel0)):
            e0 = g * PER
            top.did(eng.scalar_tensor_tensor(ev[:, :, e0:e0 + PER], other.unsqueeze(2).to_broadcast([P, NT, PER]), -1e30,
                                             lg[:, :, GP + e0:GP + e0 + PER], ALU.mult, ALU.add))
        top.wait(eng)
        top.pick(eng, ev, best1, one1)
        top.did(eng.tensor_tensor(ex, ev, best1.unsqueeze(2).to_broadcast(wide), ALU.subtract))
        assert top.steps == exp_at, top.steps
        top.did(eng.scalar_tensor_tensor(ev, one1, -1e30, ev, ALU.mult, ALU.add))
        top.wait(eng)
        top.pick(eng, ev, best2, one2)
        top.did(eng.tensor_tensor(one1, one1, one2, ALU.add))
        eng.wait_ge(s["exped"], 2)
        top.did(eng.tensor_reduce(z, ex, AX_X, ALU.add))
        top.did(eng.tensor_scalar(gp, gp, 1.0, None, ALU.add))
        top.wait(eng)
        top.did(eng.tensor_tensor(z, z, gp, ALU.mult))
        top.wait(eng)
        top.did(eng.reciprocal(z, z))
        top.did(eng.tensor_tensor(one1, one1, ex, ALU.mult))
        top.wait(eng)
        top.did(eng.tensor_tensor(wt, one1, z.unsqueeze(2).to_broadcast(wide), ALU.mult))
        top.wait(eng)
        eng.wait_ge(w_in, 16)
        high_part(eng, w3[0][:, 0], w3_raw).then_inc(s["w_high"], 1)
        eng.memset(small[:, 7, 0:1], 0.0).then_inc(s["hid_made"], 2)
        eng.wait_ge(s["hid_made"], 2)

        def out(c, t):
            return ps[:, 4 + 2 * (c % 2) + t // 2, (t % 2) * D:(t % 2 + 1) * D]

        def add_shared(c):
            eng.wait_ge(s["o_done"], c + 1)
            for t in range(4):
                n = 4 * c + t
                eng.tensor_tensor(sh.x[:, n, :], sh.x[:, n, :], out(c, t), ALU.add).then_inc(s["added"], 1)

        for u in range(UNITS_L):
            i, c, m = u // (CH * HC), u // HC % CH, u % HC
            eng.wait_ge(s["silued"], u + 1)
            whole = hid_raw[:, u % RING]
            if u >= RING:
                eng.wait_ge(s["hid_low"], u - RING + 1)
            if u == CH * HC + 2 * HC:
                eng.wait_ge(s["o_done"], CH)
            elif u in (2 * HC, 3 * HC):
                eng.wait_ge(s["o_done"], u // HC - 1)
            eng.tensor_tensor(whole, silu[:, u % 2], ps[:, 2 * (u % 2) + 1, :], ALU.mult).then_inc(s["hid_made"], 1)
            eng.wait_ge(s["hid_made"], u + 3)
            high_part(eng, hid_at(u)[0], whole).then_inc(s["hid_high"], 1)
            if i == 0 and m == HC - 1 and c >= 1:
                add_shared(c - 1)
            elif u == CH * HC:
                add_shared(CH - 1)

        def weights_high(e, r):
            sh.wait_apart(eng, w_in, e * 16 + 32)
            high_part(eng, w3[0][:, 1 - r], w3_raw).then_inc(s["w_high"], 1)

        weights_high(0, 0)
        def body(e, r):
            for c in range(CH):
                if c == 1 and not (isinstance(e, int) and e == EXPERTS - 1):
                    weights_high(e + 1, 1 - r)
                sh.wait_apart(eng, s["o_done"], (e + 1) * CH + c + 1)
                eng.wait_ge(s["added"], e * NT + 4 * c + 4)
                for t in range(4):
                    n = 4 * c + t
                    eng.scalar_tensor_tensor(sh.x[:, n, :], out(c, t), wt[:, n, bass.ds(e, 1)], sh.x[:, n, :],
                                             ALU.mult, ALU.add).then_inc(s["added"], 1)
        loop(eng, body)
        eng.wait_ge(s["added"], (EXPERTS + 1) * NT)
        nm.vector(eng, lambda t: sh.x[:, t, :], lambda t: sh.x[:, t, :], run)

    def tensor(eng):
        eng.wait_ge(*before)
        tn.tensor(eng, lambda t, c: sh.x[:, t, c * P:(c + 1) * P], trun, lambda e, t: None)
        eng.wait_ge(s["loaded"], 64)
        eng.wait_ge(tn.taken, 8 * trun + 8)
        for t in range(NT):
            dst = ps[:, 0, t * LG:(t + 1) * LG]
            for k in range(DC):
                eng.matmul(dst, hT[:, k, t * P:(t + 1) * P], gw[:, k, :], start=k == 0, stop=False)
            mm = eng.matmul(dst, sh.ones_row[0:1, :], bias[0:1, 0:LG], start=False, stop=True)
        mm.then_inc(s["logits"], 1)
        eng.wait_ge(s["high"], 6)

        def products(e, c, slot):
            if c >= 2 or not isinstance(e, int) or e >= 0:
                eng.wait_ge(s["added"], (e + 1) * NT + 4 * c - 4)
            for t in range(4):
                for m in range(HC):
                    rows = hid_at((c if e_is_shared(e) else CH + c) * HC + m)
                    mm = product_of_parts(eng, ps[:, 4 + 2 * (c % 2) + t // 2, (t % 2) * D:(t % 2 + 1) * D],
                                          [v[:, t * P:(t + 1) * P] for v in rows], [v[:, slot, m, :] for v in w3],
                                          m == 0, m == HC - 1)
            mm.then_inc(s["o_done"], 1)

        def e_is_shared(e):
            return isinstance(e, int) and e < 0

        def shared_products(c):
            eng.wait_ge(s["w_low"], 1)
            eng.wait_ge(s["hid_low"], (c + 1) * HC)
            products(-1, c, 0)

        for u in range(UNITS_L):
            i, c, m = u // (CH * HC), u // HC % CH, u % HC
            if u % (CH * HC) == 0:
                eng.wait_ge(s["low"], 2 * i + 2)
            eng.wait_ge(s["hid_made"], u + 1)
            for w in range(2):
                for k in range(DC):
                    mm = product_of_parts(eng, ps[:, 2 * (u % 2) + w, :], [v[:, i, w, k, m * P:(m + 1) * P] for v in w12],
                                          [v[:, k, c * BANK:(c + 1) * BANK] for v in hT_parts], k == 0, k == DC - 1)
            mm.then_inc(s["ab_done"], 1)
            if i == 0 and m == 1 and c >= 1:
                shared_products(c - 1)
            elif u == CH * HC + 1:
                shared_products(CH - 1)
        eng.wait_ge(s["hid_low"], UNITS_L)

        def body(e, r):
            eng.wait_ge(s["w_low"], e + 2)
            for c in range(CH):
                products(e, c, 1 - r)
        loop(eng, body)

    sh.done = (nm.normed, run * NT + NT)
    sh.top = mark
    return {"sync": sync, "pool": pool, "scalar": scalar, "vector": vector, "tensor": tensor}


def norms(sh):
    sh.norm_all()
    return {}


def causal_masks(sh):
    sh.masks = Masks(sh)
    return {"pool": sh.masks.pool}


def context_rows(sh):
    sh.context = Context(sh)
    return sh.context.stage()


def store_x(sh):
    stored = sh.sem("stored")
    normed, last = sh.done
    STEP = NT // 4

    def sync(eng):
        rows = sh.out.rearrange("b (t p) d -> p (b t) d", p=P)
        for t in range(0, NT, STEP):
            eng.wait_ge(normed, last - NT + t + STEP)
            eng.dma_start(rows[:, t:t + STEP], sh.x[:, t:t + STEP, :]).then_inc(stored, 16)
        eng.wait_ge(stored, 16 * NT // STEP)
    return {"sync": sync}


def run_phase(sh, stages):
    parts = [stage(sh) for stage in stages]
    with sh.nc.Block() as block:

        @block.sync
        def _(sp):
            for part in parts:
                if "sync" in part:
                    part["sync"](sp)

        @block.gpsimd
        def _(pool):
            for part in parts:
                if "pool" in part:
                    part["pool"](pool)

        @block.scalar
        def _(act):
            for part in parts:
                if "scalar" in part:
                    part["scalar"](act)

        @block.vector
        def _(dve):
            for part in parts:
                if "vector" in part:
                    part["vector"](dve)

        @block.tensor
        def _(pe):
            for part in parts:
                if "tensor" in part:
                    part["tensor"](pe)


def program(nc, ins, out, phases):
    with ExitStack() as ctx:
        sh = Shared(nc, ctx, ins, out)
        for n, (stages, rounded) in enumerate(phases):
            if n:
                nc.clear_and_free_semaphores(sh.phase_sems)
                nc.all_engine_barrier()
                sh.done = sh.constants
            with ExitStack() as phase_ctx:
                sh.start_phase(n, phase_ctx, rounded)
                run_phase(sh, stages)


def build(nc, ins, out):
    program(nc, ins, out, [
        ([constants, norms, mamba, mamba_out, context_rows, query_softmax_attention], 0),
        ([norms, causal_masks, self_attention], 0),
        ([norms, experts], 28672),
        ([norms, causal_masks, gelu_attention, context_rows, masked_cross_attention], 0),
        ([norms, routed_ffn, store_x], 36864),
    ])


_TRANSPOSED = ("L1_xattn_W_Q", "L1_xattn_W_K", "L1_xattn_W_V", "L1_xattn_W_O",
               "L1_ffn_w_in", "L1_ffn_w_out", "L1_ffn_w1", "L1_ffn_w2", "L1_ffn_wg", "L1_ffn_we")


def kernel(**inputs):
    import numpy as _np
    import concourse.bacc as _bacc
    from concourse import mybir as _mybir
    from concourse.bass_utils import run_bass_kernel_spmd as _run

    nc = _bacc.Bacc("TRN2", target_bir_lowering=False, num_devices=1)
    arrays, ins = {}, {}
    for name, value in inputs.items():
        a = _np.asarray(value)
        if name in _TRANSPOSED:
            a = a.swapaxes(-1, -2)
        arrays[name] = _np.ascontiguousarray(a)
        ins[name] = nc.dram_tensor(name, list(a.shape), _mybir.dt.from_np(a.dtype), kind="ExternalInput").ap()
    out = nc.dram_tensor("out", [B, S, D], F32, kind="ExternalOutput").ap()
    build(nc, ins, out)
    if not nc.is_finalized():
        nc.finalize()
    return _run(nc, [arrays], [0]).results[0]["out"]
```
